# Optimizing a Trainium2 kernel written in Bass

```python
import numpy as np
import jax
import jax.numpy as jnp

def _softmax(x, axis=-1):
    return jax.nn.softmax(x, axis=axis)

def _gelu(x):
    return jax.nn.gelu(x, approximate=True)

def _silu(x):
    return jax.nn.silu(x)

def _sigmoid(x):
    return jax.nn.sigmoid(x)

def _layernorm(x, axis=-1, eps=1e-05):
    m = jnp.mean(x, axis=axis, keepdims=True)
    v = jnp.var(x, axis=axis, keepdims=True)
    return (x - m) / jnp.sqrt(v + eps)

def _scatter_add(tgt, idx, src, axis=0):
    return tgt.at[idx].add(src)

def _segment_sum(src, seg, n):
    return jax.ops.segment_sum(src, seg, n)
kernel_name = 'mk_adaln_d2_jaxref_r8_067d98'

def setup_inputs(seed: int=0):
    np.random.seed(seed)
    _w = jnp.asarray

    def _L0_attn_setup():
        import jax, jax.numpy as jnp
        import numpy as np
        D_MODEL = 128
        D_INNER = 256
        D_STATE = 16
        DT_RANK = 64
        D_CONV = 4
        B_SZ, L = (2, 256)

        def _mamba_block(x, adj, in_proj_w, conv_w, conv_b, x_proj_w, dt_proj_w, dt_proj_b, A_log, D, out_proj_w):
            b, l, _ = x.shape
            xr = x @ in_proj_w
            xi, res = jnp.split(xr, 2, axis=-1)
            xc = jnp.swapaxes(xi, 1, 2)
            xc = jax.lax.conv_general_dilated(xc, conv_w, window_strides=(1,), padding=[(D_CONV - 1, 0)], dimension_numbers=('NCH', 'OIH', 'NCH'), feature_group_count=D_INNER)
            xc = xc + conv_b[None, :, None]
            xi = jax.nn.silu(jnp.swapaxes(xc, 1, 2))
            A = -jnp.exp(A_log)
            x_dbl = xi @ x_proj_w
            delta, Bmat, Cmat = jnp.split(x_dbl, [DT_RANK, DT_RANK + D_STATE], axis=-1)
            delta = jax.nn.softplus(delta @ dt_proj_w + dt_proj_b)
            delta_p = delta @ adj
            deltaA = jnp.exp(jnp.einsum('bld,dn->bldn', delta_p, A))
            dBu = jnp.einsum('bld,bln,bld->bldn', delta_p, Bmat, xi)

            def step(h, inputs):
                dA_t, dBu_t, C_t = inputs
                h = dA_t * h + dBu_t
                y_t = jnp.einsum('bdn,bn->bd', h, C_t)
                return (h, y_t)
            h0 = jnp.zeros((b, D_INNER, D_STATE), xi.dtype)
            _, ys = jax.lax.scan(step, h0, (jnp.swapaxes(deltaA, 0, 1), jnp.swapaxes(dBu, 0, 1), jnp.swapaxes(Cmat, 0, 1)))
            y = jnp.swapaxes(ys, 0, 1) + xi * D
            y = y * jax.nn.silu(res)
            return y @ out_proj_w
        key = jax.random.key(seed)
        ks = jax.random.split(key, 12)
        g = lambda k, shape, s: jax.random.normal(k, shape, jnp.float32) * s
        return {'x': jax.random.normal(ks[0], (B_SZ, L, D_MODEL), jnp.float32), 'adj': jax.random.uniform(ks[1], (D_INNER, D_INNER), jnp.float32) / D_INNER, 'in_proj_w': g(ks[2], (D_MODEL, 2 * D_INNER), D_MODEL ** (-0.5)), 'conv_w': g(ks[3], (D_INNER, 1, D_CONV), D_CONV ** (-0.5)), 'conv_b': g(ks[4], (D_INNER,), 0.02), 'x_proj_w': g(ks[5], (D_INNER, DT_RANK + 2 * D_STATE), D_INNER ** (-0.5)), 'dt_proj_w': g(ks[6], (DT_RANK, D_INNER), DT_RANK ** (-0.5)), 'dt_proj_b': g(ks[7], (D_INNER,), 0.02), 'A_log': jnp.log(jnp.broadcast_to(jnp.arange(1, D_STATE + 1, dtype=jnp.float32), (D_INNER, D_STATE))), 'D': jnp.ones((D_INNER,), jnp.float32), 'out_proj_w': g(ks[8], (D_INNER, D_MODEL), D_INNER ** (-0.5))}
    _L0_attn_in = _L0_attn_setup()

    def _L0_ffn_setup():
        import jax, jax.numpy as jnp
        import numpy as np
        B, S, D, F, E = (1, 128, 128, 512, 8)
        EPS = 1e-05

        def _sublayer(xs, g, b, W1e, b1e, W2e, b2e):
            mu = jnp.mean(xs, axis=-1, keepdims=True)
            var = jnp.mean(jnp.square(xs - mu), axis=-1, keepdims=True)
            h = (xs - mu) * jax.lax.rsqrt(var + EPS) * g + b
            return xs + jax.nn.relu(h @ W1e.T + b1e) @ W2e.T + b2e
        key = jax.random.key(seed)
        ks = jax.random.split(key, 4)
        x = jax.random.normal(ks[0], (B, S, D), jnp.float32)
        centroids = jax.random.normal(ks[1], (E, D), jnp.float32) * 0.1
        gamma = jnp.ones((E, D), jnp.float32)
        beta = jnp.zeros((E, D), jnp.float32)
        W1 = jax.random.normal(ks[2], (E, F, D), jnp.float32) * 0.02
        b1 = jnp.zeros((E, F), jnp.float32)
        W2 = jax.random.normal(ks[3], (E, D, F), jnp.float32) * 0.02
        b2 = jnp.zeros((E, D), jnp.float32)
        return {'x': x, 'centroids': centroids, 'gamma': gamma, 'beta': beta, 'W1': W1, 'b1': b1, 'W2': W2, 'b2': b2}
    _L0_ffn_in = _L0_ffn_setup()
    _L0_c = _w((lambda *s: np.random.randn(*s).astype(np.float32) * 0.05)(8, 128))
    _L0_wmod = _w((lambda *s: np.random.randn(*s).astype(np.float32) * 0.05)(128, 6 * 128) * 128 ** (-0.5))

    def _L1_attn_setup():
        import jax, jax.numpy as jnp
        import numpy as np
        import math
        NUM_HEADS = 16

        def _alibi_bias(L, num_heads):
            slopes = jnp.power(2.0, jnp.linspace(-4.0, -0.3, num_heads))
            pos = jnp.arange(L, dtype=jnp.float32)
            return -(slopes[:, None] * pos[None, :])
        key = jax.random.key(seed)
        ks = jax.random.split(key, 9)
        B, L, D = (2, 256, 128)
        s = 0.02
        return {'x': jax.random.normal(ks[0], (B, L, D), dtype=jnp.float32), 'Wq': jax.random.normal(ks[1], (D, D), dtype=jnp.float32) * s, 'bq': jax.random.normal(ks[2], (D,), dtype=jnp.float32) * s, 'Wk': jax.random.normal(ks[3], (D, D), dtype=jnp.float32) * s, 'bk': jax.random.normal(ks[4], (D,), dtype=jnp.float32) * s, 'Wv': jax.random.normal(ks[5], (D, D), dtype=jnp.float32) * s, 'bv': jax.random.normal(ks[6], (D,), dtype=jnp.float32) * s, 'Wo': jax.random.normal(ks[7], (D, D), dtype=jnp.float32) * s, 'bo': jax.random.normal(ks[8], (D,), dtype=jnp.float32) * s}
    _L1_attn_in = _L1_attn_setup()

    def _L1_ffn_setup():
        import jax, jax.numpy as jnp
        import numpy as np
        B, S, D, F, E = (4, 256, 128, 512, 8)
        key = jax.random.key(seed)
        ks = jax.random.split(key, 7)
        s1 = 1.0 / np.sqrt(D)
        s2 = 1.0 / np.sqrt(F)
        x = jax.random.normal(ks[0], (B, S, D), dtype=jnp.float32)
        W1 = jax.random.uniform(ks[1], (E, D, F), jnp.float32, -s1, s1)
        b1 = jax.random.uniform(ks[2], (E, F), jnp.float32, -s1, s1)
        W2 = jax.random.uniform(ks[3], (E, F, D), jnp.float32, -s2, s2)
        b2 = jax.random.uniform(ks[4], (E, D), jnp.float32, -s2, s2)
        Wr = jax.random.uniform(ks[5], (D, E), jnp.float32, -s1, s1)
        br = jax.random.uniform(ks[6], (E,), jnp.float32, -s1, s1)
        return {'x': x, 'W1': W1, 'b1': b1, 'W2': W2, 'b2': b2, 'Wr': Wr, 'br': br}
    _L1_ffn_in = _L1_ffn_setup()
    _L1_c = _w((lambda *s: np.random.randn(*s).astype(np.float32) * 0.05)(8, 128))
    _L1_wmod = _w((lambda *s: np.random.randn(*s).astype(np.float32) * 0.05)(128, 6 * 128) * 128 ** (-0.5))
    _d = {'L0_attn_x': _L0_attn_in['x'], 'L0_attn_adj': _L0_attn_in['adj'], 'L0_attn_in_proj_w': _L0_attn_in['in_proj_w'], 'L0_attn_conv_w': _L0_attn_in['conv_w'], 'L0_attn_conv_b': _L0_attn_in['conv_b'], 'L0_attn_x_proj_w': _L0_attn_in['x_proj_w'], 'L0_attn_dt_proj_w': _L0_attn_in['dt_proj_w'], 'L0_attn_dt_proj_b': _L0_attn_in['dt_proj_b'], 'L0_attn_A_log': _L0_attn_in['A_log'], 'L0_attn_D': _L0_attn_in['D'], 'L0_attn_out_proj_w': _L0_attn_in['out_proj_w'], 'L0_ffn_centroids': _L0_ffn_in['centroids'], 'L0_ffn_gamma': _L0_ffn_in['gamma'], 'L0_ffn_beta': _L0_ffn_in['beta'], 'L0_ffn_W1': _L0_ffn_in['W1'], 'L0_ffn_b1': _L0_ffn_in['b1'], 'L0_ffn_W2': _L0_ffn_in['W2'], 'L0_ffn_b2': _L0_ffn_in['b2'], 'L0_c': _L0_c, 'L0_wmod': _L0_wmod, 'L1_attn_Wq': _L1_attn_in['Wq'], 'L1_attn_bq': _L1_attn_in['bq'], 'L1_attn_Wk': _L1_attn_in['Wk'], 'L1_attn_bk': _L1_attn_in['bk'], 'L1_attn_Wv': _L1_attn_in['Wv'], 'L1_attn_bv': _L1_attn_in['bv'], 'L1_attn_Wo': _L1_attn_in['Wo'], 'L1_attn_bo': _L1_attn_in['bo'], 'L1_ffn_W1': _L1_ffn_in['W1'], 'L1_ffn_b1': _L1_ffn_in['b1'], 'L1_ffn_W2': _L1_ffn_in['W2'], 'L1_ffn_b2': _L1_ffn_in['b2'], 'L1_ffn_Wr': _L1_ffn_in['Wr'], 'L1_ffn_br': _L1_ffn_in['br'], 'L1_c': _L1_c, 'L1_wmod': _L1_wmod}
    _x0 = _d['L0_attn_x']
    _d['L0_attn_x'] = jax.random.normal(jax.random.fold_in(jax.random.key(seed), 1), (8, 256, 128), dtype=_x0.dtype)
    del _x0
    return _d

def reference(L0_attn_x, L0_attn_adj, L0_attn_in_proj_w, L0_attn_conv_w, L0_attn_conv_b, L0_attn_x_proj_w, L0_attn_dt_proj_w, L0_attn_dt_proj_b, L0_attn_A_log, L0_attn_D, L0_attn_out_proj_w, L0_ffn_centroids, L0_ffn_gamma, L0_ffn_beta, L0_ffn_W1, L0_ffn_b1, L0_ffn_W2, L0_ffn_b2, L0_c, L0_wmod, L1_attn_Wq, L1_attn_bq, L1_attn_Wk, L1_attn_bk, L1_attn_Wv, L1_attn_bv, L1_attn_Wo, L1_attn_bo, L1_ffn_W1, L1_ffn_b1, L1_ffn_W2, L1_ffn_b2, L1_ffn_Wr, L1_ffn_br, L1_c, L1_wmod):

    def _L0_attn_ref(x, adj, in_proj_w, conv_w, conv_b, x_proj_w, dt_proj_w, dt_proj_b, A_log, D, out_proj_w):
        import jax, jax.numpy as jnp
        import numpy as np
        D_MODEL = 128
        D_INNER = 256
        D_STATE = 16
        DT_RANK = 64
        D_CONV = 4
        B_SZ, L = (2, 256)

        def _mamba_block(x, adj, in_proj_w, conv_w, conv_b, x_proj_w, dt_proj_w, dt_proj_b, A_log, D, out_proj_w):
            b, l, _ = x.shape
            xr = x @ in_proj_w
            xi, res = jnp.split(xr, 2, axis=-1)
            xc = jnp.swapaxes(xi, 1, 2)
            xc = jax.lax.conv_general_dilated(xc, conv_w, window_strides=(1,), padding=[(D_CONV - 1, 0)], dimension_numbers=('NCH', 'OIH', 'NCH'), feature_group_count=D_INNER)
            xc = xc + conv_b[None, :, None]
            xi = jax.nn.silu(jnp.swapaxes(xc, 1, 2))
            A = -jnp.exp(A_log)
            x_dbl = xi @ x_proj_w
            delta, Bmat, Cmat = jnp.split(x_dbl, [DT_RANK, DT_RANK + D_STATE], axis=-1)
            delta = jax.nn.softplus(delta @ dt_proj_w + dt_proj_b)
            delta_p = delta @ adj
            deltaA = jnp.exp(jnp.einsum('bld,dn->bldn', delta_p, A))
            dBu = jnp.einsum('bld,bln,bld->bldn', delta_p, Bmat, xi)

            def step(h, inputs):
                dA_t, dBu_t, C_t = inputs
                h = dA_t * h + dBu_t
                y_t = jnp.einsum('bdn,bn->bd', h, C_t)
                return (h, y_t)
            h0 = jnp.zeros((b, D_INNER, D_STATE), xi.dtype)
            _, ys = jax.lax.scan(step, h0, (jnp.swapaxes(deltaA, 0, 1), jnp.swapaxes(dBu, 0, 1), jnp.swapaxes(Cmat, 0, 1)))
            y = jnp.swapaxes(ys, 0, 1) + xi * D
            y = y * jax.nn.silu(res)
            return y @ out_proj_w
        return _mamba_block(x, adj, in_proj_w, conv_w, conv_b, x_proj_w, dt_proj_w, dt_proj_b, A_log, D, out_proj_w)

    def _L0_ffn_ref(x, centroids, gamma, beta, W1, b1, W2, b2):
        import jax, jax.numpy as jnp
        import numpy as np
        B, S, D, F, E = (1, 128, 128, 512, 8)
        EPS = 1e-05

        def _sublayer(xs, g, b, W1e, b1e, W2e, b2e):
            mu = jnp.mean(xs, axis=-1, keepdims=True)
            var = jnp.mean(jnp.square(xs - mu), axis=-1, keepdims=True)
            h = (xs - mu) * jax.lax.rsqrt(var + EPS) * g + b
            return xs + jax.nn.relu(h @ W1e.T + b1e) @ W2e.T + b2e
        feats = x.reshape(-1, x.shape[-1])
        scores = jax.lax.stop_gradient(feats @ centroids.T)
        expert = jnp.argmax(scores, axis=1)
        onehot = jax.nn.one_hot(expert, E, dtype=feats.dtype)
        alpha = jax.nn.sigmoid(jnp.sum(feats * centroids[expert], axis=-1, keepdims=True))
        ys = jax.vmap(_sublayer, in_axes=(None, 0, 0, 0, 0, 0, 0))(feats, gamma, beta, W1, b1, W2, b2)
        y = jnp.einsum('te,etd->td', onehot, ys)
        out = alpha * y + (1.0 - alpha) * feats
        return out.reshape(x.shape)

    def _L1_attn_ref(x, Wq, bq, Wk, bk, Wv, bv, Wo, bo):
        import jax, jax.numpy as jnp
        import numpy as np
        import math
        NUM_HEADS = 16

        def _alibi_bias(L, num_heads):
            slopes = jnp.power(2.0, jnp.linspace(-4.0, -0.3, num_heads))
            pos = jnp.arange(L, dtype=jnp.float32)
            return -(slopes[:, None] * pos[None, :])
        B, L, D = x.shape
        H = NUM_HEADS
        hd = D // H
        scale = math.sqrt(hd)

        def proj(W, b):
            return (jnp.einsum('bld,ed->ble', x, W) + b).reshape(B, L, H, hd)
        q = proj(Wq, bq)
        k = proj(Wk, bk)
        v = proj(Wv, bv)
        scores = jnp.einsum('bqhd,bkhd->bhqk', q, k) / scale
        bias = _alibi_bias(L, H)
        scores = scores + bias[None, :, None, :]
        attn = jax.nn.softmax(scores, axis=-1)
        out = jnp.einsum('bhqk,bkhd->bqhd', attn, v).reshape(B, L, D)
        return jnp.einsum('bld,ed->ble', out, Wo) + bo

    def _L1_ffn_ref(x, W1, b1, W2, b2, Wr, br):
        import jax, jax.numpy as jnp
        import numpy as np
        B, S, D, F, E = (4, 256, 128, 512, 8)
        b, s, d = x.shape
        e = Wr.shape[1]
        logits = x @ Wr + br
        idx = jnp.argmax(logits, axis=-1)
        probs = jax.nn.softmax(logits, axis=-1)
        gates = jnp.take_along_axis(probs, idx[..., None], axis=-1)[..., 0]
        xf = x.reshape(-1, d)
        idxf = idx.reshape(-1)
        gf = gates.reshape(-1)
        out = jnp.zeros_like(xf)
        for ei in range(e):
            h = jax.nn.gelu(xf @ W1[ei] + b1[ei], approximate=False)
            y = h @ W2[ei] + b2[ei]
            mask = (idxf == ei).astype(xf.dtype)
            out = out + y * (gf * mask)[:, None]
        return out.reshape(b, s, d)
    x = L0_attn_x
    mod = (_silu(L0_c) @ L0_wmod).reshape(L0_c.shape[0], 6, 1, -1)
    sa, ca, ga, sb, cb, gb = (mod[:, 0], mod[:, 1], mod[:, 2], mod[:, 3], mod[:, 4], mod[:, 5])
    ga = (2 * (ga >= 0) - 1) * jnp.maximum(jnp.abs(ga), 0.25)
    gb = (2 * (gb >= 0) - 1) * jnp.maximum(jnp.abs(gb), 0.25)
    h = _layernorm(x, axis=-1) * (1 + ca) + sa
    x = x + ga * _L0_attn_ref(h, L0_attn_adj, L0_attn_in_proj_w, L0_attn_conv_w, L0_attn_conv_b, L0_attn_x_proj_w, L0_attn_dt_proj_w, L0_attn_dt_proj_b, L0_attn_A_log, L0_attn_D, L0_attn_out_proj_w)
    h = _layernorm(x, axis=-1) * (1 + cb) + sb
    x = x + gb * _L0_ffn_ref(h, L0_ffn_centroids, L0_ffn_gamma, L0_ffn_beta, L0_ffn_W1, L0_ffn_b1, L0_ffn_W2, L0_ffn_b2)
    mod = (_silu(L1_c) @ L1_wmod).reshape(L1_c.shape[0], 6, 1, -1)
    sa, ca, ga, sb, cb, gb = (mod[:, 0], mod[:, 1], mod[:, 2], mod[:, 3], mod[:, 4], mod[:, 5])
    ga = (2 * (ga >= 0) - 1) * jnp.maximum(jnp.abs(ga), 0.25)
    gb = (2 * (gb >= 0) - 1) * jnp.maximum(jnp.abs(gb), 0.25)
    h = _layernorm(x, axis=-1) * (1 + ca) + sa
    x = x + ga * _L1_attn_ref(h, L1_attn_Wq, L1_attn_bq, L1_attn_Wk, L1_attn_bk, L1_attn_Wv, L1_attn_bv, L1_attn_Wo, L1_attn_bo)
    h = _layernorm(x, axis=-1) * (1 + cb) + sb
    x = x + gb * _L1_ffn_ref(h, L1_ffn_W1, L1_ffn_b1, L1_ffn_W2, L1_ffn_b2, L1_ffn_Wr, L1_ffn_br)
    return x

_drawn_inputs = setup_inputs


def setup_inputs(seed=0):
    import zlib

    import numpy as np

    out = dict(_drawn_inputs(seed))
    spreads = {'L0_attn_D': (1.0, 0.6),
     'L0_ffn_gamma': (1.0, 0.6),
     'L0_ffn_beta': (0.0, 0.8),
     'L0_ffn_b1': (0.0, 0.8),
     'L0_ffn_b2': (0.0, 0.402)}
    factors = {'L0_attn_adj': 8.0,
     'L0_attn_conv_b': 8.0,
     'L0_attn_dt_proj_w': 8.0,
     'L0_attn_dt_proj_b': 23.775,
     'L0_attn_A_log': 21.827,
     'L0_ffn_W1': 4.385,
     'L0_ffn_W2': 3.405,
     'L1_attn_Wq': 8.0,
     'L1_attn_bq': 8.0,
     'L1_attn_Wk': 8.0,
     'L1_attn_bk': 64.0,
     'L1_attn_Wv': 8.0,
     'L1_attn_bv': 8.0,
     'L1_attn_Wo': 8.0,
     'L1_attn_bo': 8.0,
     'L1_ffn_W1': 4.729,
     'L1_ffn_b1': 8.0,
     'L1_ffn_W2': 4.453,
     'L1_ffn_b2': 24.877,
     'L1_ffn_Wr': 4.741,
     'L1_ffn_br': 8.0,
     'L1_c': 3.832,
     'L1_wmod': 3.91}
    for name, (base, spread) in spreads.items():
        noise = np.random.default_rng([zlib.crc32(name.encode()), seed]).standard_normal(out[name].shape)
        drawn = base * np.exp(spread * noise) if base else spread * noise
        out[name] = jnp.asarray(drawn.astype(out[name].dtype))
    for name, factor in factors.items():
        out[name] = (out[name] * factor).astype(out[name].dtype)
    return out
```

```python
import numpy as np
import concourse.bass as bass
from concourse import mybir
from contextlib import ExitStack

B, L, D = 8, 256, 128
T = B * L
P = 128
NT = T // P
CH = 512
NC = T // CH
DI, NS, DTR, TAPS = 256, 16, 64, 4
PAD = TAPS - 1
E, F = 8, 512
FC = F // P
H, HD = 16, 8
NB = 4
MT = 24
EPS = 1e-5
QSCALE = float(np.float32(1.0) / np.sqrt(np.float32(HD)))
QPART = (0, 0, 1, 0, 2, 1)
KPART = (0, 1, 0, 2, 0, 1)
KR = len(QPART) * HD
KMAX = KR + 3
KEXP = KMAX + 2
BLOB = 2 * F + D + FC + 2
O_W2, O_B2, O_B1, O_GB = F, 2 * F, 2 * F + D, 2 * F + D + FC


class Chain:

    def __init__(self, eng, sem):
        self.eng, self.sem, self.base, self.n = eng, sem, 0, 0

    def loop(self, i, steps):
        self.start, self.steps = self.base + self.n, steps
        self.base, self.n = i * steps + self.start, 0

    def end(self, count):
        assert self.n == self.steps, (self.n, self.steps)
        self.base, self.n = self.start + count * self.steps, 0

    def link(self, ins):
        self.n += 1
        ins.then_inc(self.sem, 1)
        self.eng.wait_ge(self.sem, self.base + self.n)


def build(nc, a, out):
    fp32, bf16, i32 = mybir.dt.float32, mybir.dt.bfloat16, mybir.dt.int32
    ALU, ACT, AX = mybir.AluOpType, mybir.ActivationFunctionType, mybir.AxisListType
    ds, ts = bass.ds, bass.ts
    ctx = ExitStack()
    with ctx:
        def sb(name, shape, dt=fp32):
            return ctx.enter_context(nc.sbuf_tensor(name, shape, dt))

        def dram(name, shape, dt=fp32):
            return nc.dram_tensor(name, shape, dt, kind="Internal").ap()

        sems = {}

        def s(name):
            if name not in sems:
                sems[name] = ctx.enter_context(nc.semaphore(name))
            return sems[name]

        x = sb("x", [P, T])
        xn = sb("xn", [P, T])
        hT = sb("hT", [P, B, PAD + L])
        ident = sb("ident", [P, P])
        tri = sb("tri", [P, P], bf16)
        ones_b = sb("ones_b", [P, P], bf16)
        ones_f = sb("ones_f", [P, P])
        epst = sb("epst", [P, 1])
        stats = sb("stats", [P, NT * 6])
        meanvar = sb("meanvar", [P, NT * 2])
        std = sb("std", [P, NT])
        rstd = sb("rstd", [P, NT])
        cT = sb("cT", [P, 2 * B])
        silc = sb("silc", [P, 2 * B])
        wmod = sb("wmod", [P, 2, 6 * D])
        modT = sb("modT", [P, 2, 2, B])
        modrow = sb("modrow", [P, B, 4, D])
        inw = sb("inw", [P, 2 * DI])
        convw = sb("convw", [P, TAPS, DI])
        convb = sb("convb", [P, 2])
        wtap = sb("wtap", [P, TAPS, DI])
        xpw = sb("xpw", [P, 2, DTR + 2 * NS])
        xbc = sb("xbc", [P, 2, P])
        dtw = sb("dtw", [DTR, DI])
        dtb = sb("dtb", [P, 2])
        adj = sb("adj", [P, 2, DI])
        alog = sb("alog", [P, 2 * NS])
        aneg = sb("aneg", [P, 2 * NS])
        dskip = sb("dskip", [P, 2])
        outw = sb("outw", [P, 2, D])
        bc = sb("bc", [P, T], bf16)
        pick = sb("pick", [P, 2 * NS, P], bf16)
        dA = [sb(f"dA{k}", [P, 2, L]) for k in (0, 1)]
        tmp = sb("tmp", [P, CH])
        big = sb("big", [P, 8 * T])
        scr = sb("scr", [P, 14, CH])
        cent = sb("cent", [P, 2, E])
        br = sb("br", [P, E])
        iot = sb("iot", [P, MT], i32)
        kth = sb("kth", [P, MT])
        down = sb("down", [P, E])
        lgt = sb("lgt", [P, NT, E])
        oh = sb("oh", [P, NT, E])
        ohb = sb("ohb", [P, NT * E], bf16)
        rt = sb("rt", [P, NT, E])
        smax = sb("smax", [P, NT])
        m16 = sb("m16", [P, NT])
        et = sb("et", [P, E, NT])
        incl = sb("incl", [P, E, NT])
        seg = sb("seg", [P, E, NT])
        ntile = sb("ntile", [P, E])
        tend = sb("tend", [P, E])
        tbeg = sb("tbeg", [P, E])
        kcmp = sb("kcmp", [P, MT, E])
        exf = sb("exf", [P, MT])
        exi = sb("exi", [P, MT], i32)
        posf = sb("posf", [P, NT])
        posi = sb("posi", [P, NT], i32)
        wgt = sb("wgt", [P, NT])
        aw = sb("aw", [P, 4, P])
        ab = sb("ab", [P, 2])
        arow = sb("arow", [P, 2, D])
        vaug = sb("vaug", [P, NT, H, HD + 1])

        pb = [ctx.enter_context(nc.psum_tensor(f"pb{k}", [P, CH], fp32)) for k in range(8)]

        xs_d = [dram(f"xs{k}", (MT * P, D)) for k in (0, 1)]
        ys_d = [dram(f"ys{k}", (MT * P, D)) for k in (0, 1)]
        qk_d = dram("qk_parts", (2, KR // HD, HD, H, T), bf16)

        xi = big[:, 0:2 * T].rearrange("p (h t) -> p h t", h=2)
        gres = big[:, 2 * T:4 * T].rearrange("p (h t) -> p h t", h=2)
        dlt = big[:, 4 * T:6 * T].rearrange("p (h t) -> p h t", h=2)
        u = big[:, 6 * T:8 * T].rearrange("p (h t) -> p h t", h=2)
        srep = scr[:, 0:2, :].rearrange("p a (c m) -> p (a c) m", m=P)
        drs = scr[0:DTR, 0, :]
        sp_e = [scr[:, 1 + h, :] for h in (0, 1)]
        sp_l = [scr[:, 3 + h, :] for h in (0, 1)]
        sp_t = [scr[:, 5 + h, :] for h in (0, 1)]
        delta = [scr[:, 7 + h, :] for h in (0, 1)]
        bcr = scr[:, 9, :]
        dBu = [scr[:, k, :] for k in (0, 1)]
        hs = [scr[:, k, :] for k in (2, 3, 12, 13)]
        hc = [scr[:, k, :] for k in (4, 5)]
        bsb = [scr[:, k, :] for k in (6, 7)]
        yg = [scr[:, k, :] for k in (8, 9)]
        yt = [scr[:, k, :] for k in (10, 11)]
        blob = [big[:, k * BLOB:(k + 1) * BLOB] for k in range(NB)]
        e0 = NB * BLOB
        xt = [big[:, e0 + k * P:e0 + (k + 1) * P] for k in range(NB)]
        xtT = [big[:, e0 + (NB + k) * P:e0 + (NB + k + 1) * P] for k in range(NB)]
        ysb = [big[:, e0 + (2 * NB + k) * P:e0 + (2 * NB + k + 1) * P] for k in range(NB)]
        h1 = [big[:, e0 + 3 * NB * P + k * F:e0 + 3 * NB * P + (k + 1) * F] for k in range(NB)]
        assert e0 + 3 * NB * P + NB * F <= 5 * T
        h2 = big[:, 5 * T:6 * T]
        h2T = big[:, 6 * T:7 * T]
        yall = big[:, 7 * T:8 * T]
        qA = [big[:, k * T:(k + 1) * T].bitcast(bf16).rearrange("p (h l) -> p h l", h=H) for k in (0, 1)]
        kA = [big[:, k * T:(k + 1) * T].bitcast(bf16).rearrange("p (h l) -> p h l", h=H) for k in (2, 3)]
        parts = [[big[:, (8 + 3 * qk + p_) * T // 2:(9 + 3 * qk + p_) * T // 2].bitcast(bf16)
                  for p_ in range(3)] for qk in (0, 1)]
        qf = [scr[:, k, :] for k in (0, 1)]
        qr = [scr[:, k, :] for k in (2, 3)]
        pexp = [scr[:, k, :] for k in range(4, 8)]
        osb = scr[:, 8, 0:2 * D]
        oT = scr[:, 8, 2 * D:4 * D]
        mx = scr[:, 9, 0:2 * H]
        mneg = scr[:, 9, 2 * H:4 * H]
        rden = scr[:, 9, 4 * H:6 * H]
        mpart = scr[0:2 * H, 10, 0:P].bitcast(bf16)
        osum = scr[:, 11, 0:2 * D]

        W_LOADS = [
            (cT[:, :], a["cT"]), (wmod[:, :, :], a["wmod"]), (inw[:, :], a["in_w"]),
            (convw[:, :, :], a["conv_w"]), (convb[:, :], a["conv_b"]), (alog[:, :], a["A_log"]),
            (xpw[:, :, :], a["xp_w"]), (xbc[:, :, :], a["xbc_w"]),
            (dtw[:, :], a["dt_w"]), (dtb[:, :], a["dt_b"]), (adj[:, :, :], a["adj"]),
            (dskip[:, :], a["d_skip"]), (outw[:, :, :], a["out_w"]), (cent[:, :, :], a["router_w"]),
            (br[:, :], a["br"]), (aw[:, :, :], a["attn_w"]), (ab[:, :], a["attn_b"]), (arow[:, :, :], a["attn_row"]),
        ]
        ALL_W = 16 * len(W_LOADS)
        CONSTS = 12

        def apart(eng):
            eng.sem_inc(s("apart"), 1)

        block = ctx.enter_context(nc.Block())

        @block.sync
        def _(sp):
            for q in range(NC):
                sp.dma_start(x[:, q * CH:(q + 1) * CH].rearrange("p (t d) -> p t d", d=D),
                             a["x"][q * CH:(q + 1) * CH, :].rearrange("(t p) d -> p t d", p=P)).then_inc(s("x_in"), 16)
            for dst, src in W_LOADS:
                sp.dma_start(dst, src).then_inc(s("w_in"), 16)
            sp.wait_ge(s("zeroed"), 1)
            for k in range(2):
                for m in range(2):
                    sp.dma_start(xs_d[k][m * 12 * P:(m + 1) * 12 * P, :].rearrange("(t p) d -> p t d", p=P),
                                 big[:, 6 * T:6 * T + 12 * P].rearrange("p (t d) -> p t d", d=D)
                                 ).then_inc(s("zeros_out"), 16)

            def experts(k):
                sp.wait_ge(s(f"f{k}_tiles"), 1)
                sp.wait_ge(s(f"f{k}_xs_out"), 16 * NT)

                def load(t, m, first):
                    if not first:
                        sp.wait_ge(s(f"f{k}_ys"), t - NB + 1)
                    e = sp.value_load(exi[0:1, ds(t, 1)], min_val=0, max_val=E - 1)
                    sp.dma_start(blob[m], a[f"blob{k}"][ds(e, 1), :, :].rearrange("a p c -> (a p) c")
                                 ).then_inc(s(f"f{k}_in{m}"), 16)
                    sp.dma_start(xt[m], xs_d[k][ds(t * P, P), :]).then_inc(s(f"f{k}_in{m}"), 16)

                for m in range(NB):
                    load(m, m, True)
                with sp.Fori(1, MT // NB) as i:
                    for m in range(NB):
                        load(i * NB + m, m, False)

            experts(0)

            for qk in range(2):
                sp.wait_ge(s("parts"), NC * (qk + 1))
                for c, part in enumerate((QPART, KPART)[qk]):
                    sp.dma_start(qk_d[qk, c, :, :, :].rearrange("d h t -> h d t"),
                                 parts[qk][part]).then_inc(s("parts_out"), 16)
            sp.wait_ge(s("parts_out"), 16 * 2 * len(QPART))
            for m in range(2):
                sp.dma_start(qA[m][KR:KMAX, :, :], a["one_rows"][0:3, :, :]).then_inc(s("rows_in"), 16)
                sp.dma_start(kA[m][KR:KMAX, :, :], a["bias_rows"]).then_inc(s("rows_in"), 16)
                sp.dma_start(kA[m][KMAX:KEXP, :, :], a["one_rows"][3:5, :, :]).then_inc(s("rows_in"), 16)

            def load_qk(b, m):
                for dst, qk in ((qA[m], 0), (kA[m], 1)):
                    sp.dma_start(dst[0:KR, :, :],
                                 qk_d[qk, :, :, :, ds(b * L, L)].rearrange("c d h l -> (c d) h l")
                                 ).then_inc(s(f"qk_in{m}"), 16)

            def load_max(b, m):
                sp.wait_ge(s("mparts"), b + 1)
                for r in range(2):
                    sp.dma_start(qA[m][KMAX + r:KMAX + r + 1, :, :].rearrange("p h l -> p (h l)"),
                                 mpart[:, r * P:(r + 1) * P]).then_inc(s("max_in"), 16)

            load_qk(0, 0)
            load_max(0, 0)
            load_qk(1, 1)
            load_max(1, 1)
            with sp.Fori(0, (B - 2) // 2) as i:
                for m in range(2):
                    b = i * 2 + (2 + m)
                    sp.wait_ge(s("sT"), (b - 1) * H)
                    load_qk(b, m)
                    load_max(b, m)

            experts(1)

            for q in range(NC):
                sp.wait_ge(s("x_final"), 2 * (q + 1))
                sp.dma_start(out[q * CH:(q + 1) * CH, :].rearrange("(t p) d -> p t d", p=P),
                             x[:, q * CH:(q + 1) * CH].rearrange("p (t d) -> p t d", d=D)).then_inc(s("out_done"), 16)
            sp.wait_ge(s("out_done"), 16 * NC)

        @block.gpsimd
        def _(pool):
            chain = Chain(pool, s("pool_step"))
            nc.gpsimd.memset(big[:, 6 * T:6 * T + 12 * P], 0.0).then_inc(s("zeroed"), 1)
            chain.link(nc.gpsimd.memset(ident[:, :], 0.0))
            nc.gpsimd.affine_select(out=ident[:, :], in_=ident[:, :], compare_op=ALU.not_equal, fill=1.0,
                                    base=0, pattern=[[-1, P]], channel_multiplier=1).then_inc(s("consts"), 1)
            nc.gpsimd.memset(ones_f[:, :], 1.0).then_inc(s("consts"), 1)
            nc.gpsimd.memset(epst[:, :], EPS).then_inc(s("consts"), 1)
            nc.gpsimd.memset(hT[:, :, 0:PAD], 0.0).then_inc(s("consts"), 1)
            for k in range(2):
                nc.gpsimd.memset(dA[k][:, :, 0:1], 0.0).then_inc(s("consts"), 1)
            chain.link(nc.gpsimd.memset(pick[:, :, :], 0.0))
            for off in (0, 64):
                chain.link(nc.gpsimd.affine_select(
                    out=pick[:, :, :], in_=pick[:, :, :], compare_op=ALU.not_equal, fill=1.0,
                    base=-off, pattern=[[-1, 2 * NS], [0, P]], channel_multiplier=1))
            nc.gpsimd.affine_select(
                out=pick[:, :, :], in_=pick[:, :, :], compare_op=ALU.not_equal, fill=1.0,
                base=-96, pattern=[[-1, 2 * NS], [0, P]], channel_multiplier=1).then_inc(s("consts"), 1)
            chain.link(nc.gpsimd.memset(ones_b[:, :], 1.0))
            nc.gpsimd.affine_select(out=tri[:, :], in_=ones_b[:, :], compare_op=ALU.is_gt, fill=0.0,
                                    base=0, pattern=[[1, P]], channel_multiplier=-1).then_inc(s("consts"), 1)
            chain.link(nc.gpsimd.iota(iot[:, :], pattern=[[1, MT]], base=0, channel_multiplier=0))
            chain.link(nc.gpsimd.tensor_copy(kth[:, :], iot[:, :]))
            nc.gpsimd.tensor_scalar(down[:, :], kth[:, 0:E], -1.0, float(E), ALU.mult, ALU.add).then_inc(s("consts"), 1)
            chain.link(nc.gpsimd.memset(seg[:, :, :], 1.0))
            nc.gpsimd.memset(seg[:, :, 0:1], 0.0).then_inc(s("consts"), 1)
            nc.gpsimd.memset(bc[:, :], 0.0).then_inc(s("consts"), 1)
            nc.gpsimd.memset(vaug[:, :, :, HD:HD + 1], 1.0).then_inc(s("consts"), 1)

            pool.wait_ge(s("u"), 2 * NC)
            with pool.Fori(0, NC) as c:
                for n in range(NS):
                    pool.wait_ge(s("bsb"), c * NS + (n + 1))
                    for h in range(2):
                        step = c * 2 * NS + (2 * n + h)
                        if n:
                            pool.wait_ge(s("scan"), step - 1)
                        else:
                            pool.wait_ge(s("scan"), c * 2 * NS)
                        apart(pool)
                        nc.gpsimd.tensor_tensor(dBu[h], u[:, h, ts(c, CH)], bsb[n % 2], ALU.mult
                                                ).then_inc(s("dBu"), 1)

            def experts(k, rows):
                pool.wait_ge(s("zeros_out"), 64)
                pool.wait_ge(s(f"f{k}_pos"), 1)
                for t in range(NT):
                    nc.gpsimd.indirect_dma_start(
                        out=xs_d[k], out_offset=bass.IndirectOffsetOnAxis(ap=posi[:, t:t + 1], axis=0),
                        in_=rows[:, t * P:(t + 1) * P], in_offset=None).then_inc(s(f"f{k}_xs_out"), 16)
                with pool.Fori(0, MT // NB) as i:
                    for m in range(NB):
                        t = i * NB + m
                        pool.wait_ge(s(f"f{k}_ys"), t + 1)
                        pool.dma_start(ys_d[k][ds(t * P, P), :], ysb[m]).then_inc(s(f"f{k}_ys_out{m}"), 16)
                for m in range(NB):
                    pool.wait_ge(s(f"f{k}_ys_out{m}"), 16 * MT // NB)
                for t in range(NT):
                    nc.gpsimd.indirect_dma_start(
                        out=yall[:, t * P:(t + 1) * P], out_offset=None, in_=ys_d[k],
                        in_offset=bass.IndirectOffsetOnAxis(ap=posi[:, t:t + 1], axis=0)).then_inc(s(f"f{k}_y_in"), 16)

            experts(0, xn)
            experts(1, h2)

        @block.scalar
        def _(act):
            chain = Chain(act, s("act_step"))
            act.wait_ge(s("w_in"), ALL_W)
            act.wait_ge(s("consts"), CONSTS)

            def ln_std(key):
                act.wait_ge(s(f"{key}_mv"), NT)
                nc.scalar.activation(std[:, :], meanvar[:, 1::2], ACT.Sqrt, bias=epst[:, 0:1]).then_inc(s(f"{key}_std"), 1)

            def modulate(key, k):
                with act.Fori(0, B // 2) as i:
                    for m in range(2):
                        b = i * 2 + m
                        act.wait_ge(s(f"{key}_xT"), b + 1)
                        apart(act)
                        nc.scalar.activation(hT[:, ds(b, 1), PAD:PAD + L].rearrange("p a l -> p (a l)"), pb[m][:, 0:L],
                                             ACT.Identity, scale=modT[:, k, 1, ds(b, 1)],
                                             bias=modT[:, k, 0, ds(b, 1)]).then_inc(s(f"{key}_hT"), 1)

            def mod_rows(k):
                for b in range(B):
                    act.wait_ge(s(f"m{k}_ps"), b + 1)
                    nc.scalar.activation(modrow[:, b, :, :].rearrange("p k d -> p (k d)"), pb[6 + b % 2][:, :],
                                         ACT.Copy).then_inc(s(f"m{k}_cp"), 1)

            chain.link(nc.scalar.activation(aneg[:, :], alog[:, :], ACT.Exp))
            nc.scalar.mul(aneg[:, :], aneg[:, :], -1.0).then_inc(s("aneg"), 1)
            nc.scalar.activation(silc[:, :], cT[:, :], ACT.Silu).then_inc(s("silc"), 1)
            mod_rows(0)
            ln_std("ln0")
            act.wait_ge(s("modT"), 2)
            modulate("ln0", 0)

            nc.scalar.preload_act_table(ACT.Silu)
            with act.Fori(0, NC) as c:
                for h in range(2):
                    act.wait_ge(s("inproj"), c * 4 + (h + 1))
                    apart(act)
                    nc.scalar.activation(xi[:, h, ts(c, CH)], pb[2 + h][:, :], ACT.Silu, bias=convb[:, h:h + 1]
                                         ).then_inc(s("xi"), 1)
                for h in range(2):
                    act.wait_ge(s("inproj"), c * 4 + (h + 3))
                    apart(act)
                    nc.scalar.activation(gres[:, h, ts(c, CH)], pb[4 + h][:, :], ACT.Silu).then_inc(s("xi"), 1)

            nc.scalar.preload_act_table(ACT.Ln)
            with act.Fori(0, NC) as c:
                chain.loop(c, 6)
                act.wait_ge(s("draw"), c + 1)
                act.wait_ge(s("dtp"), c * 2)
                nc.scalar.activation(drs, pb[6][0:DTR, :], ACT.Copy).then_inc(s("drs"), 1)
                act.wait_ge(s("delta"), c)
                for h in range(2):
                    act.wait_ge(s("dtp"), c * 2 + (h + 1))
                    chain.link(nc.scalar.activation(sp_t[h], pb[h][:, :], ACT.Identity, bias=dtb[:, h:h + 1]))
                    chain.link(nc.scalar.activation(sp_e[h], sp_t[h], ACT.Abs))
                    chain.link(nc.scalar.activation(sp_e[h], sp_e[h], ACT.Exp, scale=-1.0))
                    nc.scalar.activation(sp_l[h], sp_e[h], ACT.Ln, bias=1.0).then_inc(s("spl"), 1)
                for h in range(2):
                    act.wait_ge(s("adjp"), c * 2 + (h + 1))
                    apart(act)
                    nc.scalar.activation(dlt[:, h, ts(c, CH)], pb[2 + h][:, :], ACT.Copy).then_inc(s("dlt"), 1)
            chain.end(NC)

            act.wait_ge(s("dlt"), 2 * NC)
            with act.Fori(0, NC) as c:
                for n in range(NS):
                    act.wait_ge(s("bbp"), c * NS + (n + 1))
                    if n:
                        act.wait_ge(s("dBu"), c * 2 * NS + (2 * n - 2))
                    else:
                        act.wait_ge(s("dBu"), c * 2 * NS)
                    nc.scalar.activation(bsb[n % 2], pb[n % 2][:, :], ACT.Copy).then_inc(s("bsb"), 1)
                    for h in range(2):
                        if n:
                            act.wait_ge(s("scan"), c * 2 * NS + (2 * n + h - 1))
                        else:
                            act.wait_ge(s("scan"), c * 2 * NS)
                        apart(act)
                        nc.scalar.activation(
                            dA[h][:, :, 1:L], dlt[:, h, ts(c, CH)].rearrange("p (b l) -> p b l", b=2)[:, :, 1:L],
                            ACT.Exp, scale=aneg[:, h * NS + n:h * NS + n + 1]).then_inc(s("dA"), 1)

            def router(k, h2_key):
                with act.Fori(0, B // 2) as i:
                    for m in range(2):
                        b = i * 2 + m
                        act.wait_ge(s(f"f{k}_h2Tp"), b + 1)
                        apart(act)
                        nc.scalar.activation(h2T[:, ts(b, L)], pb[m][:, 0:L], ACT.Copy).then_inc(s(f"f{k}_h2T"), 1)

            def experts(k, func):
                nc.scalar.preload_act_table(func)
                def tile(i, m, first):
                    t = i * NB + m
                    if not first:
                        act.wait_ge(s(f"f{k}_yp"), t - NB + 1)
                    act.wait_ge(s(f"f{k}_in{m}"), i * 32 + 32)
                    act.wait_ge(s(f"f{k}_hid"), t + 1)
                    for f in range(FC):
                        nc.scalar.activation(h1[m][:, f * P:(f + 1) * P], pb[2 + m % 2][:, f * P:(f + 1) * P], func,
                                             bias=blob[m][:, O_B1 + f:O_B1 + f + 1]).then_inc(s(f"f{k}_h1"), 1)
                for m in range(NB):
                    tile(0, m, True)
                with act.Fori(1, MT // NB) as i:
                    for m in range(NB):
                        tile(i, m, False)

            ln_std("ln1")
            ln_std("lnf")
            router(0, None)
            act.wait_ge(s("f0_nmax"), 1)
            nc.scalar.activation(m16[:, :], smax[:, :], ACT.Exp, scale=-1.0).then_inc(s("f0_e"), 1)
            experts(0, ACT.Relu)

            act.wait_ge(s("x_f0"), B)
            mod_rows(1)
            ln_std("ln2")
            modulate("ln2", 1)
            act.wait_ge(s("abs"), 1)
            for qk in range(2):
                with act.Fori(0, NC // 2) as i:
                    for m in range(2):
                        c = i * 2 + m
                        act.wait_ge(s("qkp"), c + (NC * qk + 1))
                        act.wait_ge(s("parts"), i * 2 + NC * qk)
                        nc.scalar.activation(qf[m], pb[2 + m][:, :], ACT.Identity, bias=ab[:, qk:qk + 1],
                                             scale=QSCALE if qk == 0 else 1.0).then_inc(s("qf"), 1)
            nc.scalar.preload_act_table(ACT.Exp)

            def attn(b, first):
                for h in range(H):
                    act.wait_ge(s("sT"), b * H + (h + 1))
                    if not (first and h < 4):
                        act.wait_ge(s("pv"), b * H + (h - 3))
                    nc.scalar.activation(pexp[h % 4], pb[2 + h % 2][:, :], ACT.Exp).then_inc(s("pT"), 1)
                    if h == 4 and not first:
                        out_T(b - 1)

            def out_T(b):
                act.wait_ge(s("oTp"), b + 1)
                nc.scalar.activation(oT, pb[6][:, 0:L], ACT.Copy).then_inc(s("oT"), 1)

            attn(0, True)
            with act.Fori(0, (B - 2) // 2) as i:
                for m in range(2):
                    attn(i * 2 + (1 + m), False)
            attn(B - 1, False)
            out_T(B - 1)

            ln_std("ln3")
            router(1, None)
            act.wait_ge(s("f1_nmax"), 1)
            nc.scalar.activation(rt[:, :, :], lgt[:, :, :], ACT.Exp).then_inc(s("f1_e"), 1)
            experts(1, ACT.Gelu)

        @block.vector
        def _(dve):
            chain = Chain(dve, s("dve_step"))
            V = nc.vector

            def layernorm(key, src, dst):
                with dve.Fori(0, NT) as i:
                    chain.loop(i, 1)
                    chain.link(V.bn_stats(stats[:, ts(i, 6)], src[:, ts(i, P)]))
                chain.end(NT)
                for t in range(NT):
                    V.bn_aggr(meanvar[:, 2 * t:2 * t + 2], stats[:, 6 * t:6 * t + 6]).then_inc(s(f"{key}_mv"), 1)
                dve.wait_ge(s(f"{key}_std"), 1)
                chain.link(V.reciprocal(rstd[:, :], std[:, :]))
                with dve.Fori(0, NT) as i:
                    V.tensor_scalar(dst[:, ts(i, P)], src[:, ts(i, P)], meanvar[:, ds(i * 2, 1)], rstd[:, ds(i, 1)],
                                    ALU.subtract, ALU.mult).then_inc(s(f"{key}_xn"), 1)

            def repeat_c(k):
                for b in range(B):
                    V.tensor_scalar(srep[:, b, :], ones_f[:, :], silc[:, k * B + b:k * B + b + 1], None,
                                    ALU.mult).then_inc(s(f"m{k}_rep"), 1)

            def mod_rows(k):
                dve.wait_ge(s(f"m{k}_cp"), B)
                chain.link(V.tensor_scalar(modrow[:, :, 2, :], modrow[:, :, 2, :], 1.0, None, ALU.add))
                for j in (0, 3):
                    for hb in range(2):
                        g = modrow[:, 4 * hb:4 * hb + 4, j, :]
                        sign = tmp[:, :].rearrange("p (b d) -> p b d", b=4)
                        chain.link(V.tensor_scalar(sign, g, 0.0, 0.5, ALU.is_ge, ALU.subtract))
                        chain.link(V.scalar_tensor_tensor(g, g, -1.0, g, ALU.mult, ALU.max))
                        chain.link(V.tensor_scalar(g, g, 0.25, 2.0, ALU.max, ALU.mult))
                        chain.link(V.tensor_tensor(g, g, sign, ALU.mult))

            dve.wait_ge(s("w_in"), ALL_W)
            dve.wait_ge(s("consts"), CONSTS)
            dve.wait_ge(s("silc"), 1)
            repeat_c(0)
            for tap in range(TAPS):
                V.tensor_tensor(wtap[:, tap, :], inw[:, 0:DI], convw[:, tap, :], ALU.mult).then_inc(s("wtap"), 1)
            dve.wait_ge(s("modTp"), 1)
            for j in range(2):
                V.tensor_scalar(modT[:, :, j, :], pb[5][:, 0:4 * B].rearrange("p (k j b) -> p k j b", k=2, j=2)[:, :, j, :],
                                float(j), None, ALU.add).then_inc(s("modT"), 1)
            dve.wait_ge(s("x_in"), 16 * NC)
            layernorm("ln0", x, xn)
            mod_rows(0)

            dve.wait_ge(s("zeros_out"), 64)
            with dve.Fori(0, NC) as c:
                chain.loop(c, 4)
                dve.wait_ge(s("bcp"), c + 1)
                t = ts(c, CH)
                apart(dve)
                V.tensor_copy(bc[0:32, t], pb[7][0:32, :])
                chain.link(V.tensor_copy(bc[64:128, t], pb[7][64:128, :]))
                chain.link(V.tensor_tensor(bcr[64:128, :], pb[7][64:128, :], bc[64:128, t], ALU.subtract))
                apart(dve)
                chain.link(V.tensor_copy(bc[64:128, t], bcr[64:128, :]))
                chain.link(V.tensor_tensor(bcr[96:128, :], bcr[96:128, :], bc[96:128, t], ALU.subtract))
                apart(dve)
                V.tensor_copy(bc[96:128, t], bcr[96:128, :]).then_inc(s("bc"), 1)
                dve.wait_ge(s("spl"), c * 2 + 2)
                dve.wait_ge(s("adjp"), c * 2)
                for h in range(2):
                    last = V.scalar_tensor_tensor(delta[h], sp_t[h], 0.0, sp_l[h], ALU.max, ALU.add)
                last.then_inc(s("delta"), 1)
                for h in range(2):
                    dve.wait_ge(s("dlt"), c * 2 + (h + 1))
                    V.tensor_tensor(u[:, h, ts(c, CH)], dlt[:, h, ts(c, CH)], xi[:, h, ts(c, CH)], ALU.mult).then_inc(s("u"), 1)
            chain.end(NC)

            with dve.Fori(0, NC) as c:
                chain.loop(c, 3)

                def scan(n, h):
                    step = c * 2 * NS + (2 * n + h)
                    dve.wait_ge(s("dA"), step + 1)
                    dve.wait_ge(s("dBu"), step + 1)
                    dve.wait_ge(s("hc"), c * 2 * NS + max(2 * n + h - 3, 0))
                    V.tensor_tensor_scan(hs[(2 * n + h) % 4], dA[h][:, :, :].rearrange("p b l -> p (b l)"), dBu[h], 0.0,
                                         ALU.mult, ALU.add).then_inc(s("scan"), 1)

                def times_c(n, h):
                    step = c * 2 * NS + (2 * n + h)
                    dve.wait_ge(s("scan"), step + 1)
                    dve.wait_ge(s("cbp"), c * NS + (n + 1))
                    dve.wait_ge(s("hsum"), step - 1 if n else c * 2 * NS)
                    V.tensor_tensor(hc[h], hs[(2 * n + h) % 4], pb[2 + n % 2][:, :], ALU.mult).then_inc(s("hc"), 1)

                scan(0, 0)
                for n in range(NS):
                    scan(n, 1)
                    times_c(n, 0)
                    if n + 1 < NS:
                        scan(n + 1, 0)
                    times_c(n, 1)
                dve.wait_ge(s("outp"), c)
                for h in range(2):
                    dve.wait_ge(s("hsum"), c * 2 * NS + (2 * NS - 1 + h))
                    chain.link(V.scalar_tensor_tensor(yt[h], xi[:, h, ts(c, CH)], dskip[:, h:h + 1], pb[4 + h][:, :],
                                                      ALU.mult, ALU.add))
                    V.tensor_tensor(yg[h], yt[h], gres[:, h, ts(c, CH)], ALU.mult).then_inc(s("yg"), 1)
                dve.wait_ge(s("outp"), c + 1)
                for t in range(CH // P):
                    last = V.tensor_tensor(tmp[:, t * P:(t + 1) * P], pb[6][:, t * P:(t + 1) * P],
                                           modrow[:, ds(c * 2 + t // 2, 1), 0, :].rearrange("p a d -> p (a d)"), ALU.mult)
                chain.link(last)
                V.tensor_tensor(x[:, ts(c, CH)], x[:, ts(c, CH)], tmp[:, :], ALU.add).then_inc(s("x_a"), 1)
            chain.end(NC)

            def modulate_rows(k):
                with dve.Fori(0, B) as b:
                    chain.loop(b, 2)
                    rows = h2[:, ts(b, L)].rearrange("p (t d) -> p t d", d=D)
                    for t in range(2):
                        last = V.tensor_tensor(h2[:, ds(b * L + t * D, D)], xn[:, ds(b * L + t * D, D)],
                                               modrow[:, ds(b, 1), 2, :].rearrange("p a d -> p (a d)"), ALU.mult)
                    chain.link(last)
                    for t in range(2):
                        last = V.tensor_tensor(h2[:, ds(b * L + t * D, D)], h2[:, ds(b * L + t * D, D)],
                                               modrow[:, ds(b, 1), 1, :].rearrange("p a d -> p (a d)"), ALU.add)
                    chain.link(last)
                    dve.sem_inc(s(f"f{k}_h2"), 1)
                chain.end(B)

            def router(k):
                dve.wait_ge(s(f"f{k}_sc"), 1)
                sc = pb[7][:, 0:NT * E].rearrange("p (t e) -> p t e", e=E)
                if k:
                    chain.link(V.tensor_tensor(lgt[:, :, :], sc, br[:, :].unsqueeze(1).to_broadcast([P, NT, E]), ALU.add))
                else:
                    chain.link(V.tensor_copy(lgt[:, :, :], sc))
                chain.link(V.tensor_reduce(smax[:, :], lgt[:, :, :], AX.X, ALU.max))
                mbc = smax[:, :].unsqueeze(2).to_broadcast([P, NT, E])
                chain.link(V.tensor_tensor(oh[:, :, :], lgt[:, :, :], mbc, ALU.is_ge))
                chain.link(V.tensor_tensor(oh[:, :, :], oh[:, :, :], down[:, :].unsqueeze(1).to_broadcast([P, NT, E]), ALU.mult))
                if k:
                    V.tensor_tensor(lgt[:, :, :], lgt[:, :, :], mbc, ALU.subtract).then_inc(s("f1_nmax"), 1)
                else:
                    dve.sem_inc(s("f0_nmax"), 1)
                chain.link(V.tensor_reduce(posf[:, :], oh[:, :, :], AX.X, ALU.max))
                chain.link(V.tensor_tensor(oh[:, :, :], oh[:, :, :], posf[:, :].unsqueeze(2).to_broadcast([P, NT, E]), ALU.is_equal))
                V.tensor_copy(ohb[:, :], oh[:, :, :].rearrange("p t e -> p (t e)")).then_inc(s(f"f{k}_oh"), 1)
                dve.wait_ge(s(f"f{k}_e"), 1)
                if k:
                    chain.link(V.tensor_reduce(m16[:, :], rt[:, :, :], AX.X, ALU.add))
                else:
                    chain.link(V.tensor_scalar(m16[:, :], m16[:, :], 1.0, None, ALU.add))
                chain.link(V.reciprocal(wgt[:, :], m16[:, :]))
                dve.wait_ge(s(f"f{k}_rank"), 2)
                chain.link(V.tensor_copy(et[:, :, :], pb[6][:, 0:NT * E].rearrange("p (t e) -> p e t", e=E)))
                flat = lambda v: v[:, :, :].rearrange("p e t -> p (e t)")
                chain.link(V.tensor_tensor_scan(flat(incl), flat(seg), flat(et), 0.0, ALU.mult, ALU.add))
                kk = kcmp[:, 0:NT, :].rearrange("p k e -> p e k")
                chain.link(V.tensor_scalar(exf[:, :], kth[:, :], float(P), None, ALU.mult))
                chain.link(V.tensor_tensor(kk, incl[:, :, NT - 1:NT].to_broadcast([P, E, NT]),
                                           exf[:, 0:NT].unsqueeze(1).to_broadcast([P, E, NT]), ALU.is_gt))
                chain.link(V.tensor_reduce(ntile[:, :], kk, AX.X, ALU.add))
                chain.link(V.tensor_tensor_scan(tend[:, :], ones_f[:, 0:E], ntile[:, :], 0.0, ALU.mult, ALU.add))
                chain.link(V.tensor_tensor(kcmp[:, :, :], kth[:, :].unsqueeze(2).to_broadcast([P, MT, E]),
                                           tend[:, :].unsqueeze(1).to_broadcast([P, MT, E]), ALU.is_ge))
                chain.link(V.tensor_reduce(exf[:, :], kcmp[:, :, :], AX.X, ALU.add))
                V.tensor_scalar(exi[:, :], exf[:, :], float(E - 1), None, ALU.min).then_inc(s(f"f{k}_tiles"), 1)
                chain.link(V.tensor_tensor(tbeg[:, :], tend[:, :], ntile[:, :], ALU.subtract))
                chain.link(V.tensor_tensor(flat(incl), flat(incl), flat(et), ALU.subtract))
                chain.link(V.scalar_tensor_tensor(incl[:, :, :], tbeg[:, :].unsqueeze(2).to_broadcast([P, E, NT]), float(P),
                                                  incl[:, :, :], ALU.mult, ALU.add))
                chain.link(V.tensor_tensor(rt[:, :, :], incl[:, :, :].rearrange("p e t -> p t e"),
                                           pb[5][:, 0:NT * E].rearrange("p (t e) -> p t e", e=E), ALU.add))
                chain.link(V.tensor_tensor(rt[:, :, :], rt[:, :, :], oh[:, :, :], ALU.mult))
                chain.link(V.tensor_reduce(posf[:, :], rt[:, :, :], AX.X, ALU.add))
                V.tensor_copy(posi[:, :], posf[:, :]).then_inc(s(f"f{k}_pos"), 1)

            def experts(k):
                def rows_T(i, m):
                    t = i * NB + m
                    dve.wait_ge(s(f"f{k}_in{m}"), i * 32 + 32)
                    dve.wait_ge(s(f"f{k}_xTp"), t + 1)
                    if k:
                        V.tensor_copy(xtT[m], pb[m % 2][:, 0:P]).then_inc(s(f"f{k}_xtT"), 1)
                    else:
                        V.tensor_scalar(xtT[m], pb[m % 2][:, 0:P], blob[m][:, O_GB:O_GB + 1], blob[m][:, O_GB + 1:O_GB + 2],
                                        ALU.mult, ALU.add).then_inc(s(f"f{k}_xtT"), 1)

                def rows_out(t, m, stored):
                    dve.wait_ge(s(f"f{k}_yp"), t + 1)
                    if stored is not None:
                        dve.wait_ge(s(f"f{k}_ys_out{m}"), stored * 16)
                    V.tensor_tensor(ysb[m], pb[4 + m % 2][:, 0:P], blob[m][:, O_B2:O_B2 + D], ALU.add).then_inc(s(f"f{k}_ys"), 1)

                for m in range(NB):
                    rows_T(0, m)
                    if m:
                        rows_out(m - 1, m - 1, None)
                with dve.Fori(1, MT // NB) as i:
                    for m in range(NB):
                        rows_T(i, m)
                        rows_out(i * NB + (m - 1), (m - 1) % NB, i if m else i - 1)
                rows_out(MT - 1, NB - 1, MT // NB - 1)

            def combine(k):
                dve.wait_ge(s(f"f{k}_y_in"), 16 * NT)
                with dve.Fori(0, B) as b:
                    chain.loop(b, 2)
                    dve.wait_ge(s("x_final" if k else "x_f0"), b)
                    for t in range(2):
                        col = ds(b * L + t * D, D)
                        w = wgt[:, ds(b * 2 + t, 1)]
                        if k == 0:
                            last = V.scalar_tensor_tensor(tmp[:, t * D:(t + 1) * D], yall[:, col], w, h2[:, col], ALU.mult, ALU.add)
                        else:
                            last = V.tensor_scalar(tmp[:, t * D:(t + 1) * D], yall[:, col], w, None, ALU.mult)
                    chain.link(last)
                    for t in range(2):
                        last = V.tensor_tensor(tmp[:, t * D:(t + 1) * D], tmp[:, t * D:(t + 1) * D],
                                               modrow[:, ds(b, 1), 3, :].rearrange("p a d -> p (a d)"), ALU.mult)
                    chain.link(last)
                    V.tensor_tensor(x[:, ts(b, L)], x[:, ts(b, L)], tmp[:, 0:L], ALU.add).then_inc(s("x_final" if k else "x_f0"), 1)
                chain.end(B)

            dve.wait_ge(s("x_a"), NC)
            layernorm("ln1", x, xn)
            dve.wait_ge(s("ln1_xn"), NT)
            modulate_rows(0)
            layernorm("lnf", h2, xn)
            router(0)
            experts(0)
            repeat_c(1)
            combine(0)
            mod_rows(1)
            dve.wait_ge(s("x_f0"), B)
            layernorm("ln2", x, xn)

            V.tensor_scalar(ab[:, 0:1], ab[:, 0:1], QSCALE, None, ALU.mult).then_inc(s("abs"), 1)
            for qk in range(2):
                with dve.Fori(0, NC // 2) as i:
                    chain.loop(i, 6)
                    for m in range(2):
                        c = i * 2 + m
                        t = ts(c, CH)
                        dve.wait_ge(s("qf"), c + (NC * qk + 1))
                        apart(dve)
                        chain.link(V.tensor_copy(parts[qk][0][:, t], qf[m]))
                        chain.link(V.tensor_tensor(qr[m], qf[m], parts[qk][0][:, t], ALU.subtract))
                        apart(dve)
                        chain.link(V.tensor_copy(parts[qk][1][:, t], qr[m]))
                        V.tensor_tensor(parts[qk][2][:, t], qr[m], parts[qk][1][:, t], ALU.subtract).then_inc(s("parts"), 1)
                chain.end(NC // 2)
            with dve.Fori(0, NC // 2) as i:
                for m in range(2):
                    c = i * 2 + m
                    dve.wait_ge(s("vp"), c + 1)
                    for t in range(CH // P):
                        last = V.tensor_tensor(vaug[:, ds(c * 4 + t, 1), :, 0:HD].rearrange("p a h d -> p (a h) d"),
                                               pb[4 + m][:, t * P:(t + 1) * P].rearrange("p (h d) -> p h d", d=HD),
                                               arow[:, 0, :].rearrange("p (h d) -> p h d", d=HD), ALU.add)
                    last.then_inc(s("v"), 1)

            def max_head(b, h):
                dve.wait_ge(s("maxp"), b * H + (h + 1))
                V.tensor_reduce(mx[:, 2 * h:2 * h + 2], pb[h % 2][:, :].rearrange("p (q l) -> p q l", q=2), AX.X, ALU.max
                                ).then_inc(s("mx"), 1)

            def max_rows(b):
                dve.wait_ge(s("mx"), b * H + H)
                V.tensor_scalar(mneg, mx, -1.0, None, ALU.mult).then_inc(s("mneg"), 1)
                dve.wait_ge(s("mT"), b + 1)
                dve.wait_ge(s("max_in"), b * 32)
                chain.link(V.tensor_copy(mpart[:, 0:P], pb[7][0:2 * H, 0:P]))
                V.tensor_tensor(mpart[:, P:2 * P], pb[7][0:2 * H, 0:P], mpart[:, 0:P], ALU.subtract).then_inc(s("mparts"), 1)

            def normalise(b, bank):
                dve.wait_ge(s("pv"), b * H + H)
                o = pb[bank][:, 0:2 * H * (HD + 1)].rearrange("p (g d) -> p g d", d=HD + 1)
                chain.link(V.reciprocal(rden.unsqueeze(2), o[:, :, HD:HD + 1]))
                V.tensor_tensor(osb.rearrange("p (g d) -> p g d", d=HD), o[:, :, 0:HD],
                                rden.unsqueeze(2).to_broadcast([P, 2 * H, HD]), ALU.mult).then_inc(s("osb"), 1)

            def residual(b):
                dve.wait_ge(s("aop"), b + 1)
                for q in range(2):
                    last = V.tensor_tensor(osum[:, q * D:(q + 1) * D], pb[6][:, L + q * D:L + (q + 1) * D], arow[:, 1, :], ALU.add)
                chain.link(last)
                for q in range(2):
                    last = V.tensor_tensor(osum[:, q * D:(q + 1) * D], osum[:, q * D:(q + 1) * D],
                                           modrow[:, ds(b, 1), 0, :].rearrange("p a d -> p (a d)"), ALU.mult)
                chain.link(last)
                V.tensor_tensor(x[:, ds(b * L, L)], x[:, ds(b * L, L)], osum, ALU.add).then_inc(s("x_b"), 1)

            def attn(b, m, first, last_b):
                if not first:
                    normalise(b - 1, 4 + (1 - m))
                if not last_b:
                    for h in range(H):
                        max_head(b + 1, h)
                        if h == 3 and not first:
                            residual(b - 1)
                    max_rows(b + 1)
                elif not first:
                    residual(b - 1)

            for h in range(H):
                max_head(0, h)
            max_rows(0)
            attn(0, 0, True, False)
            with dve.Fori(0, (B - 2) // 2) as i:
                chain.loop(i, 8)
                for m in (1, 0):
                    attn(i * 2 + (2 - m), m, False, False)
            chain.end((B - 2) // 2)
            attn(B - 1, 1, False, True)
            normalise(B - 1, 5)
            residual(B - 1)

            dve.wait_ge(s("x_b"), B)
            layernorm("ln3", x, xn)
            dve.wait_ge(s("ln3_xn"), NT)
            modulate_rows(1)
            router(1)
            experts(1)
            combine(1)

        @block.tensor
        def _(pe):
            mm = nc.tensor.matmul

            def mod_rows(k):
                pe.wait_ge(s(f"m{k}_rep"), B)
                for b in range(B):
                    if b >= 2:
                        pe.wait_ge(s(f"m{k}_cp"), b - 1)
                    mm(pb[6 + b % 2][:, :], srep[:, b, :], wmod[:, k, 2 * D:6 * D], start=True, stop=True).then_inc(s(f"m{k}_ps"), 1)

            def transposes(ready, src, done, used):
                for b in range(B):
                    pe.wait_ge(s(ready), (b + 1) * (2 if ready.startswith("ln") else 1))
                    if b >= 2:
                        pe.wait_ge(s(used), b - 1)
                    for t in range(2):
                        last = nc.tensor.transpose(pb[b % 2][:, t * P:(t + 1) * P], src[:, b * L + t * P:b * L + (t + 1) * P], ident[:, :])
                    last.then_inc(s(done), 1)

            pe.wait_ge(s("w_in"), ALL_W)
            pe.wait_ge(s("consts"), CONSTS)
            pe.wait_ge(s("silc"), 1)
            for k in range(2):
                for j in range(2):
                    col = (2 * k + j) * B
                    last = mm(pb[5][:, col:col + B], wmod[:, k, j * D:(j + 1) * D], silc[:, k * B:(k + 1) * B], start=True, stop=True)
            last.then_inc(s("modTp"), 1)
            mod_rows(0)
            transposes("ln0_xn", xn, "ln0_xT", "ln0_hT")

            pe.wait_ge(s("wtap"), TAPS)
            pe.wait_ge(s("modT"), 2)
            with pe.Fori(0, NC) as c:
                pe.wait_ge(s("ln0_hT"), c * 2 + 2)
                pe.wait_ge(s("xi"), c * 4)
                for h in range(2):
                    for tap in range(TAPS):
                        last = mm(pb[2 + h][:, :], wtap[:, tap, h * P:(h + 1) * P], hT[:, ds(c * 2, 2), tap:tap + L],
                                  start=(tap == 0), stop=(tap == TAPS - 1))
                    last.then_inc(s("inproj"), 1)
                for h in range(2):
                    mm(pb[4 + h][:, :], inw[:, DI + h * P:DI + (h + 1) * P], hT[:, ds(c * 2, 2), PAD:PAD + L],
                       start=True, stop=True).then_inc(s("inproj"), 1)

            with pe.Fori(0, NC) as c:
                t = ts(c, CH)
                pe.wait_ge(s("xi"), c * 4 + 4)
                pe.wait_ge(s("drs"), c)
                for h in range(2):
                    last = mm(pb[6][0:DTR, :], xpw[:, h, 0:DTR], xi[:, h, t], start=(h == 0), stop=(h == 1))
                last.then_inc(s("draw"), 1)
                pe.wait_ge(s("bc"), c)
                for h in range(2):
                    last = mm(pb[7][:, :], xbc[:, h, :], xi[:, h, t], start=(h == 0), stop=(h == 1))
                last.then_inc(s("bcp"), 1)
                pe.wait_ge(s("drs"), c + 1)
                pe.wait_ge(s("delta"), c)
                for h in range(2):
                    mm(pb[h][:, :], dtw[:, h * P:(h + 1) * P], drs, start=True, stop=True).then_inc(s("dtp"), 1)
                pe.wait_ge(s("delta"), c + 1)
                pe.wait_ge(s("dlt"), c * 2)
                pe.wait_ge(s("u"), c * 2)
                if True:
                    pe.wait_ge(s("xi"), 4 * NC)
                for h in range(2):
                    for g in range(2):
                        last = mm(pb[2 + h][:, :], adj[:, g, h * P:(h + 1) * P], delta[g], start=(g == 0), stop=(g == 1))
                    last.then_inc(s("adjp"), 1)

            pe.wait_ge(s("bc"), NC)
            pe.wait_ge(s("dlt"), 2 * NC)
            pe.wait_ge(s("u"), 2 * NC)
            with pe.Fori(0, NC) as c:
                t = ts(c, CH)

                def sum_state(n):
                    for h in range(2):
                        pe.wait_ge(s("hc"), c * 2 * NS + (2 * n + h + 1))
                        mm(pb[4 + h][:, :], ident[:, :], hc[h], start=(n == 0), stop=(n == NS - 1)).then_inc(s("hsum"), 1)

                for n in range(NS):
                    pe.wait_ge(s("bsb"), c * NS + (n - 1 if n else 0))
                    mm(pb[n % 2][:, :], pick[:, n, :], bc[:, t], start=True, stop=True).then_inc(s("bbp"), 1)
                    pe.wait_ge(s("hc"), c * 2 * NS + (2 * n - 2 if n else 0))
                    mm(pb[2 + n % 2][:, :], pick[:, NS + n, :], bc[:, t], start=True, stop=True).then_inc(s("cbp"), 1)
                    if n == 0:
                        pe.wait_ge(s("yg"), c * 2)
                    else:
                        sum_state(n - 1)
                sum_state(NS - 1)
                pe.wait_ge(s("yg"), c * 2 + 2)
                pe.wait_ge(s("x_a"), c)
                for q in range(CH // P):
                    for h in range(2):
                        last = mm(pb[6][:, q * P:(q + 1) * P], yg[h][:, q * P:(q + 1) * P], outw[:, h, :],
                                  start=(h == 0), stop=(h == 1))
                last.then_inc(s("outp"), 1)

            def router(k):
                transposes(f"f{k}_h2", h2, f"f{k}_h2Tp", f"f{k}_h2T")
                pe.wait_ge(s(f"f{k}_h2T"), B)
                for t in range(NT):
                    last = mm(pb[7][:, t * E:(t + 1) * E], h2T[:, t * P:(t + 1) * P], cent[:, k, :], start=True, stop=True)
                last.then_inc(s(f"f{k}_sc"), 1)
                pe.wait_ge(s(f"f{k}_oh"), 1)
                mm(pb[5][:, 0:NT * E], tri[:, :], ohb[:, :], start=True, stop=True).then_inc(s(f"f{k}_rank"), 1)
                mm(pb[6][:, 0:NT * E], ones_b[:, :], ohb[:, :], start=True, stop=True).then_inc(s(f"f{k}_rank"), 1)

            def experts(k):
                pe.wait_ge(s(f"f{k}_pos"), 1)

                def up(i, m):
                    t = i * NB + m
                    pe.wait_ge(s(f"f{k}_in{m}"), i * 32 + 32)
                    nc.tensor.transpose(pb[m % 2][:, 0:P], xt[m], ident[:, :]).then_inc(s(f"f{k}_xTp"), 1)
                    pe.wait_ge(s(f"f{k}_xtT"), t + 1)
                    for f in range(FC):
                        last = mm(pb[2 + m % 2][:, f * P:(f + 1) * P], blob[m][:, f * P:(f + 1) * P], xtT[m], start=True, stop=True)
                    last.then_inc(s(f"f{k}_hid"), 1)

                def down_(t, m, first):
                    pe.wait_ge(s(f"f{k}_h1"), t * FC + FC)
                    if not first:
                        pe.wait_ge(s(f"f{k}_ys"), t - 1)
                    for f in range(FC):
                        last = mm(pb[4 + m % 2][:, 0:P], h1[m][:, f * P:(f + 1) * P], blob[m][:, O_W2 + f * P:O_W2 + (f + 1) * P],
                                  start=(f == 0), stop=(f == FC - 1))
                    last.then_inc(s(f"f{k}_yp"), 1)

                for m in range(NB):
                    up(0, m)
                    if m:
                        down_(m - 1, m - 1, m < 3)
                with pe.Fori(1, MT // NB) as i:
                    for m in range(NB):
                        up(i, m)
                        down_(i * NB + (m - 1), (m - 1) % NB, False)
                down_(MT - 1, NB - 1, False)

            router(0)
            experts(0)
            mod_rows(1)
            transposes("ln2_xn", xn, "ln2_xT", "ln2_hT")

            pe.wait_ge(s("ln2_hT"), B)
            for qk in range(2):
                with pe.Fori(0, NC // 2) as i:
                    for m in range(2):
                        c = i * 2 + m
                        pe.wait_ge(s("qf"), i * 2 + NC * qk)
                        mm(pb[2 + m][:, :], aw[:, qk, :], hT[:, ds(c * 2, 2), PAD:PAD + L], start=True, stop=True).then_inc(s("qkp"), 1)
            for c in range(NC):
                if c >= 2:
                    pe.wait_ge(s("v"), c - 1)
                for t in range(CH // P):
                    last = mm(pb[4 + c % 2][:, t * P:(t + 1) * P],
                              hT[:, c * 2 + t // 2, PAD + (t % 2) * P:PAD + (t % 2 + 1) * P],
                              aw[:, 2, :], start=True, stop=True)
                last.then_inc(s("vp"), 1)
            pe.wait_ge(s("v"), NC)
            pe.wait_ge(s("rows_in"), 96)

            def max_scores(b, m, h, first):
                if not (first and h < 2):
                    pe.wait_ge(s("mx"), b * H + (h - 1))
                for q in range(2):
                    last = mm(pb[h % 2][:, q * L:(q + 1) * L], qA[m][0:KMAX, h, q * P:(q + 1) * P], kA[m][0:KMAX, h, :],
                              start=True, stop=True)
                last.then_inc(s("maxp"), 1)

            def max_T(b):
                pe.wait_ge(s("mneg"), b + 1)
                nc.tensor.transpose(pb[7][0:2 * H, 0:P], mneg, ident[:, :]).then_inc(s("mT"), 1)

            def exp_scores(b, m, h, first):
                if not (first and h < 2):
                    pe.wait_ge(s("pT"), b * H + (h - 1))
                for k in range(2):
                    last = mm(pb[2 + h % 2][:, k * L:(k + 1) * L], kA[m][0:KEXP, h, k * P:(k + 1) * P], qA[m][0:KEXP, h, :],
                              start=True, stop=True)
                last.then_inc(s("sT"), 1)

            def values(b, m, h):
                pe.wait_ge(s("pT"), b * H + (h + 1))
                for q in range(2):
                    for k in range(2):
                        col = (q * H + h) * (HD + 1)
                        last = mm(pb[4 + m][:, col:col + HD + 1], pexp[h % 4][:, k * L + q * P:k * L + (q + 1) * P],
                                  vaug[:, ds(b * 2 + k, 1), h, :].rearrange("p a d -> p (a d)"), start=(k == 0), stop=(k == 1))
                last.then_inc(s("pv"), 1)

            def out_T(b, first):
                pe.wait_ge(s("osb"), b + 1)
                if not first:
                    pe.wait_ge(s("x_b"), b)
                for q in range(2):
                    last = nc.tensor.transpose(pb[6][:, q * P:(q + 1) * P], osb[:, q * D:(q + 1) * D], ident[:, :])
                last.then_inc(s("oTp"), 1)

            def out_proj(b):
                pe.wait_ge(s("oT"), b + 1)
                for q in range(2):
                    last = mm(pb[6][:, L + q * D:L + (q + 1) * D], oT[:, q * P:(q + 1) * P], aw[:, 3, :], start=True, stop=True)
                last.then_inc(s("aop"), 1)

            def attn(b, m, first, last_b, loads):
                pe.wait_ge(s("max_in"), b * 32 + 32)
                for h in range(H):
                    exp_scores(b, m, h, first)
                    if h:
                        values(b, m, h - 1)
                    if h == 3 and not first:
                        out_T(b - 1, False)
                    if h == 6 and not first:
                        out_proj(b - 1)
                    if h == 4 and not last_b:
                        pe.wait_ge(s(f"qk_in{1 - m}"), loads * 32)
                    if h >= 4 and not last_b:
                        max_scores(b + 1, 1 - m, h - 4, False)
                values(b, m, H - 1)
                if not last_b:
                    for h in range(H - 4, H):
                        max_scores(b + 1, 1 - m, h, False)
                    max_T(b + 1)

            pe.wait_ge(s("qk_in0"), 32)
            for h in range(H):
                max_scores(0, 0, h, True)
            max_T(0)
            attn(0, 0, True, False, 1)
            with pe.Fori(0, (B - 2) // 2) as i:
                for m in (1, 0):
                    attn(i * 2 + (2 - m), m, False, False, i + 2)
            attn(B - 1, 1, False, True, 0)
            out_T(B - 1, False)
            out_proj(B - 1)

            router(1)
            experts(1)


def _kernel_arrays(i):
    g = {k: np.asarray(v) for k, v in i.items()}
    c = np.ascontiguousarray
    halves = lambda w: c(w.reshape(2, P, -1).transpose(1, 0, 2))
    xp = g["L0_attn_x_proj_w"]
    bcw = xp[:, DTR:]
    f32 = np.float32
    pos = np.arange(L, dtype=f32)
    slopes = np.power(f32(2.0), np.linspace(-4.0, -0.3, H, dtype=f32)).astype(f32)
    bias = -(slopes[:, None] * pos[None, :])
    bf = mybir.dt.np(mybir.dt.bfloat16)
    rows, rest = [], bias
    for _ in range(3):
        part = rest.astype(bf)
        rows.append(part)
        rest = rest - part.astype(f32)

    def blob(w1, w2, b1, b2, gamma, beta):
        cols = [w1, w2.reshape(E, FC, P, D).transpose(0, 2, 1, 3).reshape(E, P, FC * D),
                np.broadcast_to(b2[:, None, :], (E, P, D)), b1.reshape(E, FC, P).transpose(0, 2, 1),
                gamma[:, :, None], beta[:, :, None]]
        return c(np.concatenate(cols, axis=2))

    none = np.zeros((E, D), f32)
    return {
        "x": c(g["L0_attn_x"].reshape(T, D)),
        "cT": c(np.concatenate([g["L0_c"].T, g["L1_c"].T], axis=1)),
        "wmod": c(np.stack([g["L0_wmod"], g["L1_wmod"]], axis=1)),
        "in_w": c(g["L0_attn_in_proj_w"]),
        "conv_w": c(np.broadcast_to(g["L0_attn_conv_w"].reshape(DI, TAPS).T[None], (P, TAPS, DI))),
        "conv_b": c(g["L0_attn_conv_b"].reshape(2, P).T),
        "A_log": c(halves(g["L0_attn_A_log"]).reshape(P, 2 * NS)),
        "xp_w": halves(xp),
        "xbc_w": halves(np.concatenate([bcw, np.zeros((DI, 32), f32), bcw, bcw], axis=1)),
        "dt_w": c(g["L0_attn_dt_proj_w"]),
        "dt_b": c(g["L0_attn_dt_proj_b"].reshape(2, P).T),
        "adj": halves(g["L0_attn_adj"]),
        "d_skip": c(g["L0_attn_D"].reshape(2, P).T),
        "out_w": halves(g["L0_attn_out_proj_w"]),
        "router_w": c(np.stack([g["L0_ffn_centroids"].T, g["L1_ffn_Wr"]], axis=1)),
        "br": c(np.broadcast_to(g["L1_ffn_br"], (P, E))),
        "attn_w": c(np.stack([g[f"L1_attn_W{n}"].T for n in "qkvo"], axis=1)),
        "attn_b": c(np.stack([g["L1_attn_bq"], g["L1_attn_bk"]], axis=1)),
        "attn_row": c(np.broadcast_to(np.stack([g["L1_attn_bv"], g["L1_attn_bo"]])[None], (P, 2, D))),
        "bias_rows": c(np.stack(rows)),
        "one_rows": np.ones((5, H, L), bf),
        "blob0": blob(g["L0_ffn_W1"].transpose(0, 2, 1), g["L0_ffn_W2"].transpose(0, 2, 1), g["L0_ffn_b1"], g["L0_ffn_b2"],
                      g["L0_ffn_gamma"], g["L0_ffn_beta"]),
        "blob1": blob(g["L1_ffn_W1"], g["L1_ffn_W2"], g["L1_ffn_b1"], g["L1_ffn_b2"], none, none),
    }


def kernel(**inputs):
    import concourse.bacc as _bacc
    from concourse.bass_utils import run_bass_kernel_spmd as _run

    nc = _bacc.Bacc("TRN2", target_bir_lowering=False, num_devices=1)
    arrays = _kernel_arrays(inputs)
    aps = {name: nc.dram_tensor(f"in_{name}", v.shape, mybir.dt.from_np(v.dtype), kind="ExternalInput").ap()
           for name, v in arrays.items()}
    out = nc.dram_tensor("out", (T, D), mybir.dt.float32, kind="ExternalOutput").ap()
    build(nc, aps, out)
    r = _run(nc, [{f"in_{name}": v for name, v in arrays.items()}], core_ids=[0])
    return r.results[0]["out"].reshape(B, L, D)
```

```python
import numpy as np
import concourse.bass as bass
from concourse import mybir
from contextlib import ExitStack

B, L, D = 8, 256, 128
T = B * L
P = 128
NT = T // P
CH = 512
NC = T // CH
DI, NS, DTR, TAPS = 256, 16, 64, 4
PAD = TAPS - 1
E, F = 8, 512
FC = F // P
H, HD = 16, 8
ET = 2 * P
MT = T // ET + E - 1
NB = 5
EPS = 1e-5
CREDIT = 8
QSCALE = float(np.float32(1.0) / np.sqrt(np.float32(HD)))
QPART = (0, 0, 1, 0, 2, 1)
KPART = (0, 1, 0, 2, 0, 1)
KR = len(QPART) * HD
KMAX = KR + 3
KEXP = KMAX + 2
BLOB = 2 * F + 1 + FC + 2
O_W2, O_B2, O_B1, O_GB = F, 2 * F, 2 * F + 1, 2 * F + 1 + FC


class Steps:

    def __init__(self):
        self.base, self.n = 0, 0

    def next(self):
        self.n += 1
        return self.base + self.n

    def loop(self, i, steps):
        self.start, self.steps = self.base + self.n, steps
        self.base, self.n = i * steps + self.start, 0

    def end(self, count):
        assert self.n == self.steps, (self.n, self.steps)
        self.base, self.n = self.start + count * self.steps, 0


def build(nc, a, out):
    fp32, bf16, i32 = mybir.dt.float32, mybir.dt.bfloat16, mybir.dt.int32
    ALU, ACT, AX = mybir.AluOpType, mybir.ActivationFunctionType, mybir.AxisListType
    ds, ts = bass.ds, bass.ts
    ctx = ExitStack()
    with ctx:
        def sb(name, shape, dt=fp32):
            return ctx.enter_context(nc.sbuf_tensor(name, shape, dt))

        def dram(name, shape, dt=fp32):
            return nc.dram_tensor(name, shape, dt, kind="Internal").ap()

        sems = {}

        def s(name):
            if name not in sems:
                sems[name] = ctx.enter_context(nc.semaphore(name))
            return sems[name]

        x = sb("x", [P, T])
        xn = sb("xn", [P, T])
        hT = sb("hT", [P, B, PAD + L])
        ident = sb("ident", [P, P])
        tri = sb("tri", [P, P], bf16)
        ones_b = sb("ones_b", [P, P], bf16)
        ones_f = sb("ones_f", [P, P])
        epst = sb("epst", [P, 1])
        stats = sb("stats", [P, NT * 6])
        meanvar = sb("meanvar", [P, NT * 2])
        std = sb("std", [P, NT])
        rstd = sb("rstd", [P, NT])
        cT = sb("cT", [P, 2 * B])
        silc = sb("silc", [P, 2 * B])
        wmod = sb("wmod", [P, 2, 6 * D])
        modT = sb("modT", [P, 2, 2, B])
        modrow = [sb(f"modrow{k}", [P, B, 4, D]) for k in (0, 1)]
        inw = sb("inw", [P, 2 * DI])
        convb = sb("convb", [P, 2])
        xpw = sb("xpw", [P, 2, DTR + 2 * NS])
        xbc = sb("xbc", [P, 2, P])
        dtw = sb("dtw", [DTR, DI])
        dtb = sb("dtb", [P, 2])
        adj = sb("adj", [P, 2, DI])
        alog = sb("alog", [P, 2 * NS])
        aneg = sb("aneg", [P, 2 * NS])
        dskip = sb("dskip", [P, 2])
        outw = sb("outw", [P, 2, D])
        bc = sb("bc", [P, T], bf16)
        pick = sb("pick", [P, 2 * NS, P], bf16)
        dA = [sb(f"dA{k}", [P, 2, L]) for k in range(4)]
        tmp = sb("tmp", [P, CH])
        big = sb("big", [P, 8 * T])
        scr = sb("scr", [P, 19, CH])
        cent = sb("cent", [P, 2, E])
        br = sb("br", [P, E])
        iot = sb("iot", [P, MT], i32)
        kth = sb("kth", [P, MT])
        down = sb("down", [P, E])
        lgt = sb("lgt", [P, NT, E])
        oh = sb("oh", [P, NT, E])
        ohb = sb("ohb", [P, NT * E], bf16)
        rt = sb("rt", [P, NT, E])
        smax = sb("smax", [P, NT])
        m16 = sb("m16", [P, NT])
        et = sb("et", [P, E, NT])
        incl = sb("incl", [P, E, NT])
        seg = sb("seg", [P, E, NT])
        ntile = sb("ntile", [P, E])
        tend = sb("tend", [P, E])
        tbeg = sb("tbeg", [P, E])
        kcmp = sb("kcmp", [P, MT, E])
        exf = sb("exf", [P, MT])
        exi = sb("exi", [P, MT], i32)
        posf = sb("posf", [P, NT])
        posi = sb("posi", [P, NT], i32)
        wgt = sb("wgt", [P, NT])
        aw = sb("aw", [P, 4, P])
        ab = sb("ab", [P, 2])
        arow = sb("arow", [P, 2, D])

        pb = [ctx.enter_context(nc.psum_tensor(f"pb{k}", [P, CH], fp32)) for k in range(8)]

        xs_d = [dram(f"xs{k}", (MT * ET, D)) for k in (0, 1)]
        ys_d = [dram(f"ys{k}", (MT * ET, D)) for k in (0, 1)]
        qk_d = dram("qk_parts", (2, KR // HD, HD, H, T), bf16)

        xi = big[:, 0:2 * T].rearrange("p (h t) -> p h t", h=2)
        gres = big[:, 2 * T:4 * T].rearrange("p (h t) -> p h t", h=2)
        dlt = big[:, 4 * T:6 * T].rearrange("p (h t) -> p h t", h=2)
        u = big[:, 6 * T:8 * T].rearrange("p (h t) -> p h t", h=2)
        srep = scr[:, 0:4, :].rearrange("p a (c m) -> p (a c) m", m=P)
        convw = scr[:, 11:13, :].rearrange("p a (t c) -> p (a t) c", c=DI)
        wtap = scr[:, 13:15, :].rearrange("p a (t c) -> p (a t) c", c=DI)
        drs = scr[0:DTR, 0, :]
        sp_e = [scr[:, 1 + h, :] for h in (0, 1)]
        sp_l = [scr[:, 3 + h, :] for h in (0, 1)]
        sp_t = [scr[:, 5 + h, :] for h in (0, 1)]
        delta = [scr[:, 7 + h, :] for h in (0, 1)]
        bcr = scr[:, 9, :]
        dBu = [scr[:, k, :] for k in range(4)]
        hs = [scr[:, k, :] for k in range(4, 8)]
        hc = [scr[:, k, :] for k in range(8, 12)]
        bsb = [scr[:, k, :] for k in range(12, 15)]
        yg = [scr[:, k, :] for k in (15, 16)]
        yt = [scr[:, k, :] for k in (17, 18)]
        sign = scr[:, 17:19, :].rearrange("p a (b d) -> p (a b) d", d=D)
        blob = [big[:, k * BLOB:(k + 1) * BLOB] for k in range(NB)]
        e0 = NB * BLOB
        xt = [big[:, e0 + k * ET:e0 + (k + 1) * ET] for k in range(NB)]
        ysb = [big[:, e0 + (NB + k) * ET:e0 + (NB + k + 1) * ET] for k in range(NB)]
        assert e0 + 2 * NB * ET <= 5 * T
        h1 = [scr[:, 2 * k:2 * k + 2, :].rearrange("p a (f t) -> p (a f) t", f=2) for k in range(NB)]
        xtT = [scr[:, 2 * NB + k, 0:ET] for k in range(NB)]
        ytT = [scr[:, 2 * NB + k, ET:2 * ET] for k in range(NB)]
        assert 3 * NB <= 19
        h2 = big[:, 5 * T:6 * T]
        h2T = big[:, 6 * T:7 * T]
        yall = big[:, 7 * T:8 * T]
        qA = [big[:, k * T:(k + 1) * T].bitcast(bf16).rearrange("p (h l) -> p h l", h=H) for k in (0, 1)]
        kA = [big[:, k * T:(k + 1) * T].bitcast(bf16).rearrange("p (h l) -> p h l", h=H) for k in (2, 3)]
        parts = [[big[:, (8 + 3 * qk + p_) * T // 2:(9 + 3 * qk + p_) * T // 2].bitcast(bf16)
                  for p_ in range(3)] for qk in (0, 1)]
        vz = [big[:, (4 + 2 * k) * T:(6 + 2 * k) * T].rearrange("p (k g j c) -> p (k g) j c", k=2, g=2, j=HD) for k in (0, 1)]
        qf = [scr[:, k, :] for k in (0, 1)]
        qr = [scr[:, k, :] for k in (2, 3)]
        pexp = [scr[:, k, :] for k in range(4, 8)]
        oT = scr[:, 8, 0:L]
        rden = [scr[0:P // 2, 12 + g, 0:L] for g in (0, 1)]
        mx = scr[:, 9, 0:2 * H]
        mneg = scr[:, 9, 2 * H:4 * H]
        mpart = scr[0:2 * H, 10, 0:P].bitcast(bf16)
        vsb = scr[:, 14:18, :].rearrange("p a (t d) -> p (a t) d", d=D)
        osum = scr[:, 11, 0:2 * D]

        MOD_LOADS = [(cT[:, :], a["cT"]), (wmod[:, :, :], a["wmod"])]
        IN_LOADS = [(inw[:, :], a["in_w"]), (convw[:, :, :], a["conv_w"]), (convb[:, :], a["conv_b"])]
        W_LOADS = [
            (xpw[:, :, :], a["xp_w"]), (xbc[:, :, :], a["xbc_w"]),
            (dtw[:, :], a["dt_w"]), (dtb[:, :], a["dt_b"]), (adj[:, :, :], a["adj"]), (alog[:, :], a["A_log"]),
            (dskip[:, :], a["d_skip"]), (outw[:, :, :], a["out_w"]), (cent[:, :, :], a["router_w"]),
            (br[:, :], a["br"]), (aw[:, :, :], a["attn_w"]), (ab[:, :], a["attn_b"]), (arow[:, :, :], a["attn_row"]),
        ]
        ALL_W = 16 * len(W_LOADS)
        CONSTS, LATE_CONSTS = 4, 9

        CREDITED = {
            "Activation": "ln2_hT xi drs dlt bsb pT qf ln0_hT oT f0_h2T f1_h2T f0_h1 f1_h1",
            "DVE": "delta bc u scan hc yg x_a parts mx nrm x_b x_f0 x_final f0_ys f1_ys f0_ytT f1_ytT",
            "PE": "dtp adjp hsum outp pv sT aop f0_yp f1_yp",
            "Pool": "dBu vz",
        }

        def give_credit(eng, names):
            for name in names.split():
                eng.sem_inc(s(name), CREDIT)

        def apart(eng):
            eng.sem_inc(s("apart"), 1)

        block = ctx.enter_context(nc.Block())

        @block.sync
        def _(sp):
            for dst, src in MOD_LOADS:
                sp.dma_start(dst, src).then_inc(s("mod_in"), 16)
            for q in range(NC):
                sp.dma_start(x[:, q * CH:(q + 1) * CH].rearrange("p (t d) -> p t d", d=D),
                             a["x"][q * CH:(q + 1) * CH, :].rearrange("(t p) d -> p t d", p=P)).then_inc(s("x_in"), 16)
            for dst, src in IN_LOADS:
                sp.dma_start(dst, src).then_inc(s("inproj_in"), 16)
            for dst, src in W_LOADS:
                sp.dma_start(dst, src).then_inc(s("w_in"), 16)
            sp.wait_ge(s("zeroed"), 1)
            for k in range(2):
                for m in range(2):
                    sp.dma_start(xs_d[k][m * MT * P:(m + 1) * MT * P, :].rearrange("(t p) d -> p t d", p=P),
                                 big[:, 6 * T:6 * T + MT * P].rearrange("p (t d) -> p t d", d=D)
                                 ).then_inc(s("zeros_out"), 16)

            def experts(k):
                sp.wait_ge(s(f"f{k}_tiles"), 1)
                sp.wait_ge(s(f"f{k}_xs_out"), 16 * NT)

                def load(t, m, first):
                    if not first:
                        sp.wait_ge(s(f"f{k}_ytT"), t - NB + 1 + CREDIT)
                    e = sp.value_load(exi[0:1, ds(t, 1)], min_val=0, max_val=E - 1)
                    sp.dma_start(blob[m], a[f"blob{k}"][ds(e, 1), :, :].rearrange("a p c -> (a p) c")
                                 ).then_inc(s(f"f{k}_in{m}"), 16)
                    sp.dma_start(xt[m].rearrange("p (q d) -> p q d", d=D),
                                 xs_d[k][ds(t * ET, ET), :].rearrange("(q p) d -> p q d", p=P)).then_inc(s(f"f{k}_in{m}"), 16)

                for m in range(NB):
                    load(m, m, True)
                with sp.Fori(1, MT // NB) as i:
                    for m in range(NB):
                        load(i * NB + m, m, False)

            experts(0)

            for qk in range(2):
                sp.wait_ge(s("parts"), NC * (qk + 1) + CREDIT)
                for c, part in enumerate((QPART, KPART)[qk]):
                    sp.dma_start(qk_d[qk, c, :, :, :].rearrange("d h t -> h d t"),
                                 parts[qk][part]).then_inc(s("parts_out"), 16)
            sp.wait_ge(s("parts_out"), 16 * 2 * len(QPART))
            for m in range(2):
                sp.dma_start(qA[m][KR:KMAX, :, :], a["one_rows"][0:3, :, :]).then_inc(s("rows_in"), 16)
                sp.dma_start(kA[m][KR:KMAX, :, :], a["bias_rows"]).then_inc(s("rows_in"), 16)
                sp.dma_start(kA[m][KMAX:KEXP, :, :], a["one_rows"][3:5, :, :]).then_inc(s("rows_in"), 16)

            def load_qk(b, m):
                for dst, qk in ((qA[m], 0), (kA[m], 1)):
                    sp.dma_start(dst[0:KR, :, :],
                                 qk_d[qk, :, :, :, ds(b * L, L)].rearrange("c d h l -> (c d) h l")
                                 ).then_inc(s(f"qk_in{m}"), 16)

            def load_max(b, m):
                sp.wait_ge(s("mparts"), b + 1)
                for r in range(2):
                    sp.dma_start(qA[m][KMAX + r:KMAX + r + 1, :, :].rearrange("p h l -> p (h l)"),
                                 mpart[:, r * P:(r + 1) * P]).then_inc(s("max_in"), 16)

            load_qk(0, 0)
            load_max(0, 0)
            load_qk(1, 1)
            load_max(1, 1)
            with sp.Fori(0, (B - 2) // 2) as i:
                for m in range(2):
                    b = i * 2 + (2 + m)
                    sp.wait_ge(s("sT"), (b - 1) * H + CREDIT)
                    load_qk(b, m)
                    load_max(b, m)

            experts(1)

            for q in range(NC):
                sp.wait_ge(s("x_final"), 2 * (q + 1) + CREDIT)
                sp.dma_start(out[q * CH:(q + 1) * CH, :].rearrange("(t p) d -> p t d", p=P),
                             x[:, q * CH:(q + 1) * CH].rearrange("p (t d) -> p t d", d=D)).then_inc(s("out_done"), 16)
            sp.wait_ge(s("out_done"), 16 * NC)

        @block.gpsimd
        def _(pool):
            give_credit(pool, CREDITED["Pool"])
            own = Steps()
            nc.gpsimd.memset(ident[:, :], 0.0).then_inc(s("pool_step"), 1)
            pool.wait_ge(s("pool_step"), own.next())
            nc.gpsimd.affine_select(out=ident[:, :], in_=ident[:, :], compare_op=ALU.not_equal, fill=1.0,
                                    base=0, pattern=[[-1, P]], channel_multiplier=1).then_inc(s("consts"), 1)
            nc.gpsimd.memset(ones_f[:, :], 1.0).then_inc(s("consts"), 1)
            nc.gpsimd.memset(epst[:, :], EPS).then_inc(s("consts"), 1)
            nc.gpsimd.memset(hT[:, :, 0:PAD], 0.0).then_inc(s("consts"), 1)
            nc.gpsimd.memset(big[:, 6 * T:6 * T + MT * P], 0.0).then_inc(s("zeroed"), 1)
            for k in range(4):
                nc.gpsimd.memset(dA[k][:, :, 0:1], 0.0).then_inc(s("late_consts"), 1)
            nc.gpsimd.memset(pick[:, :, :], 0.0).then_inc(s("pool_step"), 1)
            pool.wait_ge(s("pool_step"), own.next())
            for off in (0, 64):
                nc.gpsimd.affine_select(
         out=pick[:, :, :], in_=pick[:, :, :], compare_op=ALU.not_equal, fill=1.0,
         base=-off, pattern=[[-1, 2 * NS], [0, P]], channel_multiplier=1).then_inc(s("pool_step"), 1)
                pool.wait_ge(s("pool_step"), own.next())
            nc.gpsimd.affine_select(
                out=pick[:, :, :], in_=pick[:, :, :], compare_op=ALU.not_equal, fill=1.0,
                base=-96, pattern=[[-1, 2 * NS], [0, P]], channel_multiplier=1).then_inc(s("late_consts"), 1)
            nc.gpsimd.memset(ones_b[:, :], 1.0).then_inc(s("pool_step"), 1)
            pool.wait_ge(s("pool_step"), own.next())
            nc.gpsimd.affine_select(out=tri[:, :], in_=ones_b[:, :], compare_op=ALU.is_gt, fill=0.0,
                                    base=0, pattern=[[1, P]], channel_multiplier=-1).then_inc(s("late_consts"), 1)
            nc.gpsimd.iota(iot[:, :], pattern=[[1, MT]], base=0, channel_multiplier=0).then_inc(s("pool_step"), 1)
            pool.wait_ge(s("pool_step"), own.next())
            nc.gpsimd.tensor_copy(kth[:, :], iot[:, :]).then_inc(s("pool_step"), 1)
            pool.wait_ge(s("pool_step"), own.next())
            nc.gpsimd.tensor_scalar(down[:, :], kth[:, 0:E], -1.0, float(E), ALU.mult, ALU.add).then_inc(s("late_consts"), 1)
            nc.gpsimd.memset(seg[:, :, :], 1.0).then_inc(s("pool_step"), 1)
            pool.wait_ge(s("pool_step"), own.next())
            nc.gpsimd.memset(seg[:, :, 0:1], 0.0).then_inc(s("late_consts"), 1)
            nc.gpsimd.memset(bc[:, :], 0.0).then_inc(s("late_consts"), 1)

            for k in range(2):
                pool.wait_ge(s(f"m{k}_cp"), B)
                nc.gpsimd.tensor_scalar(modrow[k][:, :, 2, :], modrow[k][:, :, 2, :], 1.0, 1.0, ALU.mult, ALU.add).then_inc(s("pool_step"), 1)
                pool.wait_ge(s("pool_step"), own.next())
                for j in (0, 3):
                    g = modrow[k][:, :, j, :]
                    nc.gpsimd.tensor_scalar(sign, g, 0.0, None, ALU.is_ge).then_inc(s("pool_step"), 1)
                    pool.wait_ge(s("pool_step"), own.next())
                    nc.gpsimd.tensor_scalar(sign, sign, 2.0, -1.0, ALU.mult, ALU.add).then_inc(s("pool_step"), 1)
                    pool.wait_ge(s("pool_step"), own.next())
                    nc.gpsimd.tensor_tensor(g, g, sign, ALU.mult).then_inc(s("pool_step"), 1)
                    pool.wait_ge(s("pool_step"), own.next())
                    nc.gpsimd.tensor_scalar(g, g, 0.25, None, ALU.max).then_inc(s("pool_step"), 1)
                    pool.wait_ge(s("pool_step"), own.next())
                    nc.gpsimd.tensor_tensor(g, g, sign, ALU.mult).then_inc(s("pool_step"), 1)
                    pool.wait_ge(s("pool_step"), own.next())
                pool.sem_inc(s("gates"), 1)

            pool.wait_ge(s("u"), 2 * NC + CREDIT)
            with pool.Fori(0, NC) as c:
                for n in range(NS):
                    pool.wait_ge(s("bsb"), c * NS + (n + 1 + CREDIT))
                    for h in range(2):
                        step = 2 * n + h
                        pool.wait_ge(s("scan"), c * 2 * NS + (step - 3 + CREDIT))
                        apart(pool)
                        nc.gpsimd.tensor_tensor(dBu[step % 4], u[:, h, ts(c, CH)], bsb[n % 3], ALU.mult
                                                ).then_inc(s("dBu"), 1)

            def experts(k, rows):
                pool.wait_ge(s("zeros_out"), 64)
                pool.wait_ge(s(f"f{k}_pos"), 1)
                for t in range(NT):
                    nc.gpsimd.indirect_dma_start(
                        out=xs_d[k], out_offset=bass.IndirectOffsetOnAxis(ap=posi[:, t:t + 1], axis=0),
                        in_=rows[:, t * P:(t + 1) * P], in_offset=None).then_inc(s(f"f{k}_xs_out"), 16)
                with pool.Fori(0, MT // NB) as i:
                    for m in range(NB):
                        t = i * NB + m
                        pool.wait_ge(s(f"f{k}_ys"), t + 1 + CREDIT)
                        pool.dma_start(ys_d[k][ds(t * ET, ET), :].rearrange("(q p) d -> p q d", p=P),
                                       ysb[m].rearrange("p (q d) -> p q d", d=D)).then_inc(s(f"f{k}_ys_out{m}"), 16)
                for m in range(NB):
                    pool.wait_ge(s(f"f{k}_ys_out{m}"), 16 * MT // NB)
                for t in range(NT):
                    nc.gpsimd.indirect_dma_start(
                        out=yall[:, t * P:(t + 1) * P], out_offset=None, in_=ys_d[k],
                        in_offset=bass.IndirectOffsetOnAxis(ap=posi[:, t:t + 1], axis=0)).then_inc(s(f"f{k}_y_in"), 16)

            experts(0, xn)

            pool.wait_ge(s("parts_out"), 16 * 2 * len(QPART))
            for m in range(2):
                nc.gpsimd.memset(vz[m].rearrange("p k j c -> p (k j c)"), 0.0).then_inc(s("pool_step"), 1)
                pool.wait_ge(s("pool_step"), own.next())
                for j in range(HD):
                    nc.gpsimd.memset(vz[m][:, :, j, P // 2 + j * HD:P // 2 + (j + 1) * HD], 1.0)

            def spread_v(b, m):
                for j in range(HD):
                    last = nc.gpsimd.tensor_copy(
                        vz[m][:, :, j, j * HD:(j + 1) * HD],
                        vsb[:, ds(b * 2, 2), :].rearrange("p k (g j d) -> p (k g) j d", g=2, j=HD)[:, :, j, :])
                last.then_inc(s("vz"), 1)

            pool.wait_ge(s("v"), NC)
            spread_v(0, 0)
            spread_v(1, 1)
            with pool.Fori(0, (B - 2) // 2) as i:
                for m in range(2):
                    b = i * 2 + (2 + m)
                    pool.wait_ge(s("pv"), (b - 1) * H + CREDIT)
                    apart(pool)
                    spread_v(b, m)

            experts(1, h2)

        @block.scalar
        def _(act):
            give_credit(act, CREDITED["Activation"])
            own = Steps()
            act.wait_ge(s("mod_in"), 16 * len(MOD_LOADS))

            def ln_std(key):
                act.wait_ge(s(f"{key}_mv"), NT)
                nc.scalar.activation(std[:, :], meanvar[:, 1::2], ACT.Sqrt, bias=epst[:, 0:1]).then_inc(s(f"{key}_std"), 1)

            def modulate(key, k):
                with act.Fori(0, B // 2) as i:
                    for m in range(2):
                        b = i * 2 + m
                        act.wait_ge(s(f"{key}_xT"), b + 1)
                        apart(act)
                        nc.scalar.activation(hT[:, ds(b, 1), PAD:PAD + L].rearrange("p a l -> p (a l)"), pb[m][:, 0:L],
                                             ACT.Identity, scale=modT[:, k, 1, ds(b, 1)],
                                             bias=modT[:, k, 0, ds(b, 1)]).then_inc(s(f"{key}_hT"), 1)

            def mod_rows(k):
                for b in range(B):
                    act.wait_ge(s(f"m{k}_ps"), b + 1)
                    nc.scalar.activation(modrow[k][:, b, :, :].rearrange("p k d -> p (k d)"), pb[6 + b % 2][:, :],
                                         ACT.Copy).then_inc(s(f"m{k}_cp"), 1)

            nc.scalar.activation(silc[:, :], cT[:, :], ACT.Silu).then_inc(s("silc"), 1)
            act.wait_ge(s("consts"), CONSTS)
            ln_std("ln0")
            act.wait_ge(s("modT"), 2)
            modulate("ln0", 0)
            for k in range(2):
                mod_rows(k)

            act.wait_ge(s("inproj_in"), 16 * len(IN_LOADS))
            nc.scalar.preload_act_table(ACT.Silu)
            with act.Fori(0, NC) as c:
                for h in range(2):
                    act.wait_ge(s("inproj"), c * 4 + (h + 1))
                    apart(act)
                    nc.scalar.activation(xi[:, h, ts(c, CH)], pb[2 + h][:, :], ACT.Silu, bias=convb[:, h:h + 1]
                                         ).then_inc(s("xi"), 1)
                for h in range(2):
                    act.wait_ge(s("inproj"), c * 4 + (h + 3))
                    apart(act)
                    nc.scalar.activation(gres[:, h, ts(c, CH)], pb[4 + h][:, :], ACT.Silu).then_inc(s("xi"), 1)

            act.wait_ge(s("w_in"), ALL_W)
            act.wait_ge(s("late_consts"), LATE_CONSTS)
            nc.scalar.preload_act_table(ACT.Ln)
            nc.scalar.activation(aneg[:, :], alog[:, :], ACT.Exp).then_inc(s("act_step"), 1)
            act.wait_ge(s("act_step"), own.next())
            nc.scalar.mul(aneg[:, :], aneg[:, :], -1.0).then_inc(s("aneg"), 1)
            with act.Fori(0, NC) as c:
                own.loop(c, 6)
                act.wait_ge(s("draw"), c + 1)
                act.wait_ge(s("dtp"), c * 2 + CREDIT)
                nc.scalar.activation(drs, pb[6][0:DTR, :], ACT.Copy).then_inc(s("drs"), 1)
                act.wait_ge(s("delta"), c + CREDIT)
                for h in range(2):
                    act.wait_ge(s("dtp"), c * 2 + (h + 1 + CREDIT))
                    nc.scalar.activation(sp_t[h], pb[h][:, :], ACT.Identity, bias=dtb[:, h:h + 1]).then_inc(s("act_step"), 1)
                    act.wait_ge(s("act_step"), own.next())
                    nc.scalar.activation(sp_e[h], sp_t[h], ACT.Abs).then_inc(s("act_step"), 1)
                    act.wait_ge(s("act_step"), own.next())
                    nc.scalar.activation(sp_e[h], sp_e[h], ACT.Exp, scale=-1.0).then_inc(s("act_step"), 1)
                    act.wait_ge(s("act_step"), own.next())
                    nc.scalar.activation(sp_l[h], sp_e[h], ACT.Ln, bias=1.0).then_inc(s("spl"), 1)
                for h in range(2):
                    act.wait_ge(s("adjp"), c * 2 + (h + 1 + CREDIT))
                    apart(act)
                    nc.scalar.activation(dlt[:, h, ts(c, CH)], pb[2 + h][:, :], ACT.Copy).then_inc(s("dlt"), 1)
            own.end(NC)

            act.wait_ge(s("dlt"), 2 * NC + CREDIT)
            with act.Fori(0, NC) as c:
                for n in range(NS):
                    act.wait_ge(s("bbp"), c * NS + (n + 1))
                    act.wait_ge(s("dBu"), c * 2 * NS + (2 * n - 4 + CREDIT))
                    nc.scalar.activation(bsb[n % 3], pb[n % 2][:, :], ACT.Copy).then_inc(s("bsb"), 1)
                    for h in range(2):
                        step = 2 * n + h
                        act.wait_ge(s("scan"), c * 2 * NS + (step - 3 + CREDIT))
                        apart(act)
                        nc.scalar.activation(
                            dA[step % 4][:, :, 1:L], dlt[:, h, ts(c, CH)].rearrange("p (b l) -> p b l", b=2)[:, :, 1:L],
                            ACT.Exp, scale=aneg[:, h * NS + n:h * NS + n + 1]).then_inc(s("dA"), 1)

            def router(k, h2_key):
                with act.Fori(0, B // 2) as i:
                    for m in range(2):
                        b = i * 2 + m
                        act.wait_ge(s(f"f{k}_h2Tp"), b + 1)
                        apart(act)
                        nc.scalar.activation(h2T[:, ts(b, L)], pb[m][:, 0:L], ACT.Copy).then_inc(s(f"f{k}_h2T"), 1)

            def experts(k, func):
                nc.scalar.preload_act_table(func)
                def tile(i, m, first):
                    t = i * NB + m
                    if not first:
                        act.wait_ge(s(f"f{k}_yp"), t - NB + 1 + CREDIT)
                    act.wait_ge(s(f"f{k}_in{m}"), i * 32 + 32)
                    for f in range(FC):
                        act.wait_ge(s(f"f{k}_hid"), t * 2 + f // 2 + 1)
                        nc.scalar.activation(h1[m][:, f, :], pb[1 + f // 2][:, (f % 2) * ET:(f % 2 + 1) * ET], func,
                                             bias=blob[m][:, O_B1 + f:O_B1 + f + 1]).then_inc(s(f"f{k}_h1"), 1)
                for m in range(NB):
                    tile(0, m, True)
                with act.Fori(1, MT // NB) as i:
                    for m in range(NB):
                        tile(i, m, False)

            ln_std("ln1")
            ln_std("lnf")
            router(0, None)
            act.wait_ge(s("f0_nmax"), 1)
            nc.scalar.activation(m16[:, :], smax[:, :], ACT.Exp, scale=-1.0).then_inc(s("f0_e"), 1)
            experts(0, ACT.Relu)

            ln_std("ln2")
            modulate("ln2", 1)
            act.wait_ge(s("abs"), 1)
            for qk in range(2):
                with act.Fori(0, NC // 2) as i:
                    for m in range(2):
                        c = i * 2 + m
                        act.wait_ge(s("qkp"), c + (NC * qk + 1))
                        act.wait_ge(s("parts"), i * 2 + NC * qk + CREDIT)
                        nc.scalar.activation(qf[m], pb[2 + m][:, :], ACT.Identity, bias=ab[:, qk:qk + 1],
                                             scale=QSCALE if qk == 0 else 1.0).then_inc(s("qf"), 1)
            nc.scalar.preload_act_table(ACT.Exp)

            def attn(b, first):
                for h in range(H):
                    act.wait_ge(s("sT"), b * H + (h + 1 + CREDIT))
                    if not (first and h < 4):
                        act.wait_ge(s("pv"), b * H + (h - 3 + CREDIT))
                    nc.scalar.activation(pexp[h % 4], pb[2 + h % 2][:, :], ACT.Exp).then_inc(s("pT"), 1)

            attn(0, True)
            with act.Fori(0, (B - 2) // 2) as i:
                for m in range(2):
                    attn(i * 2 + (1 + m), False)
            attn(B - 1, False)

            ln_std("ln3")
            router(1, None)
            act.wait_ge(s("f1_nmax"), 1)
            nc.scalar.activation(rt[:, :, :], lgt[:, :, :], ACT.Exp).then_inc(s("f1_e"), 1)
            experts(1, ACT.Gelu)

        @block.vector
        def _(dve):
            give_credit(dve, CREDITED["DVE"])
            own = Steps()
            V = nc.vector

            def stats_of(key, src):
                for t in range(NT):
                    last = V.bn_stats(stats[:, 6 * t:6 * t + 6], src[:, t * P:(t + 1) * P])
                last.then_inc(s("dve_step"), 1)
                dve.wait_ge(s("dve_step"), own.next())
                for t in range(NT):
                    V.bn_aggr(meanvar[:, 2 * t:2 * t + 2], stats[:, 6 * t:6 * t + 6]).then_inc(s(f"{key}_mv"), 1)
                dve.wait_ge(s(f"{key}_std"), 1)
                V.reciprocal(rstd[:, :], std[:, :]).then_inc(s("dve_step"), 1)
                dve.wait_ge(s("dve_step"), own.next())

            def layernorm(key, src, dst):
                stats_of(key, src)
                for t in range(NT):
                    V.tensor_scalar(dst[:, t * P:(t + 1) * P], src[:, t * P:(t + 1) * P], meanvar[:, 2 * t:2 * t + 1],
                                    rstd[:, t:t + 1], ALU.subtract, ALU.mult).then_inc(s(f"{key}_xn"), 1)

            dve.wait_ge(s("consts"), CONSTS)
            dve.wait_ge(s("silc"), 1)
            for b in range(2 * B):
                V.tensor_scalar(srep[:, b, :], ones_f[:, :], silc[:, b:b + 1], None, ALU.mult).then_inc(s("srep"), 1)
            dve.wait_ge(s("modTp"), 1)
            for j in range(2):
                V.tensor_scalar(modT[:, :, j, :], pb[5][:, 0:4 * B].rearrange("p (k j b) -> p k j b", k=2, j=2)[:, :, j, :],
                                float(j), None, ALU.add).then_inc(s("modT"), 1)
            dve.wait_ge(s("x_in"), 16 * NC)
            layernorm("ln0", x, xn)
            dve.wait_ge(s("inproj_in"), 16 * len(IN_LOADS))
            for tap in range(TAPS):
                V.tensor_tensor(wtap[:, tap, :], inw[:, 0:DI], convw[:, tap, :], ALU.mult).then_inc(s("wtap"), 1)

            dve.wait_ge(s("w_in"), ALL_W)
            dve.wait_ge(s("late_consts"), LATE_CONSTS)
            dve.wait_ge(s("m1_ps"), B)
            dve.wait_ge(s("zeros_out"), 64)
            with dve.Fori(0, NC) as c:
                own.loop(c, 4)
                dve.wait_ge(s("bcp"), c + 1)
                t = ts(c, CH)
                apart(dve)
                V.tensor_copy(bc[0:32, t], pb[7][0:32, :])
                V.tensor_copy(bc[64:128, t], pb[7][64:128, :]).then_inc(s("dve_step"), 1)
                dve.wait_ge(s("dve_step"), own.next())
                V.tensor_tensor(bcr[64:128, :], pb[7][64:128, :], bc[64:128, t], ALU.subtract).then_inc(s("dve_step"), 1)
                dve.wait_ge(s("dve_step"), own.next())
                apart(dve)
                V.tensor_copy(bc[64:128, t], bcr[64:128, :]).then_inc(s("dve_step"), 1)
                dve.wait_ge(s("dve_step"), own.next())
                V.tensor_tensor(bcr[96:128, :], bcr[96:128, :], bc[96:128, t], ALU.subtract).then_inc(s("dve_step"), 1)
                dve.wait_ge(s("dve_step"), own.next())
                apart(dve)
                V.tensor_copy(bc[96:128, t], bcr[96:128, :]).then_inc(s("bc"), 1)
                dve.wait_ge(s("spl"), c * 2 + 2)
                dve.wait_ge(s("adjp"), c * 2 + CREDIT)
                for h in range(2):
                    last = V.scalar_tensor_tensor(delta[h], sp_t[h], 0.0, sp_l[h], ALU.max, ALU.add)
                last.then_inc(s("delta"), 1)
                for h in range(2):
                    dve.wait_ge(s("dlt"), c * 2 + (h + 1 + CREDIT))
                    V.tensor_tensor(u[:, h, ts(c, CH)], dlt[:, h, ts(c, CH)], xi[:, h, ts(c, CH)], ALU.mult).then_inc(s("u"), 1)
            own.end(NC)

            dve.wait_ge(s("gates"), 2)
            with dve.Fori(0, NC) as c:
                own.loop(c, 3)

                def scan(n, h):
                    step = 2 * n + h
                    dve.wait_ge(s("hc"), c * 2 * NS + (step - 3 + CREDIT))
                    dve.wait_ge(s("dA"), c * 2 * NS + (step + 1))
                    dve.wait_ge(s("dBu"), c * 2 * NS + (step + 1 + CREDIT))
                    V.tensor_tensor_scan(hs[step % 4], dA[step % 4][:, :, :].rearrange("p b l -> p (b l)"), dBu[step % 4],
                                         0.0, ALU.mult, ALU.add).then_inc(s("scan"), 1)

                def times_c(n, h):
                    step = 2 * n + h
                    dve.wait_ge(s("cbp"), c * NS + (n + 1))
                    dve.wait_ge(s("hsum"), c * 2 * NS + (step - 3 + CREDIT))
                    dve.wait_ge(s("scan"), c * 2 * NS + (step + 1 + CREDIT))
                    V.tensor_tensor(hc[step % 4], hs[step % 4], pb[2 + n % 2][:, :], ALU.mult).then_inc(s("hc"), 1)

                scan(0, 0)
                for n in range(NS):
                    scan(n, 1)
                    times_c(n, 0)
                    if n + 1 < NS:
                        scan(n + 1, 0)
                    times_c(n, 1)
                dve.wait_ge(s("outp"), c + CREDIT)
                for h in range(2):
                    dve.wait_ge(s("hsum"), c * 2 * NS + (2 * NS - 1 + h + CREDIT))
                    V.scalar_tensor_tensor(yt[h], xi[:, h, ts(c, CH)], dskip[:, h:h + 1], pb[4 + h][:, :],
                                           ALU.mult, ALU.add).then_inc(s("dve_step"), 1)
                    dve.wait_ge(s("dve_step"), own.next())
                    V.tensor_tensor(yg[h], yt[h], gres[:, h, ts(c, CH)], ALU.mult).then_inc(s("yg"), 1)
                dve.wait_ge(s("outp"), c + 1 + CREDIT)
                for t in range(CH // P):
                    last = V.tensor_tensor(tmp[:, t * P:(t + 1) * P], pb[6][:, t * P:(t + 1) * P],
                                           modrow[0][:, ds(c * 2 + t // 2, 1), 0, :].rearrange("p a d -> p (a d)"), ALU.mult)
                last.then_inc(s("dve_step"), 1)
                dve.wait_ge(s("dve_step"), own.next())
                V.tensor_tensor(x[:, ts(c, CH)], x[:, ts(c, CH)], tmp[:, :], ALU.add).then_inc(s("x_a"), 1)
            own.end(NC)

            def layernorm_rows(key, k):
                stats_of(key, x)
                cols = [slice(t * P, (t + 1) * P) for t in range(NT)]
                for t in range(NT):
                    last = V.scalar_tensor_tensor(xn[:, cols[t]], x[:, cols[t]], meanvar[:, 2 * t:2 * t + 1],
                                                  modrow[k][:, t // 2, 2, :], ALU.subtract, ALU.mult)
                last.then_inc(s("dve_step"), 1)
                dve.wait_ge(s("dve_step"), own.next())
                for t in range(NT):
                    last = V.scalar_tensor_tensor(h2[:, cols[t]], xn[:, cols[t]], rstd[:, t:t + 1],
                                                  modrow[k][:, t // 2, 1, :], ALU.mult, ALU.add)
                    if t % 2:
                        last.then_inc(s(f"f{k}_h2"), 1)

            def router(k):
                dve.wait_ge(s(f"f{k}_sc"), 1)
                sc = pb[7][:, 0:NT * E].rearrange("p (t e) -> p t e", e=E)
                if k:
                    V.tensor_tensor(lgt[:, :, :], sc, br[:, :].unsqueeze(1).to_broadcast([P, NT, E]), ALU.add).then_inc(s("dve_step"), 1)
                    dve.wait_ge(s("dve_step"), own.next())
                else:
                    V.tensor_copy(lgt[:, :, :], sc).then_inc(s("dve_step"), 1)
                    dve.wait_ge(s("dve_step"), own.next())
                V.tensor_reduce(smax[:, :], lgt[:, :, :], AX.X, ALU.max).then_inc(s("dve_step"), 1)
                dve.wait_ge(s("dve_step"), own.next())
                mbc = smax[:, :].unsqueeze(2).to_broadcast([P, NT, E])
                V.tensor_tensor(oh[:, :, :], lgt[:, :, :], mbc, ALU.is_ge).then_inc(s("dve_step"), 1)
                dve.wait_ge(s("dve_step"), own.next())
                V.tensor_tensor(oh[:, :, :], oh[:, :, :], down[:, :].unsqueeze(1).to_broadcast([P, NT, E]), ALU.mult).then_inc(s("dve_step"), 1)
                dve.wait_ge(s("dve_step"), own.next())
                if k:
                    V.tensor_tensor(lgt[:, :, :], lgt[:, :, :], mbc, ALU.subtract).then_inc(s("f1_nmax"), 1)
                else:
                    dve.sem_inc(s("f0_nmax"), 1)
                V.tensor_reduce(posf[:, :], oh[:, :, :], AX.X, ALU.max).then_inc(s("dve_step"), 1)
                dve.wait_ge(s("dve_step"), own.next())
                V.tensor_tensor(oh[:, :, :], oh[:, :, :], posf[:, :].unsqueeze(2).to_broadcast([P, NT, E]), ALU.is_equal).then_inc(s("dve_step"), 1)
                dve.wait_ge(s("dve_step"), own.next())
                V.tensor_copy(ohb[:, :], oh[:, :, :].rearrange("p t e -> p (t e)")).then_inc(s(f"f{k}_oh"), 1)
                dve.wait_ge(s(f"f{k}_e"), 1)
                if k:
                    V.tensor_reduce(m16[:, :], rt[:, :, :], AX.X, ALU.add).then_inc(s("dve_step"), 1)
                    dve.wait_ge(s("dve_step"), own.next())
                else:
                    V.tensor_scalar(m16[:, :], m16[:, :], 1.0, None, ALU.add).then_inc(s("dve_step"), 1)
                    dve.wait_ge(s("dve_step"), own.next())
                V.reciprocal(wgt[:, :], m16[:, :]).then_inc(s("dve_step"), 1)
                dve.wait_ge(s("dve_step"), own.next())
                dve.wait_ge(s(f"f{k}_rank"), 2)
                V.tensor_copy(et[:, :, :], pb[6][:, 0:NT * E].rearrange("p (t e) -> p e t", e=E)).then_inc(s("dve_step"), 1)
                dve.wait_ge(s("dve_step"), own.next())
                flat = lambda v: v[:, :, :].rearrange("p e t -> p (e t)")
                V.tensor_tensor_scan(flat(incl), flat(seg), flat(et), 0.0, ALU.mult, ALU.add).then_inc(s("dve_step"), 1)
                dve.wait_ge(s("dve_step"), own.next())
                kk = kcmp[:, 0:T // ET, :].rearrange("p k e -> p e k")
                V.tensor_scalar(exf[:, :], kth[:, :], float(ET), None, ALU.mult).then_inc(s("dve_step"), 1)
                dve.wait_ge(s("dve_step"), own.next())
                V.tensor_tensor(kk, incl[:, :, NT - 1:NT].to_broadcast([P, E, T // ET]),
                                exf[:, 0:T // ET].unsqueeze(1).to_broadcast([P, E, T // ET]), ALU.is_gt).then_inc(s("dve_step"), 1)
                dve.wait_ge(s("dve_step"), own.next())
                V.tensor_reduce(ntile[:, :], kk, AX.X, ALU.add).then_inc(s("dve_step"), 1)
                dve.wait_ge(s("dve_step"), own.next())
                V.tensor_tensor_scan(tend[:, :], ones_f[:, 0:E], ntile[:, :], 0.0, ALU.mult, ALU.add).then_inc(s("dve_step"), 1)
                dve.wait_ge(s("dve_step"), own.next())
                V.tensor_tensor(kcmp[:, :, :], kth[:, :].unsqueeze(2).to_broadcast([P, MT, E]),
                                tend[:, :].unsqueeze(1).to_broadcast([P, MT, E]), ALU.is_ge).then_inc(s("dve_step"), 1)
                dve.wait_ge(s("dve_step"), own.next())
                V.tensor_reduce(exf[:, :], kcmp[:, :, :], AX.X, ALU.add).then_inc(s("dve_step"), 1)
                dve.wait_ge(s("dve_step"), own.next())
                V.tensor_scalar(exi[:, :], exf[:, :], float(E - 1), None, ALU.min).then_inc(s(f"f{k}_tiles"), 1)
                V.tensor_tensor(tbeg[:, :], tend[:, :], ntile[:, :], ALU.subtract).then_inc(s("dve_step"), 1)
                dve.wait_ge(s("dve_step"), own.next())
                V.tensor_tensor(flat(incl), flat(incl), flat(et), ALU.subtract).then_inc(s("dve_step"), 1)
                dve.wait_ge(s("dve_step"), own.next())
                V.scalar_tensor_tensor(incl[:, :, :], tbeg[:, :].unsqueeze(2).to_broadcast([P, E, NT]), float(ET),
                                       incl[:, :, :], ALU.mult, ALU.add).then_inc(s("dve_step"), 1)
                dve.wait_ge(s("dve_step"), own.next())
                V.tensor_tensor(rt[:, :, :], incl[:, :, :].rearrange("p e t -> p t e"),
                                pb[5][:, 0:NT * E].rearrange("p (t e) -> p t e", e=E), ALU.add).then_inc(s("dve_step"), 1)
                dve.wait_ge(s("dve_step"), own.next())
                V.tensor_tensor(rt[:, :, :], rt[:, :, :], oh[:, :, :], ALU.mult).then_inc(s("dve_step"), 1)
                dve.wait_ge(s("dve_step"), own.next())
                V.tensor_reduce(posf[:, :], rt[:, :, :], AX.X, ALU.add).then_inc(s("dve_step"), 1)
                dve.wait_ge(s("dve_step"), own.next())
                V.tensor_copy(posi[:, :], posf[:, :]).then_inc(s(f"f{k}_pos"), 1)

            def experts(k):
                def rows_T(i, m):
                    t = i * NB + m
                    dve.wait_ge(s(f"f{k}_in{m}"), i * 32 + 32)
                    dve.wait_ge(s(f"f{k}_xTp"), t + 1)
                    if k:
                        V.tensor_copy(xtT[m], pb[0][:, 0:ET]).then_inc(s(f"f{k}_xtT"), 1)
                    else:
                        V.tensor_scalar(xtT[m], pb[0][:, 0:ET], blob[m][:, O_GB:O_GB + 1], blob[m][:, O_GB + 1:O_GB + 2],
                                        ALU.mult, ALU.add).then_inc(s(f"f{k}_xtT"), 1)

                def plus_b2(t, m):
                    dve.wait_ge(s(f"f{k}_yp"), t + 1 + CREDIT)
                    V.tensor_scalar(ytT[m], pb[3][:, 0:ET], blob[m][:, O_B2:O_B2 + 1], None, ALU.add
                                    ).then_inc(s(f"f{k}_ytT"), 1)

                def rows_out(t, m, stored):
                    dve.wait_ge(s(f"f{k}_yb"), t + 1)
                    if stored is not None:
                        dve.wait_ge(s(f"f{k}_ys_out{m}"), stored * 16)
                    V.tensor_copy(ysb[m], pb[4][:, 0:ET]).then_inc(s(f"f{k}_ys"), 1)

                for m in range(NB):
                    rows_T(0, m)
                    if m:
                        plus_b2(m - 1, m - 1)
                    if m >= 2:
                        rows_out(m - 2, m - 2, None)
                with dve.Fori(1, MT // NB) as i:
                    for m in range(NB):
                        rows_T(i, m)
                        plus_b2(i * NB + (m - 1), (m - 1) % NB)
                        rows_out(i * NB + (m - 2), (m - 2) % NB, i if m >= 2 else i - 1)
                rows_out(MT - 2, NB - 2, MT // NB - 1)
                plus_b2(MT - 1, NB - 1)
                rows_out(MT - 1, NB - 1, MT // NB - 1)

            def combine(k):
                dve.wait_ge(s(f"f{k}_y_in"), 16 * NT)
                for b in range(B):
                    part = tmp[:, (b % 2) * L:(b % 2 + 1) * L]
                    if b >= 2:
                        dve.wait_ge(s("x_final" if k else "x_f0"), b - 1 + CREDIT)
                    for t in range(2):
                        tile = slice((2 * b + t) * D, (2 * b + t + 1) * D)
                        w = wgt[:, 2 * b + t:2 * b + t + 1]
                        if k == 0:
                            last = V.scalar_tensor_tensor(part[:, t * D:(t + 1) * D], yall[:, tile], w, h2[:, tile], ALU.mult, ALU.add)
                            if t:
                                last.then_inc(s("dve_step"), 1)
                                dve.wait_ge(s("dve_step"), own.next())
                        else:
                            last = V.scalar_tensor_tensor(part[:, t * D:(t + 1) * D], yall[:, tile], w, modrow[k][:, b, 3, :],
                                                          ALU.mult, ALU.mult)
                    if k == 0:
                        last = V.tensor_tensor(part.rearrange("p (t d) -> p t d", t=2), part.rearrange("p (t d) -> p t d", t=2),
                                               modrow[k][:, b:b + 1, 3, :].to_broadcast([P, 2, D]), ALU.mult)
                    last.then_inc(s("dve_step"), 1)
                    dve.wait_ge(s("dve_step"), own.next())
                    V.tensor_tensor(x[:, b * L:(b + 1) * L], x[:, b * L:(b + 1) * L], part, ALU.add
                                    ).then_inc(s("x_final" if k else "x_f0"), 1)

            dve.wait_ge(s("x_a"), NC + CREDIT)
            layernorm_rows("ln1", 0)
            dve.wait_ge(s("f0_h2"), B)
            layernorm("lnf", h2, xn)
            router(0)
            experts(0)
            combine(0)
            dve.wait_ge(s("x_f0"), B + CREDIT)
            layernorm("ln2", x, xn)

            V.tensor_scalar(ab[:, 0:1], ab[:, 0:1], QSCALE, None, ALU.mult).then_inc(s("abs"), 1)
            for qk in range(2):
                with dve.Fori(0, NC // 2) as i:
                    own.loop(i, 6)
                    for m in range(2):
                        c = i * 2 + m
                        t = ts(c, CH)
                        dve.wait_ge(s("qf"), c + (NC * qk + 1 + CREDIT))
                        apart(dve)
                        V.tensor_copy(parts[qk][0][:, t], qf[m]).then_inc(s("dve_step"), 1)
                        dve.wait_ge(s("dve_step"), own.next())
                        V.tensor_tensor(qr[m], qf[m], parts[qk][0][:, t], ALU.subtract).then_inc(s("dve_step"), 1)
                        dve.wait_ge(s("dve_step"), own.next())
                        apart(dve)
                        V.tensor_copy(parts[qk][1][:, t], qr[m]).then_inc(s("dve_step"), 1)
                        dve.wait_ge(s("dve_step"), own.next())
                        V.tensor_tensor(parts[qk][2][:, t], qr[m], parts[qk][1][:, t], ALU.subtract).then_inc(s("parts"), 1)
                own.end(NC // 2)
            with dve.Fori(0, NC // 2) as i:
                for m in range(2):
                    c = i * 2 + m
                    dve.wait_ge(s("vp"), c + 1)
                    for t in range(CH // P):
                        last = V.tensor_tensor(vsb[:, ds(c * 4 + t, 1), :].rearrange("p a d -> p (a d)"),
                                               pb[4 + m][:, t * P:(t + 1) * P], arow[:, 0, :], ALU.add)
                    last.then_inc(s("v"), 1)

            def max_head(b, h):
                dve.wait_ge(s("maxp"), b * H + (h + 1))
                V.tensor_reduce(mx[:, 2 * h:2 * h + 2], pb[h % 2][:, :].rearrange("p (q l) -> p q l", q=2), AX.X, ALU.max
                                ).then_inc(s("mx"), 1)

            def max_rows(b):
                dve.wait_ge(s("mx"), b * H + H + CREDIT)
                V.tensor_scalar(mneg, mx, -1.0, None, ALU.mult).then_inc(s("mneg"), 1)
                dve.wait_ge(s("mT"), b + 1)
                dve.wait_ge(s("max_in"), b * 32)
                V.tensor_copy(mpart[:, 0:P], pb[7][0:2 * H, 0:P]).then_inc(s("dve_step"), 1)
                dve.wait_ge(s("dve_step"), own.next())
                V.tensor_tensor(mpart[:, P:2 * P], pb[7][0:2 * H, 0:P], mpart[:, 0:P], ALU.subtract).then_inc(s("mparts"), 1)

            def normalise(b, g):
                dve.wait_ge(s("pv"), b * H + (g + 1) * H // 2 + CREDIT)
                V.reciprocal(rden[g], pb[4 + g][P // 2:P, 0:L]).then_inc(s("dve_step"), 1)
                dve.wait_ge(s("dve_step"), own.next())
                if g == 0:
                    dve.wait_ge(s("aop"), b + CREDIT)
                V.tensor_tensor(oT[g * P // 2:(g + 1) * P // 2, :], pb[4 + g][0:P // 2, 0:L], rden[g], ALU.mult
                                ).then_inc(s("nrm"), 1)

            def residual(b):
                dve.wait_ge(s("aop"), b + 1 + CREDIT)
                for q in range(2):
                    last = V.tensor_tensor(osum[:, q * D:(q + 1) * D], pb[6][:, q * D:(q + 1) * D], arow[:, 1, :], ALU.add)
                last.then_inc(s("dve_step"), 1)
                dve.wait_ge(s("dve_step"), own.next())
                for q in range(2):
                    last = V.tensor_tensor(osum[:, q * D:(q + 1) * D], osum[:, q * D:(q + 1) * D],
                                           modrow[1][:, ds(b, 1), 0, :].rearrange("p a d -> p (a d)"), ALU.mult)
                last.then_inc(s("dve_step"), 1)
                dve.wait_ge(s("dve_step"), own.next())
                V.tensor_tensor(x[:, ds(b * L, L)], x[:, ds(b * L, L)], osum, ALU.add).then_inc(s("x_b"), 1)

            def attn(b, first, last_b):
                if not first:
                    normalise(b - 1, 1)
                for h in range(H):
                    if not last_b:
                        max_head(b + 1, h)
                    if h == 4 and not first:
                        residual(b - 1)
                    if h == 10:
                        normalise(b, 0)
                if not last_b:
                    max_rows(b + 1)

            for h in range(H):
                max_head(0, h)
            max_rows(0)
            attn(0, True, False)
            with dve.Fori(0, (B - 2) // 2) as i:
                own.loop(i, 10)
                for m in range(2):
                    attn(i * 2 + (1 + m), False, False)
            own.end((B - 2) // 2)
            attn(B - 1, False, True)
            normalise(B - 1, 1)
            residual(B - 1)

            dve.wait_ge(s("x_b"), B + CREDIT)
            layernorm_rows("ln3", 1)
            router(1)
            experts(1)
            combine(1)

        @block.tensor
        def _(pe):
            give_credit(pe, CREDITED["PE"])
            mm = nc.tensor.matmul

            def mod_rows(k):
                for b in range(B):
                    pe.wait_ge(s("srep"), k * B + b + 1)
                    if b >= 2:
                        pe.wait_ge(s(f"m{k}_cp"), b - 1)
                    elif k:
                        pe.wait_ge(s("m0_cp"), B + b - 1)
                    mm(pb[6 + b % 2][:, :], srep[:, k * B + b, :], wmod[:, k, 2 * D:6 * D], start=True, stop=True).then_inc(s(f"m{k}_ps"), 1)

            def transposes(ready, src, done, used):
                for b in range(B):
                    pe.wait_ge(s(ready), (b + 1) * (2 if ready.startswith("ln") else 1))
                    if b >= 2:
                        pe.wait_ge(s(used), b - 1 + CREDIT)
                    for t in range(2):
                        last = nc.tensor.transpose(pb[b % 2][:, t * P:(t + 1) * P], src[:, b * L + t * P:b * L + (t + 1) * P], ident[:, :])
                    last.then_inc(s(done), 1)

            pe.wait_ge(s("mod_in"), 16 * len(MOD_LOADS))
            pe.wait_ge(s("consts"), CONSTS)
            pe.wait_ge(s("silc"), 1)
            for k in range(2):
                for j in range(2):
                    col = (2 * k + j) * B
                    last = mm(pb[5][:, col:col + B], wmod[:, k, j * D:(j + 1) * D], silc[:, k * B:(k + 1) * B], start=True, stop=True)
            last.then_inc(s("modTp"), 1)
            transposes("ln0_xn", xn, "ln0_xT", "ln0_hT")
            for k in range(2):
                mod_rows(k)

            pe.wait_ge(s("wtap"), TAPS)
            pe.wait_ge(s("modT"), 2)
            with pe.Fori(0, NC) as c:
                pe.wait_ge(s("ln0_hT"), c * 2 + 2 + CREDIT)
                pe.wait_ge(s("xi"), c * 4 + CREDIT)
                for h in range(2):
                    for tap in range(TAPS):
                        last = mm(pb[2 + h][:, :], wtap[:, tap, h * P:(h + 1) * P], hT[:, ds(c * 2, 2), tap:tap + L],
                                  start=(tap == 0), stop=(tap == TAPS - 1))
                    last.then_inc(s("inproj"), 1)
                for h in range(2):
                    mm(pb[4 + h][:, :], inw[:, DI + h * P:DI + (h + 1) * P], hT[:, ds(c * 2, 2), PAD:PAD + L],
                       start=True, stop=True).then_inc(s("inproj"), 1)

            pe.wait_ge(s("w_in"), ALL_W)
            pe.wait_ge(s("late_consts"), LATE_CONSTS)
            pe.wait_ge(s("m1_cp"), B)
            with pe.Fori(0, NC) as c:
                t = ts(c, CH)
                pe.wait_ge(s("xi"), c * 4 + 4 + CREDIT)
                pe.wait_ge(s("drs"), c + CREDIT)
                for h in range(2):
                    last = mm(pb[6][0:DTR, :], xpw[:, h, 0:DTR], xi[:, h, t], start=(h == 0), stop=(h == 1))
                last.then_inc(s("draw"), 1)
                pe.wait_ge(s("bc"), c + CREDIT)
                for h in range(2):
                    last = mm(pb[7][:, :], xbc[:, h, :], xi[:, h, t], start=(h == 0), stop=(h == 1))
                last.then_inc(s("bcp"), 1)
                pe.wait_ge(s("drs"), c + 1 + CREDIT)
                pe.wait_ge(s("delta"), c + CREDIT)
                for h in range(2):
                    mm(pb[h][:, :], dtw[:, h * P:(h + 1) * P], drs, start=True, stop=True).then_inc(s("dtp"), 1)
                pe.wait_ge(s("delta"), c + 1 + CREDIT)
                pe.wait_ge(s("dlt"), c * 2 + CREDIT)
                pe.wait_ge(s("u"), c * 2 + CREDIT)
                if True:
                    pe.wait_ge(s("xi"), 4 * NC + CREDIT)
                for h in range(2):
                    for g in range(2):
                        last = mm(pb[2 + h][:, :], adj[:, g, h * P:(h + 1) * P], delta[g], start=(g == 0), stop=(g == 1))
                    last.then_inc(s("adjp"), 1)

            pe.wait_ge(s("bc"), NC + CREDIT)
            pe.wait_ge(s("dlt"), 2 * NC + CREDIT)
            pe.wait_ge(s("u"), 2 * NC + CREDIT)
            with pe.Fori(0, NC) as c:
                t = ts(c, CH)

                def b_row(n):
                    pe.wait_ge(s("bsb"), c * NS + (n - 1 + CREDIT))
                    mm(pb[n % 2][:, :], pick[:, n, :], bc[:, t], start=True, stop=True).then_inc(s("bbp"), 1)

                def c_row(n):
                    pe.wait_ge(s("hc"), c * 2 * NS + (2 * n - 2 + CREDIT))
                    mm(pb[2 + n % 2][:, :], pick[:, NS + n, :], bc[:, t], start=True, stop=True).then_inc(s("cbp"), 1)

                def sum_state(n):
                    for h in range(2):
                        pe.wait_ge(s("hc"), c * 2 * NS + (2 * n + h + 1 + CREDIT))
                        mm(pb[4 + h][:, :], ident[:, :], hc[(2 * n + h) % 4], start=(n == 0), stop=(n == NS - 1)).then_inc(s("hsum"), 1)

                b_row(0)
                b_row(1)
                c_row(0)
                pe.wait_ge(s("yg"), c * 2 + CREDIT)
                for n in range(NS):
                    if n + 2 < NS:
                        b_row(n + 2)
                    if n + 1 < NS:
                        c_row(n + 1)
                    if n:
                        sum_state(n - 1)
                sum_state(NS - 1)
                pe.wait_ge(s("yg"), c * 2 + 2 + CREDIT)
                pe.wait_ge(s("x_a"), c + CREDIT)
                for q in range(CH // P):
                    for h in range(2):
                        last = mm(pb[6][:, q * P:(q + 1) * P], yg[h][:, q * P:(q + 1) * P], outw[:, h, :],
                                  start=(h == 0), stop=(h == 1))
                last.then_inc(s("outp"), 1)

            def router(k):
                transposes(f"f{k}_h2", h2, f"f{k}_h2Tp", f"f{k}_h2T")
                pe.wait_ge(s(f"f{k}_h2T"), B + CREDIT)
                for t in range(NT):
                    last = mm(pb[7][:, t * E:(t + 1) * E], h2T[:, t * P:(t + 1) * P], cent[:, k, :], start=True, stop=True)
                last.then_inc(s(f"f{k}_sc"), 1)
                pe.wait_ge(s(f"f{k}_oh"), 1)
                mm(pb[5][:, 0:NT * E], tri[:, :], ohb[:, :], start=True, stop=True).then_inc(s(f"f{k}_rank"), 1)
                mm(pb[6][:, 0:NT * E], ones_b[:, :], ohb[:, :], start=True, stop=True).then_inc(s(f"f{k}_rank"), 1)

            def experts(k):
                pe.wait_ge(s(f"f{k}_pos"), 1)

                def up(i, m):
                    t = i * NB + m
                    pe.wait_ge(s(f"f{k}_in{m}"), i * 32 + 32)
                    for q in range(2):
                        last = nc.tensor.transpose(pb[0][:, q * P:(q + 1) * P], xt[m][:, q * P:(q + 1) * P], ident[:, :])
                    last.then_inc(s(f"f{k}_xTp"), 1)
                    pe.wait_ge(s(f"f{k}_xtT"), t + 1)
                    for g in range(2):
                        pe.wait_ge(s(f"f{k}_h1"), t * FC + (2 * g - 2 + CREDIT))
                        for f in range(2):
                            last = mm(pb[1 + g][:, f * ET:(f + 1) * ET], blob[m][:, (2 * g + f) * P:(2 * g + f + 1) * P], xtT[m],
                                      start=True, stop=True)
                        last.then_inc(s(f"f{k}_hid"), 1)

                def down_(t, m):
                    pe.wait_ge(s(f"f{k}_h1"), t * FC + FC + CREDIT)
                    pe.wait_ge(s(f"f{k}_ytT"), t + CREDIT)
                    for f in range(FC):
                        last = mm(pb[3][:, 0:ET], blob[m][:, O_W2 + f * P:O_W2 + (f + 1) * P], h1[m][:, f, :],
                                  start=(f == 0), stop=(f == FC - 1))
                    last.then_inc(s(f"f{k}_yp"), 1)

                def back(t, m):
                    pe.wait_ge(s(f"f{k}_ytT"), t + 1 + CREDIT)
                    pe.wait_ge(s(f"f{k}_ys"), t + CREDIT)
                    for q in range(2):
                        last = nc.tensor.transpose(pb[4][:, q * P:(q + 1) * P], ytT[m][:, q * P:(q + 1) * P], ident[:, :])
                    last.then_inc(s(f"f{k}_yb"), 1)

                for m in range(NB):
                    up(0, m)
                    if m:
                        down_(m - 1, m - 1)
                    if m >= 2:
                        back(m - 2, m - 2)
                with pe.Fori(1, MT // NB) as i:
                    for m in range(NB):
                        up(i, m)
                        down_(i * NB + (m - 1), (m - 1) % NB)
                        back(i * NB + (m - 2), (m - 2) % NB)
                back(MT - 2, NB - 2)
                down_(MT - 1, NB - 1)
                back(MT - 1, NB - 1)

            router(0)
            experts(0)
            transposes("ln2_xn", xn, "ln2_xT", "ln2_hT")

            pe.wait_ge(s("ln2_hT"), B + CREDIT)
            for qk in range(2):
                with pe.Fori(0, NC // 2) as i:
                    for m in range(2):
                        c = i * 2 + m
                        pe.wait_ge(s("qf"), i * 2 + NC * qk + CREDIT)
                        mm(pb[2 + m][:, :], aw[:, qk, :], hT[:, ds(c * 2, 2), PAD:PAD + L], start=True, stop=True).then_inc(s("qkp"), 1)
            for c in range(NC):
                if c >= 2:
                    pe.wait_ge(s("v"), c - 1)
                for t in range(CH // P):
                    last = mm(pb[4 + c % 2][:, t * P:(t + 1) * P],
                              hT[:, c * 2 + t // 2, PAD + (t % 2) * P:PAD + (t % 2 + 1) * P],
                              aw[:, 2, :], start=True, stop=True)
                last.then_inc(s("vp"), 1)
            pe.wait_ge(s("v"), NC)
            pe.wait_ge(s("rows_in"), 96)

            def max_scores(b, m, h, first):
                if not (first and h < 2):
                    pe.wait_ge(s("mx"), b * H + (h - 1 + CREDIT))
                for q in range(2):
                    last = mm(pb[h % 2][:, q * L:(q + 1) * L], qA[m][0:KMAX, h, q * P:(q + 1) * P], kA[m][0:KMAX, h, :],
                              start=True, stop=True)
                last.then_inc(s("maxp"), 1)

            def max_T(b):
                pe.wait_ge(s("mneg"), b + 1)
                nc.tensor.transpose(pb[7][0:2 * H, 0:P], mneg, ident[:, :]).then_inc(s("mT"), 1)

            def exp_scores(b, m, h, first):
                if not (first and h < 2):
                    pe.wait_ge(s("pT"), b * H + (h - 1 + CREDIT))
                for k in range(2):
                    last = mm(pb[2 + h % 2][:, k * L:(k + 1) * L], kA[m][0:KEXP, h, k * P:(k + 1) * P], qA[m][0:KEXP, h, :],
                              start=True, stop=True)
                last.then_inc(s("sT"), 1)

            def values(b, m, h):
                g = h // (H // 2)
                pe.wait_ge(s("pT"), b * H + (h + 1 + CREDIT))
                if h % (H // 2) == 0:
                    pe.wait_ge(s("nrm"), b * 2 + (g - 1 + CREDIT))
                for k in range(2):
                    last = mm(pb[4 + g][:, 0:L], vz[m][:, 2 * k + g, h % HD, :], pexp[h % 4][:, k * L:(k + 1) * L],
                              start=(h % (H // 2) == 0 and k == 0), stop=(h % (H // 2) == H // 2 - 1 and k == 1))
                last.then_inc(s("pv"), 1)

            def out_proj(b):
                pe.wait_ge(s("nrm"), b * 2 + 2 + CREDIT)
                pe.wait_ge(s("x_b"), b + CREDIT)
                for q in range(2):
                    last = mm(pb[6][:, q * D:(q + 1) * D], oT[:, q * P:(q + 1) * P], aw[:, 3, :], start=True, stop=True)
                last.then_inc(s("aop"), 1)

            def attn(b, m, first, last_b, loads):
                pe.wait_ge(s("max_in"), b * 32 + 32)
                pe.wait_ge(s("vz"), b + 1 + CREDIT)
                for h in range(H):
                    exp_scores(b, m, h, first)
                    if h:
                        values(b, m, h - 1)
                    if h == 2 and not first:
                        out_proj(b - 1)
                    if not last_b:
                        if h == 5:
                            pe.wait_ge(s(f"qk_in{1 - m}"), loads * 32)
                        if 5 <= h < 13:
                            max_scores(b + 1, 1 - m, 2 * (h - 5), False)
                            max_scores(b + 1, 1 - m, 2 * (h - 5) + 1, False)
                        if h == 14:
                            max_T(b + 1)
                values(b, m, H - 1)

            pe.wait_ge(s("qk_in0"), 32)
            for h in range(H):
                max_scores(0, 0, h, True)
            max_T(0)
            attn(0, 0, True, False, 1)
            with pe.Fori(0, (B - 2) // 2) as i:
                for m in (1, 0):
                    attn(i * 2 + (2 - m), m, False, False, i + 2)
            attn(B - 1, 1, False, True, 0)
            out_proj(B - 1)

            router(1)
            experts(1)


def _kernel_arrays(i):
    g = {k: np.asarray(v) for k, v in i.items()}
    c = np.ascontiguousarray
    halves = lambda w: c(w.reshape(2, P, -1).transpose(1, 0, 2))
    xp = g["L0_attn_x_proj_w"]
    bcw = xp[:, DTR:]
    f32 = np.float32
    pos = np.arange(L, dtype=f32)
    slopes = np.power(f32(2.0), np.linspace(-4.0, -0.3, H, dtype=f32)).astype(f32)
    bias = -(slopes[:, None] * pos[None, :])
    bf = mybir.dt.np(mybir.dt.bfloat16)
    rows, rest = [], bias
    for _ in range(3):
        part = rest.astype(bf)
        rows.append(part)
        rest = rest - part.astype(f32)

    def blob(w1, w2, b1, b2, gamma, beta):
        cols = [w1, w2.reshape(E, FC, P, D).transpose(0, 2, 1, 3).reshape(E, P, FC * D),
                b2[:, :, None], b1.reshape(E, FC, P).transpose(0, 2, 1),
                gamma[:, :, None], beta[:, :, None]]
        return c(np.concatenate(cols, axis=2))

    none = np.zeros((E, D), f32)
    return {
        "x": c(g["L0_attn_x"].reshape(T, D)),
        "cT": c(np.concatenate([g["L0_c"].T, g["L1_c"].T], axis=1)),
        "wmod": c(np.stack([g["L0_wmod"], g["L1_wmod"]], axis=1)),
        "in_w": c(g["L0_attn_in_proj_w"]),
        "conv_w": c(np.broadcast_to(g["L0_attn_conv_w"].reshape(DI, TAPS).T[None], (P, TAPS, DI))),
        "conv_b": c(g["L0_attn_conv_b"].reshape(2, P).T),
        "A_log": c(halves(g["L0_attn_A_log"]).reshape(P, 2 * NS)),
        "xp_w": halves(xp),
        "xbc_w": halves(np.concatenate([bcw, np.zeros((DI, 32), f32), bcw, bcw], axis=1)),
        "dt_w": c(g["L0_attn_dt_proj_w"]),
        "dt_b": c(g["L0_attn_dt_proj_b"].reshape(2, P).T),
        "adj": halves(g["L0_attn_adj"]),
        "d_skip": c(g["L0_attn_D"].reshape(2, P).T),
        "out_w": halves(g["L0_attn_out_proj_w"]),
        "router_w": c(np.stack([g["L0_ffn_centroids"].T, g["L1_ffn_Wr"]], axis=1)),
        "br": c(np.broadcast_to(g["L1_ffn_br"], (P, E))),
        "attn_w": c(np.stack([g[f"L1_attn_W{n}"].T for n in "qkvo"], axis=1)),
        "attn_b": c(np.stack([g["L1_attn_bq"], g["L1_attn_bk"]], axis=1)),
        "attn_row": c(np.broadcast_to(np.stack([g["L1_attn_bv"], g["L1_attn_bo"]])[None], (P, 2, D))),
        "bias_rows": c(np.stack(rows)),
        "one_rows": np.ones((5, H, L), bf),
        "blob0": blob(g["L0_ffn_W1"].transpose(0, 2, 1), g["L0_ffn_W2"].transpose(0, 2, 1), g["L0_ffn_b1"], g["L0_ffn_b2"],
                      g["L0_ffn_gamma"], g["L0_ffn_beta"]),
        "blob1": blob(g["L1_ffn_W1"], g["L1_ffn_W2"], g["L1_ffn_b1"], g["L1_ffn_b2"], none, none),
    }


def kernel(**inputs):
    import concourse.bacc as _bacc
    from concourse.bass_utils import run_bass_kernel_spmd as _run

    nc = _bacc.Bacc("TRN2", target_bir_lowering=False, num_devices=1)
    arrays = _kernel_arrays(inputs)
    aps = {name: nc.dram_tensor(f"in_{name}", v.shape, mybir.dt.from_np(v.dtype), kind="ExternalInput").ap()
           for name, v in arrays.items()}
    out = nc.dram_tensor("out", (T, D), mybir.dt.float32, kind="ExternalOutput").ap()
    build(nc, aps, out)
    r = _run(nc, [{f"in_{name}": v for name, v in arrays.items()}], core_ids=[0])
    return r.results[0]["out"].reshape(B, L, D)
```

```python
import numpy as np
import concourse.bass as bass
from concourse import mybir
from contextlib import ExitStack

B, L, D = 8, 256, 128
T = B * L
P = 128
NT = T // P
CH = 512
NC = T // CH
DI, NS, DTR, TAPS = 256, 16, 64, 4
PAD = TAPS - 1
E, F = 8, 512
FC = F // P
H, HD = 16, 8
ET = 2 * P
MT = T // ET + E - 1
NB = 5
EPS = 1e-5
CREDIT = 8
GT = 4
LEAD = 4
HEAD = 8
QSCALE = float(np.float32(1.0) / np.sqrt(np.float32(HD)))
QPART = (0, 0, 0, 1, 1, 2)
KPART = (0, 1, 2, 0, 1, 0)
KR = len(QPART) * HD
KMAX = KR + 3
KEXP = KMAX + 2
BLOB = 2 * F + 1 + FC + 2
O_W2, O_B2, O_B1, O_GB = F, 2 * F, 2 * F + 1, 2 * F + 1 + FC


class Steps:

    def __init__(self):
        self.base, self.n = 0, 0

    def next(self):
        self.n += 1
        return self.base + self.n

    def loop(self, i, steps):
        self.start, self.steps = self.base + self.n, steps
        self.base, self.n = i * steps + self.start, 0

    def end(self, count):
        assert self.n == self.steps, (self.n, self.steps)
        self.base, self.n = self.start + count * self.steps, 0


def build(nc, a, out):
    fp32, bf16, i32 = mybir.dt.float32, mybir.dt.bfloat16, mybir.dt.int32
    ALU, ACT, AX = mybir.AluOpType, mybir.ActivationFunctionType, mybir.AxisListType
    ds, ts = bass.ds, bass.ts
    ctx = ExitStack()
    with ctx:
        def sb(name, shape, dt=fp32):
            return ctx.enter_context(nc.sbuf_tensor(name, shape, dt))

        def dram(name, shape, dt=fp32):
            return nc.dram_tensor(name, shape, dt, kind="Internal").ap()

        sems = {}

        def s(name):
            if name not in sems:
                sems[name] = ctx.enter_context(nc.semaphore(name))
            return sems[name]

        x = sb("x", [P, T])
        xn = sb("xn", [P, T])
        hT = sb("hT", [P, B, L])
        ident = sb("ident", [P, P])
        tri = sb("tri", [P, P], bf16)
        ones_b = sb("ones_b", [P, P], bf16)
        ones_f = sb("ones_f", [P, P])
        epst = sb("epst", [P, 1])
        stats = sb("stats", [P, NT * 6])
        meanvar = sb("meanvar", [P, NT * 2])
        std = sb("std", [P, NT])
        rstd = sb("rstd", [P, NT])
        cT = sb("cT", [P, 2 * B])
        silc = sb("silc", [P, 2 * B])
        wmod = sb("wmod", [P, 2, 6 * D])
        modT = sb("modT", [P, 2, 4, B])
        modrow = [sb(f"modrow{k}", [P, B, 4, D]) for k in (0, 1)]
        inw = sb("inw", [P, 2 * DI])
        convw = sb("convw", [P, 2, TAPS])
        convb = sb("convb", [P, 2])
        xpw = sb("xpw", [P, 2, DTR + 2 * NS])
        dtw = sb("dtw", [DTR, DI])
        dtb = sb("dtb", [P, 2])
        adj = sb("adj", [P, 2, DI])
        alog = sb("alog", [P, 2 * NS])
        aneg = sb("aneg", [P, 2 * NS])
        dskip = sb("dskip", [P, 2])
        ddiag = sb("ddiag", [P, 2, P])
        outw = sb("outw", [P, 2, D])
        bc = sb("bc", [P, T], bf16)
        pick = sb("pick", [P, 2 * NS, P], bf16)
        lent = modrow[1][:, :, :, :].rearrange("p b j d -> p (b j d)")
        dA = [sb(f"dA{k}", [P, 2, 2, L])[:, :, :, :] for k in (0, 1)] + [
            lent[:, k * 2 * CH:(k + 1) * 2 * CH].rearrange("p (h b l) -> p h b l", h=2, b=2) for k in (0, 1)]
        tmp = sb("tmp", [P, CH])
        big = sb("big", [P, 8 * T])
        scr = sb("scr", [P, 19, CH])
        cent = sb("cent", [P, 2, E])
        br = sb("br", [P, E])
        iot = sb("iot", [P, MT], i32)
        kth = sb("kth", [P, MT])
        down = sb("down", [P, E])
        lgt = sb("lgt", [P, NT, E])
        oh = sb("oh", [P, NT, E])
        ohb = sb("ohb", [P, NT * E], bf16)
        rt = sb("rt", [P, NT, E])
        smax = sb("smax", [P, NT])
        m16 = sb("m16", [P, NT])
        et = sb("et", [P, E, NT])
        incl = sb("incl", [P, E, NT])
        seg = sb("seg", [P, E, NT])
        ntile = sb("ntile", [P, E])
        tend = sb("tend", [P, E])
        tbeg = sb("tbeg", [P, E])
        kcmp = sb("kcmp", [P, MT, E])
        exf = sb("exf", [P, MT])
        exi = sb("exi", [P, MT], i32)
        posf = sb("posf", [P, NT])
        posi = sb("posi", [P, NT], i32)
        wgt = sb("wgt", [P, NT])
        aw = sb("aw", [P, 4, P])
        ab = sb("ab", [P, 2])
        arow = sb("arow", [P, 2, D])

        pb = [ctx.enter_context(nc.psum_tensor(f"pb{k}", [P, CH], fp32)) for k in range(8)]

        xs_d = [dram(f"xs{k}", (MT * ET, D)) for k in (0, 1)]
        ys_d = [dram(f"ys{k}", (MT * ET, D)) for k in (0, 1)]
        qk_d = dram("qk_parts", (2, KR // HD, HD, H, T), bf16)

        xi = big[:, 0:2 * T].rearrange("p (h t) -> p h t", h=2)
        gres = big[:, 2 * T:4 * T].rearrange("p (h t) -> p h t", h=2)
        dlt = big[:, 4 * T:6 * T].rearrange("p (h t) -> p h t", h=2)
        u = big[:, 6 * T:8 * T].rearrange("p (h t) -> p h t", h=2)
        srep = [big[:, 4 * T:4 * T + B * P].rearrange("p (b m) -> p b m", m=P),
                big[:, 7 * T:7 * T + B * P].rearrange("p (b m) -> p b m", m=P)]
        drs = [scr[0:DTR, k, :] for k in (0, 1)]
        bcr = [scr[DTR:DTR + 2 * NS, k, :] for k in (0, 1)]
        bmid = [scr[DTR:DTR + 2 * NS, 2 + k, 0:CH // 2].bitcast(bf16) for k in (0, 1)]
        delta = scr[:, 4:4 + 2 * NC, :].rearrange("p (c h) t -> p c h t", h=2)
        xraw = [[scr[:, 12:17, :].rearrange("p a t -> p (a t)")[:, (2 * k + h) * 2 * (PAD + L):(2 * k + h + 1) * 2 * (PAD + L)]
                 .rearrange("p (b l) -> p b l", b=2) for h in (0, 1)] for k in (0, 1)]
        dBu = [scr[:, 2 * k:2 * k + 2, :] for k in (0, 1)] + [lent[:, k * 2 * CH:(k + 1) * 2 * CH].rearrange("p (h t) -> p h t", h=2)
                                                              for k in (2, 3)]
        hs = [scr[:, 2 * k:2 * k + 2, :] for k in (2, 3)] + [hT[:, 4 * k:4 * k + 4, :].rearrange("p (h b) l -> p h (b l)", h=2)
                                                             for k in (0, 1)]
        hc = [scr[:, 2 * k:2 * k + 2, :] for k in (4, 5)] + [xn[:, 2 * k * CH:2 * (k + 1) * CH].rearrange("p (h t) -> p h t", h=2)
                                                             for k in (0, 1)]
        bsb = [scr[:, k, :] for k in (12, 13, 14, 17)]
        yg = [scr[:, k, :] for k in (15, 16)]
        sign = [scr[:, 17:19, :].rearrange("p a (b d) -> p (a b) d", d=D),
                big[:, 6 * T:6 * T + B * D].rearrange("p (b d) -> p b d", d=D)]
        blob = [big[:, k * BLOB:(k + 1) * BLOB] for k in range(NB)]
        e0 = NB * BLOB
        xt = [big[:, e0 + k * ET:e0 + (k + 1) * ET] for k in range(NB)]
        ysb = [big[:, e0 + (NB + k) * ET:e0 + (NB + k + 1) * ET] for k in range(NB)]
        assert e0 + 2 * NB * ET <= 5 * T
        h1 = [scr[:, 2 * k:2 * k + 2, :].rearrange("p a (f t) -> p (a f) t", f=2) for k in range(NB)]
        xtT = [scr[:, 2 * NB + k, 0:ET] for k in range(NB)]
        ytT = [scr[:, 2 * NB + k, ET:2 * ET] for k in range(NB)]
        assert 3 * NB <= 19
        h2 = big[:, 5 * T:6 * T]
        h2T = big[:, 6 * T:7 * T]
        ygate = hT[:, :, :].rearrange("p b l -> p (b l)")
        yall = big[:, 7 * T:8 * T]
        qA = [big[:, k * T:(k + 1) * T].bitcast(bf16).rearrange("p (h l) -> p h l", h=H) for k in (0, 1)]
        kA = [big[:, k * T:(k + 1) * T].bitcast(bf16).rearrange("p (h l) -> p h l", h=H) for k in (2, 3)]
        parts = [v.bitcast(bf16).rearrange("p (r t) -> p r t", r=3) for v in (
            scr[:, 11:14, :].rearrange("p a t -> p (a t)")[:, 0:3 * CH // 2],
            scr[:, 11:14, :].rearrange("p a t -> p (a t)")[:, 3 * CH // 2:3 * CH],
            scr[:, 4:6, :].rearrange("p a t -> p (a t)")[:, 0:3 * CH // 2],
            scr[:, 6:8, :].rearrange("p a t -> p (a t)")[:, 0:3 * CH // 2])]
        vz = [big[:, (4 + 2 * k) * T:(6 + 2 * k) * T].rearrange("p (k g j c) -> p (k g) j c", k=2, g=2, j=HD) for k in (0, 1)]
        qf = [scr[:, k, :] for k in (0, 1)]
        qr = [scr[:, k, :] for k in (2, 3)]
        pexp = [scr[:, k, :] for k in range(4, 8)]
        oT = scr[:, 8, 0:L]
        rden = [scr[0:P // 2, 12 + g, 0:L] for g in (0, 1)]
        mx = scr[:, 9, 0:2 * H]
        mneg = scr[:, 9, 2 * H:4 * H]
        mpart = scr[0:2 * H, 10, 0:P].bitcast(bf16)
        vsb = scr[:, 14:18, :].rearrange("p a (t d) -> p (a t) d", d=D)
        osum = scr[:, 11, 0:2 * D]

        MOD_LOADS = [(cT[:, :], a["cT"]), (wmod[:, :, :], a["wmod"])]
        IN_LOADS = [(inw[:, :], a["in_w"]), (convw[:, :, :], a["conv_w"]), (convb[:, :], a["conv_b"])]
        W_LOADS = [
            (xpw[:, :, :], a["xp_w"]),
            (dtw[:, :], a["dt_w"]), (dtb[:, :], a["dt_b"]), (adj[:, :, :], a["adj"]), (alog[:, :], a["A_log"]),
            (dskip[:, :], a["d_skip"]), (outw[:, :, :], a["out_w"]), (cent[:, :, :], a["router_w"]),
            (br[:, :], a["br"]), (aw[:, :, :], a["attn_w"]), (ab[:, :], a["attn_b"]), (arow[:, :, :], a["attn_row"]),
        ]
        ALL_W = 16 * len(W_LOADS)
        CONSTS, LATE_CONSTS = 7, 9

        CREDITED = {
            "Activation": "ys_out0 ys_out1 ys_out2 ys_out3 ys_out4 ln2_hT bsb pT ln0_hT oT f0_h2T f1_h2T f0_h1 f1_h1",
            "DVE": "scan hc yg x_a mx nrm x_b f0_ys f1_ys f0_ytT f1_ytT",
            "PE": "hsum outp pv sT aop f0_yp f1_yp",
            "Pool": "dBu vz",
        }

        def give_credit(eng, names):
            for name in names.split():
                eng.sem_inc(s(name), CREDIT)

        def apart(eng):
            eng.sem_inc(s("apart"), 1)

        block = ctx.enter_context(nc.Block())

        @block.sync
        def _(sp):
            for dst, src in MOD_LOADS:
                sp.dma_start(dst, src).then_inc(s("mod_in"), 16)
            for q in range(NC):
                sp.dma_start(x[:, q * CH:(q + 1) * CH].rearrange("p (t d) -> p t d", d=D),
                             a["x"][q * CH:(q + 1) * CH, :].rearrange("(t p) d -> p t d", p=P)).then_inc(s("x_in"), 16)
            for dst, src in IN_LOADS:
                sp.dma_start(dst, src).then_inc(s("inproj_in"), 16)
            for dst, src in W_LOADS:
                sp.dma_start(dst, src).then_inc(s("w_in"), 16)
            sp.wait_ge(s("zeroed"), 1)
            for k in range(2):
                for m in range(2):
                    sp.dma_start(xs_d[k][m * MT * P:(m + 1) * MT * P, :].rearrange("(t p) d -> p t d", p=P),
                                 big[:, 6 * T:6 * T + MT * P].rearrange("p (t d) -> p t d", d=D)
                                 ).then_inc(s("zeros_out"), 16)

            def experts(k):
                sp.wait_ge(s(f"f{k}_tiles"), 1)

                def load_weights(t, m):
                    e = sp.value_load(exi[0:1, ds(t, 1)], min_val=0, max_val=E - 1)
                    sp.dma_start(blob[m], a[f"blob{k}"][ds(e, 1), :, :].rearrange("a p c -> (a p) c")
                                 ).then_inc(s(f"tile_in{m}"), 16)

                def load_rows(t, m):
                    sp.dma_start(xt[m].rearrange("p (q d) -> p q d", d=D),
                                 xs_d[k][ds(t * ET, ET), :].rearrange("(q p) d -> p q d", p=P)).then_inc(s(f"tile_in{m}"), 16)

                for m in range(NB):
                    load_weights(m, m)
                sp.wait_ge(s(f"f{k}_xs_out"), 16 * NT)
                for m in range(NB):
                    load_rows(m, m)
                with sp.Fori(1, MT // NB) as i:
                    for m in range(NB):
                        t = i * NB + m
                        sp.wait_ge(s(f"f{k}_ytT"), t - NB + 1 + CREDIT)
                        load_weights(t, m)
                        load_rows(t, m)

            experts(0)

            for m in range(NB):
                sp.wait_ge(s(f"ys_out{m}"), 16 * (MT // NB) + CREDIT)
            for m in range(2):
                sp.dma_start(qA[m][KR:KMAX, :, :], a["one_rows"][0:3, :, :]).then_inc(s("rows_in"), 16)
                sp.dma_start(kA[m][KR:KMAX, :, :], a["bias_rows"]).then_inc(s("rows_in"), 16)
                sp.dma_start(kA[m][KMAX:KEXP, :, :], a["one_rows"][3:5, :, :]).then_inc(s("rows_in"), 16)

            def parts_out(c):
                for qk in range(2):
                    j = (2 * c + qk) % 4
                    sp.wait_ge(s("parts"), 2 * c + qk + 1)
                    if qk == 0:
                        for first, n in ((0, 3), (3, 2), (5, 1)):
                            p0 = QPART[first]
                            sp.dma_start(qk_d[qk, first:first + n, :, :, ts(c, CH)].rearrange("c d h t -> (d h) c t"),
                                         parts[j][:, p0:p0 + 1, :].to_broadcast([P, n, CH])).then_inc(s(f"parts_out{j}"), 16)
                    else:
                        sp.dma_start(qk_d[qk, 0:3, :, :, ts(c, CH)].rearrange("c d h t -> (d h) c t"), parts[j]
                                     ).then_inc(s(f"parts_out{j}"), 16)

            def load_qk(b, m):
                sp.dma_start(qA[m][0:KR, :, :],
                             qk_d[0, :, :, :, ds(b * L, L)].rearrange("c d h l -> (c d) h l")).then_inc(s(f"qk_in{m}"), 16)
                for first, n in ((0, 3), (3, 2), (5, 1)):
                    sp.dma_start(kA[m][first * HD:(first + n) * HD, :, :],
                                 qk_d[1, 0:n, :, :, ds(b * L, L)].rearrange("c d h l -> (c d) h l")).then_inc(s(f"qk_in{m}"), 16)

            def load_max(b, m):
                sp.wait_ge(s("mparts"), b + 1)
                for r in range(2):
                    sp.dma_start(qA[m][KMAX + r:KMAX + r + 1, :, :].rearrange("p h l -> p (h l)"),
                                 mpart[:, r * P:(r + 1) * P]).then_inc(s("max_in"), 16)

            parts_out(0)
            sp.wait_ge(s("parts_out0"), 48)
            sp.wait_ge(s("parts_out1"), 16)
            load_qk(0, 0)
            parts_out(1)
            load_qk(1, 1)
            parts_out(2)
            parts_out(3)
            load_max(0, 0)
            for j in range(4):
                sp.wait_ge(s(f"parts_out{j}"), 32 if j % 2 else 96)
            load_max(1, 1)
            with sp.Fori(0, (B - 2) // 2) as i:
                for m in range(2):
                    b = i * 2 + (2 + m)
                    sp.wait_ge(s("sT"), (b - 1) * H + CREDIT)
                    load_qk(b, m)
                    load_max(b, m)

            experts(1)

            for q in range(NC):
                sp.wait_ge(s("x_final"), q + 1)
                sp.dma_start(out[q * CH:(q + 1) * CH, :].rearrange("(t p) d -> p t d", p=P),
                             x[:, q * CH:(q + 1) * CH].rearrange("p (t d) -> p t d", d=D)).then_inc(s("out_done"), 16)
            sp.wait_ge(s("out_done"), 16 * NC)

        @block.gpsimd
        def _(pool):
            give_credit(pool, CREDITED["Pool"])
            own = Steps()
            nc.gpsimd.memset(ident[:, :], 0.0).then_inc(s("pool_step"), 1)
            pool.wait_ge(s("pool_step"), own.next())
            nc.gpsimd.affine_select(out=ident[:, :], in_=ident[:, :], compare_op=ALU.not_equal, fill=1.0,
                                    base=0, pattern=[[-1, P]], channel_multiplier=1).then_inc(s("consts"), 1)
            nc.gpsimd.memset(ones_f[:, :], 1.0).then_inc(s("consts"), 1)
            nc.gpsimd.memset(epst[:, :], EPS).then_inc(s("consts"), 1)
            for k in range(2):
                for h in range(2):
                    nc.gpsimd.memset(xraw[k][h][:, :, 0:PAD], 0.0).then_inc(s("consts"), 1)
            nc.gpsimd.memset(big[:, 6 * T:6 * T + MT * P], 0.0).then_inc(s("zeroed"), 1)
            for k in range(4):
                nc.gpsimd.memset(dA[k][:, :, :, 0:1], 0.0).then_inc(s("late_consts"), 1)
            nc.gpsimd.memset(pick[:, :, :], 0.0).then_inc(s("pool_step"), 1)
            pool.wait_ge(s("pool_step"), own.next())
            for off in (0, 64):
                nc.gpsimd.affine_select(
                    out=pick[:, :, :], in_=pick[:, :, :], compare_op=ALU.not_equal, fill=1.0,
                    base=-off, pattern=[[-1, 2 * NS], [0, P]], channel_multiplier=1).then_inc(s("pool_step"), 1)
                pool.wait_ge(s("pool_step"), own.next())
            nc.gpsimd.affine_select(
                out=pick[:, :, :], in_=pick[:, :, :], compare_op=ALU.not_equal, fill=1.0,
                base=-96, pattern=[[-1, 2 * NS], [0, P]], channel_multiplier=1).then_inc(s("late_consts"), 1)
            nc.gpsimd.memset(ones_b[:, :], 1.0).then_inc(s("pool_step"), 1)
            pool.wait_ge(s("pool_step"), own.next())
            nc.gpsimd.affine_select(out=tri[:, :], in_=ones_b[:, :], compare_op=ALU.is_gt, fill=0.0,
                                    base=0, pattern=[[1, P]], channel_multiplier=-1).then_inc(s("late_consts"), 1)
            nc.gpsimd.iota(iot[:, :], pattern=[[1, MT]], base=0, channel_multiplier=0).then_inc(s("pool_step"), 1)
            pool.wait_ge(s("pool_step"), own.next())
            nc.gpsimd.tensor_copy(kth[:, :], iot[:, :]).then_inc(s("pool_step"), 1)
            pool.wait_ge(s("pool_step"), own.next())
            nc.gpsimd.tensor_scalar(down[:, :], kth[:, 0:E], -1.0, float(E), ALU.mult, ALU.add).then_inc(s("late_consts"), 1)
            nc.gpsimd.memset(seg[:, :, :], 1.0).then_inc(s("pool_step"), 1)
            pool.wait_ge(s("pool_step"), own.next())
            nc.gpsimd.memset(seg[:, :, 0:1], 0.0).then_inc(s("late_consts"), 1)
            nc.gpsimd.memset(bc[:, :], 0.0).then_inc(s("late_consts"), 1)

            def gates(k):
                sg = sign[k]
                pool.wait_ge(s(f"m{k}_cp"), B)
                nc.gpsimd.tensor_scalar(modrow[k][:, :, 2, :], modrow[k][:, :, 2, :], 1.0, 1.0, ALU.mult, ALU.add
                                        ).then_inc(s("pool_step"), 1)
                pool.wait_ge(s("pool_step"), own.next())
                for j in (0, 3):
                    g = modrow[k][:, :, j, :]
                    nc.gpsimd.tensor_scalar(sg, g, 0.0, None, ALU.is_ge).then_inc(s("pool_step"), 1)
                    pool.wait_ge(s("pool_step"), own.next())
                    nc.gpsimd.tensor_scalar(sg, sg, 2.0, -1.0, ALU.mult, ALU.add).then_inc(s("pool_step"), 1)
                    pool.wait_ge(s("pool_step"), own.next())
                    nc.gpsimd.tensor_tensor(g, g, sg, ALU.mult).then_inc(s("pool_step"), 1)
                    pool.wait_ge(s("pool_step"), own.next())
                    nc.gpsimd.tensor_scalar(g, g, 0.25, None, ALU.max).then_inc(s("pool_step"), 1)
                    pool.wait_ge(s("pool_step"), own.next())
                    nc.gpsimd.tensor_tensor(g, g, sg, ALU.mult).then_inc(s("pool_step"), 1)
                    pool.wait_ge(s("pool_step"), own.next())
                pool.sem_inc(s("gates"), 1)

            gates(0)

            pool.wait_ge(s("u"), NC)
            with pool.Fori(0, NC) as c:
                for n in range(NS):
                    pool.wait_ge(s("bsb"), c * NS + (n + 1 + CREDIT))
                    pool.wait_ge(s("scan"), c * NS + (n - 3 + CREDIT))
                    apart(pool)
                    nc.gpsimd.tensor_tensor(dBu[n % 4], u[:, :, ts(c, CH)], bsb[n % 4].unsqueeze(1).to_broadcast([P, 2, CH]),
                                            ALU.mult).then_inc(s("dBu"), 1)

            pool.wait_ge(s("dBu"), NS * NC + CREDIT)
            for b in range(B):
                nc.gpsimd.tensor_scalar(srep[1][:, b, :], ones_f[:, :], silc[:, B + b:B + b + 1], None, ALU.mult
                                        ).then_inc(s("srep1"), 1)

            def sublayer_rows(k):
                key = ("ln1_xn", "ln3_xn")[k]
                rows = [v[:, :].rearrange("p (b t d) -> p b t d", b=B, t=2) for v in (xn, h2)]
                for b in range(B):
                    pool.wait_ge(s(key), 2 * b + 2)
                    nc.gpsimd.tensor_tensor(rows[1][:, b, :, :], rows[0][:, b, :, :],
                                            modrow[k][:, b:b + 1, 2, :].to_broadcast([P, 2, D]), ALU.mult
                                            ).then_inc(s("pool_step"), 1)
                    pool.wait_ge(s("pool_step"), own.next())
                    nc.gpsimd.tensor_tensor(rows[1][:, b, :, :], rows[1][:, b, :, :],
                                            modrow[k][:, b:b + 1, 1, :].to_broadcast([P, 2, D]), ALU.add
                                            ).then_inc(s(f"f{k}_h2"), 1)

            sublayer_rows(0)

            def experts(k, rows):
                pool.wait_ge(s("zeros_out"), 64)
                pool.wait_ge(s(f"f{k}_pos"), 1)
                for t in range(NT):
                    if k == 0:
                        pool.wait_ge(s("lnf_xn"), t + 1)
                    nc.gpsimd.indirect_dma_start(
                        out=xs_d[k], out_offset=bass.IndirectOffsetOnAxis(ap=posi[:, t:t + 1], axis=0),
                        in_=rows[:, t * P:(t + 1) * P], in_offset=None).then_inc(s(f"f{k}_xs_out"), 16)
                if k == 0:
                    gates(1)
                for m in range(NB):
                    pool.wait_ge(s(f"ys_out{m}"), 16 * (k + 1) * (MT // NB) + CREDIT)
                if k == 0:
                    pool.wait_ge(s("m1_ps"), B)
                for t in range(NT):
                    nc.gpsimd.indirect_dma_start(
                        out=yall[:, t * P:(t + 1) * P], out_offset=None, in_=ys_d[k],
                        in_offset=bass.IndirectOffsetOnAxis(ap=posi[:, t:t + 1], axis=0)
                        ).then_inc(s(f"y_in{t // GT}"), 16)

            experts(0, xn)

            def clear_vz(m):
                nc.gpsimd.memset(vz[m].rearrange("p k j c -> p (k j c)"), 0.0).then_inc(s("pool_step"), 1)
                pool.wait_ge(s("pool_step"), own.next())
                for j in range(HD):
                    nc.gpsimd.memset(vz[m][:, :, j, P // 2 + j * HD:P // 2 + (j + 1) * HD], 1.0)

            def spread_v(b, m):
                for j in range(HD):
                    last = nc.gpsimd.tensor_copy(
                        vz[m][:, :, j, j * HD:(j + 1) * HD],
                        vsb[:, ds(b * 2, 2), :].rearrange("p k (g j d) -> p (k g) j d", g=2, j=HD)[:, :, j, :])
                last.then_inc(s("vz"), 1)

            for n in range(2 * NC):
                j = n % 4
                pool.wait_ge(s("mid"), n + 1)
                nc.gpsimd.tensor_tensor(parts[j][:, 2, :], qr[n % 2], parts[j][:, 1, :], ALU.subtract).then_inc(s("parts"), 1)
                if n == 1:
                    clear_vz(0)
                if n == 3:
                    pool.wait_ge(s("x_f0"), NC)
                    clear_vz(1)
                if n == 5:
                    pool.wait_ge(s("v"), 1)
                    spread_v(0, 0)
            spread_v(1, 1)
            pool.wait_ge(s("v"), NC)
            with pool.Fori(0, (B - 2) // 2) as i:
                for m in range(2):
                    b = i * 2 + (2 + m)
                    pool.wait_ge(s("pv"), (b - 1) * H + CREDIT)
                    apart(pool)
                    spread_v(b, m)

            sublayer_rows(1)
            pool.wait_ge(s("f1_h2"), B)
            experts(1, h2)

        @block.scalar
        def _(act):
            give_credit(act, CREDITED["Activation"])
            own = Steps()
            act.wait_ge(s("mod_in"), 16 * len(MOD_LOADS))

            def ln_std(key):
                act.wait_ge(s(f"{key}_mv"), NT)
                nc.scalar.activation(std[:, :], meanvar[:, 1::2], ACT.Sqrt, bias=epst[:, 0:1]).then_inc(s(f"{key}_std"), 1)

            def modulate(key, k, b, bank=0):
                act.wait_ge(s(f"{key}_xT"), b + 1)
                nc.scalar.activation(hT[:, b, :], pb[bank + b % 2][:, 0:L], ACT.Identity, scale=modT[:, k, 1, b:b + 1],
                                     bias=modT[:, k, 0, b:b + 1]).then_inc(s(f"{key}_hT"), 1)

            def mod_rows(k, rows=range(B)):
                for b in rows:
                    act.wait_ge(s(f"m{k}_ps"), b + 1)
                    nc.scalar.activation(modrow[k][:, b, :, :].rearrange("p k d -> p (k d)"), pb[2 + b % 2][:, :],
                                         ACT.Copy).then_inc(s(f"m{k}_cp"), 1)

            nc.scalar.activation(silc[:, :], cT[:, :], ACT.Silu).then_inc(s("silc"), 1)
            act.wait_ge(s("consts"), CONSTS)
            ln_std("ln0")
            act.wait_ge(s("modT"), 2)
            nc.scalar.preload_act_table(ACT.Silu)

            act.wait_ge(s("inproj_in"), 16 * len(IN_LOADS))

            def silu_xi(c):
                for h in range(2):
                    act.wait_ge(s("conv"), 2 * c + h + 1)
                    nc.scalar.activation(xi[:, h, ts(c, CH)], xi[:, h, ts(c, CH)], ACT.Silu, bias=convb[:, h:h + 1]
                                         ).then_inc(s("xi"), 1)

            for c in range(NC):
                for b in range(0 if c == 0 else 2 * c + 2, min(2 * c + 4, B)):
                    modulate("ln0", 0, b)
                for h in range(2):
                    act.wait_ge(s("inproj"), c * 4 + h + 1)
                    if c >= 2:
                        act.wait_ge(s("conv"), 2 * (c - 2) + h + 1)
                    nc.scalar.activation(xraw[c % 2][h][:, :, PAD:PAD + L], pb[2 + h][:, :].rearrange("p (b l) -> p b l", b=2),
                                         ACT.Copy).then_inc(s("raw"), 1)
                for h in range(2):
                    act.wait_ge(s("inproj"), c * 4 + h + 3)
                    nc.scalar.activation(gres[:, h, ts(c, CH)], pb[4 + h][:, :], ACT.Silu).then_inc(s("gres"), 1)
                if c:
                    silu_xi(c - 1)

            act.wait_ge(s("w_in"), ALL_W)
            act.wait_ge(s("late_consts"), LATE_CONSTS)

            def exp_neg(c):
                act.wait_ge(s("neg"), c + 1)
                nc.scalar.activation(u[:, :, ts(c, CH)], u[:, :, ts(c, CH)], ACT.Exp).then_inc(s("spe"), 1)

            def softplus_ln(chunks):
                nc.scalar.preload_act_table(ACT.Ln)
                for c in chunks:
                    act.wait_ge(s("spe"), c + 1)
                    nc.scalar.activation(u[:, :, ts(c, CH)], u[:, :, ts(c, CH)], ACT.Ln, bias=1.0).then_inc(s("spl"), 1)

            for c in range(NC):
                act.wait_ge(s("draw"), c + 1)
                if c >= 2:
                    act.wait_ge(s("dtp"), 2 * (c - 1))
                nc.scalar.activation(drs[c % 2], pb[6 + c % 2][0:DTR, :], ACT.Copy).then_inc(s("drs"), 1)
                nc.scalar.activation(bc[64:96, ts(c, CH)], pb[6 + c % 2][64:96, :], ACT.Copy).then_inc(s("bc0"), 1)
                mod_rows(0, (2 * c, 2 * c + 1))
                for h in range(2):
                    act.wait_ge(s("dtp"), 2 * c + h + 1)
                    nc.scalar.activation(delta[:, c, h, :], pb[h][:, :], ACT.Identity, bias=dtb[:, h:h + 1]).then_inc(s("pre"), 1)
                if c == 0:
                    silu_xi(NC - 1)
                elif c < NC - 1:
                    exp_neg(c - 1)
                else:
                    softplus_ln(range(NC - 2))
                    nc.scalar.preload_act_table(ACT.Exp)
            exp_neg(NC - 2)
            exp_neg(NC - 1)
            nc.scalar.activation(aneg[:, :], alog[:, :], ACT.Exp).then_inc(s("act_step"), 1)
            act.wait_ge(s("act_step"), own.next())
            nc.scalar.mul(aneg[:, :], aneg[:, :], -1.0).then_inc(s("aneg"), 1)
            softplus_ln(range(NC - 2, NC))
            nc.scalar.preload_act_table(ACT.Exp)
            for c in range(NC):
                for h in range(2):
                    act.wait_ge(s("adjp"), 2 * c + h + 1)
                    nc.scalar.activation(dlt[:, h, ts(c, CH)], pb[4 - 2 * (c % 2) + h][:, :], ACT.Copy).then_inc(s("dlt"), 1)

            act.wait_ge(s("aneg"), 1)
            act.wait_ge(s("gates"), 1)
            act.wait_ge(s("dlt"), 2 * NC)
            with act.Fori(0, NC) as c:
                for n in range(NS):
                    act.wait_ge(s("bbp"), c * NS + (n + 1))
                    act.wait_ge(s("dBu"), c * NS + (n - 3 + CREDIT))
                    nc.scalar.activation(bsb[n % 4], pb[n % 2][:, :], ACT.Copy).then_inc(s("bsb"), 1)
                    for h in range(2):
                        act.wait_ge(s("scan"), c * NS + (n - 3 + CREDIT))
                        apart(act)
                        nc.scalar.activation(
                            dA[n % 4][:, h, :, 1:L], dlt[:, h, ts(c, CH)].rearrange("p (b l) -> p b l", b=2)[:, :, 1:L],
                            ACT.Exp, scale=aneg[:, h * NS + n:h * NS + n + 1]).then_inc(s("dA"), 1)

            def router(k):
                for b in range(B):
                    act.wait_ge(s(f"f{k}_h2Tp"), b + 1)
                    nc.scalar.activation(h2T[:, b * L:(b + 1) * L], pb[b % 2][:, 0:L], ACT.Identity,
                                         scale=modT[:, k, 3, b:b + 1], bias=modT[:, k, 2, b:b + 1]).then_inc(s(f"f{k}_h2T"), 1)

            def experts(k, func):
                nc.scalar.preload_act_table(func)
                def tile(i, m, first):
                    t = i * NB + m
                    if not first:
                        act.wait_ge(s(f"f{k}_yp"), t - NB + 1 + CREDIT)
                    act.wait_ge(s(f"tile_in{m}"), i * 32 + (32 + 32 * k * (MT // NB)))
                    for f in range(FC):
                        act.wait_ge(s(f"f{k}_hid"), t * 2 + f // 2 + 1)
                        nc.scalar.activation(h1[m][:, f, :], pb[1 + f // 2][:, (f % 2) * ET:(f % 2 + 1) * ET], func,
                                             bias=blob[m][:, O_B1 + f:O_B1 + f + 1]).then_inc(s(f"f{k}_h1"), 1)

                def store(t, m):
                    act.wait_ge(s(f"f{k}_ys"), t + 1 + CREDIT)
                    act.dma_start(ys_d[k][ds(t * ET, ET), :].rearrange("(q p) d -> p q d", p=P),
                                  ysb[m].rearrange("p (q d) -> p q d", d=D)).then_inc(s(f"ys_out{m}"), 16)

                for m in range(NB):
                    tile(0, m, True)
                    if m >= 3:
                        store(m - 3, m - 3)
                with act.Fori(1, MT // NB) as i:
                    for m in range(NB):
                        tile(i, m, False)
                        store(i * NB + (m - 3), (m - 3) % NB)
                store(MT - 3, NB - 3)
                store(MT - 2, NB - 2)
                store(MT - 1, NB - 1)

            ln_std("ln1")
            router(0)
            act.wait_ge(s("f0_nmax"), 1)
            nc.scalar.activation(m16[:, :], smax[:, :], ACT.Exp, scale=-1.0).then_inc(s("f0_e"), 1)
            nc.scalar.preload_act_table(ACT.Sqrt)
            ln_std("lnf")
            mod_rows(1)
            experts(0, ACT.Relu)

            act.wait_ge(s("abs"), 1)

            def ln2_std(c):
                tiles = slice(c * GT, (c + 1) * GT)
                act.wait_ge(s("ln2_mv"), (c + 1) * GT)
                nc.scalar.activation(std[:, tiles], meanvar[:, 2 * c * GT + 1:2 * (c + 1) * GT:2], ACT.Sqrt, bias=epst[:, 0:1]
                                     ).then_inc(s("ln2_std"), 1)

            ln2_std(0)
            for c in range(NC):
                modulate("ln2", 1, 2 * c, bank=6)
                modulate("ln2", 1, 2 * c + 1, bank=6)
                if c + 1 < NC:
                    ln2_std(c + 1)
                for qk in range(2):
                    act.wait_ge(s("qkp"), 2 * c + qk + 1)
                    j = (2 * c + qk) % 4
                    if c >= 2:
                        act.wait_ge(s(f"parts_out{j}"), (48, 16)[qk])
                    nc.scalar.activation(parts[j][:, 0, :], pb[2 + qk][:, :], ACT.Identity, bias=ab[:, qk:qk + 1],
                                         scale=QSCALE if qk == 0 else 1.0)
                    if c:
                        act.wait_ge(s("mid"), 2 * (c - 1) + qk + 1)
                    nc.scalar.activation(qf[qk], pb[2 + qk][:, :], ACT.Identity, bias=ab[:, qk:qk + 1],
                                         scale=QSCALE if qk == 0 else 1.0).then_inc(s("qf"), 1)
            nc.scalar.preload_act_table(ACT.Exp)

            def attn(b, first):
                for h in range(H):
                    act.wait_ge(s("sT"), b * H + (h + 1 + CREDIT))
                    if not (first and h < 4):
                        act.wait_ge(s("pv"), b * H + (h - 3 + CREDIT))
                    nc.scalar.activation(pexp[h % 4], pb[2 + h % 2][:, :], ACT.Exp).then_inc(s("pT"), 1)

            act.wait_ge(s("parts_out2"), 96)
            act.wait_ge(s("parts_out3"), 32)
            attn(0, True)
            with act.Fori(0, (B - 2) // 2) as i:
                for m in range(2):
                    attn(i * 2 + (1 + m), False)
            attn(B - 1, False)

            ln_std("ln3")
            router(1)
            act.wait_ge(s("f1_nmax"), 1)
            nc.scalar.activation(rt[:, :, :], lgt[:, :, :], ACT.Exp).then_inc(s("f1_e"), 1)
            experts(1, ACT.Gelu)

        @block.vector
        def _(dve):
            give_credit(dve, CREDITED["DVE"])
            own = Steps()
            V = nc.vector

            def stats_of(key, src, last=None, first=0):
                if last is None:
                    for t in range(first, NT):
                        last = V.bn_stats(stats[:, 6 * t:6 * t + 6], src[:, t * P:(t + 1) * P])
                last.then_inc(s("dve_step"), 1)
                dve.wait_ge(s("dve_step"), own.next())
                for t in range(NT):
                    V.bn_aggr(meanvar[:, 2 * t:2 * t + 2], stats[:, 6 * t:6 * t + 6]).then_inc(s(f"{key}_mv"), 1)
                dve.wait_ge(s(f"{key}_std"), 1)
                V.reciprocal(rstd[:, :], std[:, :]).then_inc(s("dve_step"), 1)
                dve.wait_ge(s("dve_step"), own.next())

            def layernorm(key, src, dst, last=None, first=0):
                stats_of(key, src, last, first)
                for t in range(NT):
                    V.tensor_scalar(dst[:, t * P:(t + 1) * P], src[:, t * P:(t + 1) * P], meanvar[:, 2 * t:2 * t + 1],
                                    rstd[:, t:t + 1], ALU.subtract, ALU.mult).then_inc(s(f"{key}_xn"), 1)

            dve.wait_ge(s("consts"), CONSTS)
            dve.wait_ge(s("silc"), 1)
            for b in range(B):
                V.tensor_scalar(srep[0][:, b, :], ones_f[:, :], silc[:, b:b + 1], None, ALU.mult).then_inc(s("srep0"), 1)
            dve.wait_ge(s("modTp"), 1)
            turned = pb[5][:, 0:8 * B].rearrange("p (k m j b) -> p j (k m) b", k=2, m=2, j=2)
            for j in range(2):
                V.tensor_scalar(modT[:, :, :, :].rearrange("p k (m j) b -> p j (k m) b", j=2)[:, j, :, :], turned[:, j, :, :],
                                float(j), None, ALU.add).then_inc(s("modT"), 1)
            dve.wait_ge(s("x_in"), 16 * NC)
            layernorm("ln0", x, xn)
            dve.wait_ge(s("inproj_in"), 16 * len(IN_LOADS))

            def conv(c, h):
                acc = xi[:, h, ts(c, CH)].rearrange("p (b l) -> p b l", b=2)
                dve.wait_ge(s("raw"), 2 * c + h + 1)
                for tap in range(TAPS):
                    if tap == 0:
                        last = V.tensor_scalar(acc, xraw[c % 2][h][:, :, 0:L], convw[:, h, 0:1], None, ALU.mult)
                    else:
                        last.then_inc(s("dve_step"), 1)
                        dve.wait_ge(s("dve_step"), own.next())
                        last = V.scalar_tensor_tensor(acc, xraw[c % 2][h][:, :, tap:tap + L], convw[:, h, tap:tap + 1], acc,
                                                      ALU.mult, ALU.add)
                last.then_inc(s("conv"), 1)

            def bc_parts(c):
                t = ts(c, CH)
                rest, mid, src = bcr[c % 2], bmid[c % 2], pb[6 + c % 2][64:96, :]
                dve.wait_ge(s("bc0"), c + 1)
                V.tensor_tensor(rest, src, bc[64:96, t], ALU.subtract).then_inc(s("bc_read"), 1)
                dve.wait_ge(s("bc_read"), c + 1)
                V.tensor_copy(mid, rest).then_inc(s("dve_step"), 1)
                dve.wait_ge(s("dve_step"), own.next())
                V.tensor_copy(bc[96:128, t], mid)
                V.tensor_tensor(bc[0:32, t], rest, mid, ALU.subtract).then_inc(s("bc"), 1)

            def minus_abs(c):
                for h in range(2):
                    dve.wait_ge(s("pre"), 2 * c + h + 1)
                    last = V.scalar_tensor_tensor(u[:, h, ts(c, CH)], delta[:, c, h, :], -1.0, delta[:, c, h, :], ALU.mult, ALU.min)
                last.then_inc(s("neg"), 1)

            dve.wait_ge(s("inproj_in"), 16 * len(IN_LOADS))
            for c in range(NC):
                for h in range(2):
                    conv(c, h)
            dve.wait_ge(s("late_consts"), LATE_CONSTS)
            dve.wait_ge(s("zeros_out"), 64)
            for c in range(NC):
                bc_parts(c)
                minus_abs(c)
            for c in range(NC):
                dve.wait_ge(s("spl"), c + 1)
                V.scalar_tensor_tensor(delta[:, c, :, :], delta[:, c, :, :], 0.0, u[:, :, ts(c, CH)], ALU.max, ALU.add
                                       ).then_inc(s("delta"), 1)
            for c in range(NC):
                dve.wait_ge(s("dlt"), 2 * c + 2)
                dve.wait_ge(s("delta"), c + 1)
                V.tensor_tensor(u[:, :, ts(c, CH)], dlt[:, :, ts(c, CH)], xi[:, :, ts(c, CH)], ALU.mult).then_inc(s("u"), 1)

            dve.wait_ge(s("gates"), 1)
            def chunk(c, d):
                return ds(c * CH + d * CH, CH)

            def scan(c, d, n):
                done = NS * d + n
                dve.wait_ge(s("hc"), c * NS + (done - 3 + CREDIT))
                dve.wait_ge(s("dA"), c * 2 * NS + (2 * done + 2))
                dve.wait_ge(s("dBu"), c * NS + (done + 1 + CREDIT))
                V.tensor_tensor_scan(hs[n % 4].rearrange("p h t -> p (h t)"), dA[n % 4][:, :, :, :].rearrange("p h b l -> p (h b l)"),
                                     dBu[n % 4].rearrange("p h t -> p (h t)"), 0.0, ALU.mult, ALU.add).then_inc(s("scan"), 1)

            def times_c(c, d, n):
                done = NS * d + n
                dve.wait_ge(s("cbp"), c * NS + (done + 1))
                dve.wait_ge(s("hsum"), c * 2 * NS + (2 * done - 6 + CREDIT))
                dve.wait_ge(s("scan"), c * NS + (done + 1 + CREDIT))
                V.tensor_tensor(hc[n % 4], hs[n % 4], pb[2 + n % 2][:, :].unsqueeze(1).to_broadcast([P, 2, CH]), ALU.mult
                                ).then_inc(s("hc"), 1)

            def state(c, d, n, last_chunk=False):
                if n + 1 < NS:
                    scan(c, d, n + 1)
                elif not last_chunk:
                    scan(c, d + 1, 0)
                times_c(c, d, n)

            def gated(c, h):
                dve.wait_ge(s("outp"), c + CREDIT)
                dve.wait_ge(s("hsum"), c * 2 * NS + (2 * NS - 1 + h + CREDIT))
                V.tensor_tensor(yg[h], pb[4 + h][:, :], gres[:, h, chunk(c, 0)], ALU.mult).then_inc(s("yg"), 1)

            def add_mamba(c):
                dve.wait_ge(s("outp"), c + 1 + CREDIT)
                V.tensor_tensor(tmp[:, :].rearrange("p (b t d) -> p b t d", b=2, t=2),
                                pb[6][:, :].rearrange("p (b t d) -> p b t d", b=2, t=2),
                                modrow[0][:, ds(c * 2, 2), 0, :].unsqueeze(2).to_broadcast([P, 2, 2, D]), ALU.mult
                                ).then_inc(s("dve_step"), 1)
                dve.wait_ge(s("dve_step"), own.next())
                V.tensor_tensor(x[:, chunk(c, 0)], x[:, chunk(c, 0)], tmp[:, :], ALU.add).then_inc(s("x_a"), 1)

            for h in range(2):
                V.tensor_scalar(ddiag[:, h, :], ident[:, :], dskip[:, h:h + 1], None, ALU.mult).then_inc(s("ddiag"), 1)
            dve.wait_ge(s("gres"), 2 * NC)
            scan(0, 0, 0)
            for n in range(HEAD):
                state(0, 0, n)
            with dve.Fori(0, NC - 1) as c:
                own.loop(c, 1)
                for n in range(HEAD, NS):
                    state(c, 0, n)
                for n in range(HEAD):
                    state(c, 1, n)
                    if n == 1:
                        gated(c, 0)
                        gated(c, 1)
                add_mamba(c)
            own.end(NC - 1)
            for n in range(HEAD, NS):
                state(NC - 1, 0, n, last_chunk=True)
            gated(NC - 1, 0)
            gated(NC - 1, 1)
            add_mamba(NC - 1)

            def router(k):
                dve.wait_ge(s(f"f{k}_sc"), 1)
                sc = pb[7][:, 0:NT * E].rearrange("p (t e) -> p t e", e=E)
                if k:
                    V.tensor_tensor(lgt[:, :, :], sc, br[:, :].unsqueeze(1).to_broadcast([P, NT, E]), ALU.add).then_inc(s("dve_step"), 1)
                    dve.wait_ge(s("dve_step"), own.next())
                else:
                    V.tensor_copy(lgt[:, :, :], sc).then_inc(s("dve_step"), 1)
                    dve.wait_ge(s("dve_step"), own.next())
                V.tensor_reduce(smax[:, :], lgt[:, :, :], AX.X, ALU.max).then_inc(s("dve_step"), 1)
                dve.wait_ge(s("dve_step"), own.next())
                mbc = smax[:, :].unsqueeze(2).to_broadcast([P, NT, E])
                V.tensor_tensor(oh[:, :, :], lgt[:, :, :], mbc, ALU.is_ge).then_inc(s("dve_step"), 1)
                dve.wait_ge(s("dve_step"), own.next())
                V.tensor_tensor(oh[:, :, :], oh[:, :, :], down[:, :].unsqueeze(1).to_broadcast([P, NT, E]), ALU.mult).then_inc(s("dve_step"), 1)
                dve.wait_ge(s("dve_step"), own.next())
                if k:
                    V.tensor_tensor(lgt[:, :, :], lgt[:, :, :], mbc, ALU.subtract).then_inc(s("f1_nmax"), 1)
                else:
                    dve.sem_inc(s("f0_nmax"), 1)
                V.tensor_reduce(posf[:, :], oh[:, :, :], AX.X, ALU.max).then_inc(s("dve_step"), 1)
                dve.wait_ge(s("dve_step"), own.next())
                V.tensor_tensor(oh[:, :, :], oh[:, :, :], posf[:, :].unsqueeze(2).to_broadcast([P, NT, E]), ALU.is_equal).then_inc(s("dve_step"), 1)
                dve.wait_ge(s("dve_step"), own.next())
                V.tensor_copy(ohb[:, :], oh[:, :, :].rearrange("p t e -> p (t e)")).then_inc(s(f"f{k}_oh"), 1)
                dve.wait_ge(s(f"f{k}_e"), 1)
                if k:
                    V.tensor_reduce(m16[:, :], rt[:, :, :], AX.X, ALU.add).then_inc(s("dve_step"), 1)
                    dve.wait_ge(s("dve_step"), own.next())
                else:
                    V.tensor_scalar(m16[:, :], m16[:, :], 1.0, None, ALU.add).then_inc(s("dve_step"), 1)
                    dve.wait_ge(s("dve_step"), own.next())
                V.reciprocal(wgt[:, :], m16[:, :]).then_inc(s("dve_step"), 1)
                dve.wait_ge(s("dve_step"), own.next())
                dve.wait_ge(s(f"f{k}_rank"), 2)
                V.tensor_copy(et[:, :, :], pb[6][:, 0:NT * E].rearrange("p (t e) -> p e t", e=E)).then_inc(s("dve_step"), 1)
                dve.wait_ge(s("dve_step"), own.next())
                flat = lambda v: v[:, :, :].rearrange("p e t -> p (e t)")
                V.tensor_tensor_scan(flat(incl), flat(seg), flat(et), 0.0, ALU.mult, ALU.add).then_inc(s("dve_step"), 1)
                dve.wait_ge(s("dve_step"), own.next())
                kk = kcmp[:, 0:T // ET, :].rearrange("p k e -> p e k")
                V.tensor_scalar(exf[:, :], kth[:, :], float(ET), None, ALU.mult).then_inc(s("dve_step"), 1)
                dve.wait_ge(s("dve_step"), own.next())
                V.tensor_tensor(kk, incl[:, :, NT - 1:NT].to_broadcast([P, E, T // ET]),
                                exf[:, 0:T // ET].unsqueeze(1).to_broadcast([P, E, T // ET]), ALU.is_gt).then_inc(s("dve_step"), 1)
                dve.wait_ge(s("dve_step"), own.next())
                V.tensor_reduce(ntile[:, :], kk, AX.X, ALU.add).then_inc(s("dve_step"), 1)
                dve.wait_ge(s("dve_step"), own.next())
                V.tensor_tensor_scan(tend[:, :], ones_f[:, 0:E], ntile[:, :], 0.0, ALU.mult, ALU.add).then_inc(s("dve_step"), 1)
                dve.wait_ge(s("dve_step"), own.next())
                V.tensor_tensor(kcmp[:, :, :], kth[:, :].unsqueeze(2).to_broadcast([P, MT, E]),
                                tend[:, :].unsqueeze(1).to_broadcast([P, MT, E]), ALU.is_ge).then_inc(s("dve_step"), 1)
                dve.wait_ge(s("dve_step"), own.next())
                V.tensor_reduce(exf[:, :], kcmp[:, :, :], AX.X, ALU.add).then_inc(s("dve_step"), 1)
                dve.wait_ge(s("dve_step"), own.next())
                V.tensor_scalar(exi[:, :], exf[:, :], float(E - 1), None, ALU.min).then_inc(s(f"f{k}_tiles"), 1)
                V.tensor_tensor(tbeg[:, :], tend[:, :], ntile[:, :], ALU.subtract).then_inc(s("dve_step"), 1)
                dve.wait_ge(s("dve_step"), own.next())
                V.tensor_tensor(flat(incl), flat(incl), flat(et), ALU.subtract).then_inc(s("dve_step"), 1)
                dve.wait_ge(s("dve_step"), own.next())
                V.scalar_tensor_tensor(incl[:, :, :], tbeg[:, :].unsqueeze(2).to_broadcast([P, E, NT]), float(ET),
                                       incl[:, :, :], ALU.mult, ALU.add).then_inc(s("dve_step"), 1)
                dve.wait_ge(s("dve_step"), own.next())
                V.tensor_tensor(rt[:, :, :], incl[:, :, :].rearrange("p e t -> p t e"),
                                pb[5][:, 0:NT * E].rearrange("p (t e) -> p t e", e=E), ALU.add).then_inc(s("dve_step"), 1)
                dve.wait_ge(s("dve_step"), own.next())
                V.tensor_tensor(rt[:, :, :], rt[:, :, :], oh[:, :, :], ALU.mult).then_inc(s("dve_step"), 1)
                dve.wait_ge(s("dve_step"), own.next())
                V.tensor_reduce(posf[:, :], rt[:, :, :], AX.X, ALU.add).then_inc(s("dve_step"), 1)
                dve.wait_ge(s("dve_step"), own.next())
                V.tensor_copy(posi[:, :], posf[:, :]).then_inc(s(f"f{k}_pos"), 1)

            def experts(k):
                def rows_T(i, m):
                    t = i * NB + m
                    dve.wait_ge(s(f"tile_in{m}"), i * 32 + (32 + 32 * k * (MT // NB)))
                    dve.wait_ge(s(f"f{k}_xTp"), t + 1)
                    if k:
                        V.tensor_copy(xtT[m], pb[0][:, 0:ET]).then_inc(s(f"f{k}_xtT"), 1)
                    else:
                        V.tensor_scalar(xtT[m], pb[0][:, 0:ET], blob[m][:, O_GB:O_GB + 1], blob[m][:, O_GB + 1:O_GB + 2],
                                        ALU.mult, ALU.add).then_inc(s(f"f{k}_xtT"), 1)

                def plus_b2(t, m):
                    dve.wait_ge(s(f"f{k}_yp"), t + 1 + CREDIT)
                    V.tensor_scalar(ytT[m], pb[3][:, 0:ET], blob[m][:, O_B2:O_B2 + 1], None, ALU.add
                                    ).then_inc(s(f"f{k}_ytT"), 1)

                def rows_out(t, m, stored):
                    dve.wait_ge(s(f"f{k}_yb"), t + 1)
                    if stored is not None:
                        dve.wait_ge(s(f"ys_out{m}"), stored * 16 + 16 * k * (MT // NB) + CREDIT)
                    V.tensor_copy(ysb[m], pb[4][:, 0:ET]).then_inc(s(f"f{k}_ys"), 1)

                for m in range(NB):
                    rows_T(0, m)
                    if m >= 2:
                        plus_b2(m - 2, m - 2)
                    if m >= 3:
                        rows_out(m - 3, m - 3, None)
                with dve.Fori(1, MT // NB) as i:
                    for m in range(NB):
                        rows_T(i, m)
                        plus_b2(i * NB + (m - 2), (m - 2) % NB)
                        rows_out(i * NB + (m - 3), (m - 3) % NB, i if m >= 3 else i - 1)
                plus_b2(MT - 2, NB - 2)
                rows_out(MT - 3, NB - 3, MT // NB - 1)
                plus_b2(MT - 1, NB - 1)
                rows_out(MT - 2, NB - 2, MT // NB - 1)
                rows_out(MT - 1, NB - 1, MT // NB - 1)

            def gate_rows(k):
                for t in range(NT):
                    last = V.tensor_scalar(ygate[:, t * P:(t + 1) * P], modrow[k][:, t // 2, 3, :], wgt[:, t:t + 1], None, ALU.mult)
                last.then_inc(s("dve_step"), 1)
                dve.wait_ge(s("dve_step"), own.next())
                if k == 0:
                    for c in range(NC):
                        t = ts(c, CH)
                        V.tensor_tensor(tmp[:, :].rearrange("p (b t d) -> p b t d", b=2, t=2),
                                        h2[:, t].rearrange("p (b t d) -> p b t d", b=2, t=2),
                                        modrow[0][:, 2 * c:2 * c + 2, 3, :].unsqueeze(2).to_broadcast([P, 2, 2, D]), ALU.mult
                                        ).then_inc(s("dve_step"), 1)
                        dve.wait_ge(s("dve_step"), own.next())
                        V.tensor_tensor(x[:, t], x[:, t], tmp[:, :], ALU.add).then_inc(s("dve_step"), 1)
                        dve.wait_ge(s("dve_step"), own.next())

            def combine(k, c):
                t = ts(c, CH)
                dve.wait_ge(s(f"y_in{c}"), 16 * GT * (k + 1))
                V.tensor_tensor(yall[:, t], yall[:, t], ygate[:, t], ALU.mult).then_inc(s("dve_step"), 1)
                dve.wait_ge(s("dve_step"), own.next())
                V.tensor_tensor(x[:, t], x[:, t], yall[:, t], ALU.add).then_inc(s("x_final" if k else "x_f0"), 1)

            dve.wait_ge(s("x_a"), NC + CREDIT)
            layernorm("ln1", x, xn)
            EARLY = 10
            for t in range(EARLY):
                dve.wait_ge(s("f0_h2"), t // 2 + 1)
                V.bn_stats(stats[:, 6 * t:6 * t + 6], h2[:, t * P:(t + 1) * P])
            router(0)
            dve.wait_ge(s("f0_h2"), B)
            dve.wait_ge(s("f0_h2Tp"), B)
            layernorm("lnf", h2, xn, first=EARLY)
            gate_rows(0)
            experts(0)

            V.tensor_scalar(ab[:, 0:1], ab[:, 0:1], QSCALE, None, ALU.mult).then_inc(s("abs"), 1)

            def ln2(c):
                tiles = range(c * GT, (c + 1) * GT)
                dve.wait_ge(s("x_f0"), c + 1)
                for t in tiles:
                    last = V.bn_stats(stats[:, 6 * t:6 * t + 6], x[:, t * P:(t + 1) * P])
                last.then_inc(s("dve_step"), 1)
                dve.wait_ge(s("dve_step"), own.next())
                for t in tiles:
                    V.bn_aggr(meanvar[:, 2 * t:2 * t + 2], stats[:, 6 * t:6 * t + 6]).then_inc(s("ln2_mv"), 1)
                dve.wait_ge(s("ln2_std"), c + 1)
                V.reciprocal(rstd[:, c * GT:(c + 1) * GT], std[:, c * GT:(c + 1) * GT]).then_inc(s("dve_step"), 1)
                dve.wait_ge(s("dve_step"), own.next())
                for t in tiles:
                    V.tensor_scalar(xn[:, t * P:(t + 1) * P], x[:, t * P:(t + 1) * P], meanvar[:, 2 * t:2 * t + 1],
                                    rstd[:, t:t + 1], ALU.subtract, ALU.mult).then_inc(s("ln2_xn"), 1)

            def qkv_parts(c):
                for qk in range(2):
                    j = (2 * c + qk) % 4
                    dve.wait_ge(s("qf"), 2 * c + qk + 1)
                    if c:
                        dve.wait_ge(s("parts"), 2 * (c - 1) + qk + 1)
                    V.tensor_tensor(qr[qk], qf[qk], parts[j][:, 0, :], ALU.subtract).then_inc(s("dve_step"), 1)
                    dve.wait_ge(s("dve_step"), own.next())
                    V.tensor_copy(parts[j][:, 1, :], qr[qk]).then_inc(s("mid"), 1)
                dve.wait_ge(s("vp"), c + 1)
                V.tensor_tensor(vsb[:, 4 * c:4 * c + 4, :], pb[4 + c % 2][:, :].rearrange("p (t d) -> p t d", d=D),
                                arow[:, 0:1, :].to_broadcast([P, 4, D]), ALU.add).then_inc(s("v"), 1)

            def max_head(b, h):
                dve.wait_ge(s("maxp"), b * H + (h + 1))
                V.tensor_reduce(mx[:, 2 * h:2 * h + 2], pb[h % 2][:, :].rearrange("p (q l) -> p q l", q=2), AX.X, ALU.max
                                ).then_inc(s("mx"), 1)

            def max_rows(b):
                dve.wait_ge(s("mx"), b * H + H + CREDIT)
                V.tensor_scalar(mneg, mx, -1.0, None, ALU.mult).then_inc(s("mneg"), 1)
                dve.wait_ge(s("mT"), b + 1)
                dve.wait_ge(s("max_in"), b * 32)
                V.tensor_copy(mpart[:, 0:P], pb[7][0:2 * H, 0:P]).then_inc(s("dve_step"), 1)
                dve.wait_ge(s("dve_step"), own.next())
                V.tensor_tensor(mpart[:, P:2 * P], pb[7][0:2 * H, 0:P], mpart[:, 0:P], ALU.subtract).then_inc(s("mparts"), 1)

            def normalise(b, g):
                dve.wait_ge(s("pv"), b * H + (g + 1) * H // 2 + CREDIT)
                V.reciprocal(rden[g], pb[4 + g][P // 2:P, 0:L]).then_inc(s("dve_step"), 1)
                dve.wait_ge(s("dve_step"), own.next())
                if g == 0:
                    dve.wait_ge(s("aop"), b + CREDIT)
                V.tensor_tensor(oT[g * P // 2:(g + 1) * P // 2, :], pb[4 + g][0:P // 2, 0:L], rden[g], ALU.mult
                                ).then_inc(s("nrm"), 1)

            def residual(b):
                dve.wait_ge(s("aop"), b + 1 + CREDIT)
                for q in range(2):
                    last = V.tensor_tensor(osum[:, q * D:(q + 1) * D], pb[6][:, q * D:(q + 1) * D], arow[:, 1, :], ALU.add)
                last.then_inc(s("dve_step"), 1)
                dve.wait_ge(s("dve_step"), own.next())
                for q in range(2):
                    last = V.tensor_tensor(osum[:, q * D:(q + 1) * D], osum[:, q * D:(q + 1) * D],
                                           modrow[1][:, ds(b, 1), 0, :].rearrange("p a d -> p (a d)"), ALU.mult)
                last.then_inc(s("dve_step"), 1)
                dve.wait_ge(s("dve_step"), own.next())
                V.tensor_tensor(x[:, ds(b * L, L)], x[:, ds(b * L, L)], osum, ALU.add).then_inc(s("x_b"), 1)

            def attn(b, first, last_b):
                if not first:
                    normalise(b - 1, 1)
                    residual(b - 1)
                for h in range(H):
                    if not last_b:
                        max_head(b + 1, h)
                if not last_b:
                    max_rows(b + 1)
                normalise(b, 0)

            for c in range(NC):
                combine(0, c)
                ln2(c)
                if c:
                    qkv_parts(c - 1)
            for h in range(H):
                if h == 4:
                    qkv_parts(NC - 1)
                max_head(0, h)
            dve.wait_ge(s("parts_out0"), 96)
            dve.wait_ge(s("parts_out1"), 32)
            max_rows(0)
            attn(0, True, False)
            with dve.Fori(0, (B - 2) // 2) as i:
                own.loop(i, 10)
                for m in range(2):
                    attn(i * 2 + (1 + m), False, False)
            own.end((B - 2) // 2)
            attn(B - 1, False, True)
            normalise(B - 1, 1)
            residual(B - 1)

            dve.wait_ge(s("x_b"), B + CREDIT)
            layernorm("ln3", x, xn)
            router(1)
            gate_rows(1)
            experts(1)
            for c in range(NC):
                combine(1, c)

        @block.tensor
        def _(pe):
            give_credit(pe, CREDITED["PE"])
            mm = nc.tensor.matmul

            def mod_rows(k, rows=range(B)):
                for b in rows:
                    pe.wait_ge(s(f"srep{k}"), b + 1)
                    if b >= 2:
                        pe.wait_ge(s(f"m{k}_cp"), b - 1)
                    mm(pb[2 + b % 2][:, :], srep[k][:, b, :], wmod[:, k, 2 * D:6 * D], start=True, stop=True).then_inc(s(f"m{k}_ps"), 1)

            def transpose_pair(b, ready, src, done, used, bank=0):
                pe.wait_ge(s(ready), (b + 1) * (2 if ready.startswith("ln") else 1))
                if b >= 2:
                    pe.wait_ge(s(used), b - 1 + CREDIT)
                for t in range(2):
                    last = nc.tensor.transpose(pb[bank + b % 2][:, t * P:(t + 1) * P], src[:, b * L + t * P:b * L + (t + 1) * P], ident[:, :])
                last.then_inc(s(done), 1)

            pe.wait_ge(s("mod_in"), 16 * len(MOD_LOADS))
            pe.wait_ge(s("consts"), CONSTS)
            pe.wait_ge(s("silc"), 1)
            for k in range(2):
                for n, j in enumerate((0, 1, 3, 4)):
                    col = (4 * k + n) * B
                    last = mm(pb[5][:, col:col + B], wmod[:, k, j * D:(j + 1) * D], silc[:, k * B:(k + 1) * B], start=True, stop=True)
            last.then_inc(s("modTp"), 1)

            pe.wait_ge(s("inproj_in"), 16 * len(IN_LOADS))
            pe.wait_ge(s("modT"), 2)
            for c in range(NC):
                for b in range(0 if c == 0 else 2 * c + 2, min(2 * c + 4, B)):
                    transpose_pair(b, "ln0_xn", xn, "ln0_xT", "ln0_hT")
                pe.wait_ge(s("ln0_hT"), 2 * c + 2 + CREDIT)
                for h in range(4):
                    if c:
                        pe.wait_ge(s("raw" if h < 2 else "gres"), 2 * (c - 1) + h % 2 + 1)
                    mm(pb[2 + h][:, :], inw[:, h * P:(h + 1) * P], hT[:, 2 * c:2 * c + 2, :],
                       start=True, stop=True).then_inc(s("inproj"), 1)

            pe.wait_ge(s("w_in"), ALL_W)
            pe.wait_ge(s("late_consts"), LATE_CONSTS)
            pe.wait_ge(s("raw"), 2 * NC)
            pe.wait_ge(s("gres"), 2 * NC)
            for c in range(NC):
                t = ts(c, CH)
                pe.wait_ge(s("xi"), 2 * c + 2)
                if c >= 2:
                    pe.wait_ge(s("drs"), c - 1)
                    pe.wait_ge(s("bc_read"), c - 1)
                for h in range(2):
                    last = mm(pb[6 + c % 2][0:96, :], xpw[:, h, :], xi[:, h, t], start=(h == 0), stop=(h == 1))
                last.then_inc(s("draw"), 1)
                mod_rows(0, (2 * c, 2 * c + 1))
                pe.wait_ge(s("drs"), c + 1)
                for h in range(2):
                    if c:
                        pe.wait_ge(s("pre"), 2 * (c - 1) + h + 1)
                    mm(pb[h][:, :], dtw[:, h * P:(h + 1) * P], drs[c % 2], start=True, stop=True).then_inc(s("dtp"), 1)
            for c in range(NC):
                if c == 1:
                    pe.wait_ge(s("m0_cp"), B)
                pe.wait_ge(s("delta"), c + 1)
                for h in range(2):
                    if c >= 2:
                        pe.wait_ge(s("dlt"), 2 * (c - 2) + h + 1)
                    for g in range(2):
                        last = mm(pb[4 - 2 * (c % 2) + h][:, :], adj[:, g, h * P:(h + 1) * P], delta[:, c, g, :],
                                  start=(g == 0), stop=(g == 1))
                    last.then_inc(s("adjp"), 1)

            pe.wait_ge(s("ddiag"), 2)
            pe.wait_ge(s("bc"), NC)
            pe.wait_ge(s("dlt"), 2 * NC)
            def chunk(c, d):
                return ds(c * CH + d * CH, CH)

            def b_row(c, d, n):
                pe.wait_ge(s("bsb"), c * NS + (NS * d + n - 1 + CREDIT))
                mm(pb[n % 2][:, :], pick[:, n, :], bc[:, chunk(c, d)], start=True, stop=True).then_inc(s("bbp"), 1)

            def c_row(c, d, n):
                pe.wait_ge(s("hc"), c * NS + (NS * d + n - 1 + CREDIT))
                mm(pb[2 + n % 2][:, :], pick[:, NS + n, :], bc[:, chunk(c, d)], start=True, stop=True).then_inc(s("cbp"), 1)

            def sum_state(c, d, n):
                if n == 0:
                    pe.wait_ge(s("yg"), c * 2 + 2 * d + CREDIT)
                pe.wait_ge(s("hc"), c * NS + (NS * d + n + 1 + CREDIT))
                for h in range(2):
                    if n == 0:
                        mm(pb[4 + h][:, :], ddiag[:, h, :], xi[:, h, chunk(c, d)], start=True, stop=False)
                    mm(pb[4 + h][:, :], ident[:, :], hc[n % 4][:, h, :], start=False, stop=(n == NS - 1)).then_inc(s("hsum"), 1)

            def state(c, d, n, last_chunk=False):
                if n + LEAD < NS:
                    b_row(c, d, n + LEAD)
                elif not last_chunk:
                    b_row(c, d + 1, n + LEAD - NS)
                if n + 1 < NS:
                    c_row(c, d, n + 1)
                elif not last_chunk:
                    c_row(c, d + 1, 0)
                if n >= 2:
                    sum_state(c, d, n - 2)
                elif d:
                    sum_state(c, 0, NS - 2 + n)

            def out_proj(c, tiles):
                if 0 in tiles:
                    pe.wait_ge(s("yg"), c * 2 + 2 + CREDIT)
                    pe.wait_ge(s("x_a"), c + CREDIT)
                for q in tiles:
                    for h in range(2):
                        last = mm(pb[6][:, q * P:(q + 1) * P], yg[h][:, q * P:(q + 1) * P], outw[:, h, :],
                                  start=(h == 0), stop=(h == 1))
                if CH // P - 1 in tiles:
                    last.then_inc(s("outp"), 1)

            for n in range(LEAD):
                b_row(0, 0, n)
            c_row(0, 0, 0)
            for n in range(HEAD):
                state(0, 0, n)
            with pe.Fori(0, NC - 1) as c:
                for n in range(HEAD, NS):
                    state(c, 0, n)
                for n in range(HEAD):
                    state(c, 1, n)
                    if n in (3, 4):
                        out_proj(c, (2 * n - 6, 2 * n - 5))
            for n in range(HEAD, NS):
                state(NC - 1, 0, n, last_chunk=True)
            sum_state(NC - 1, 0, NS - 2)
            sum_state(NC - 1, 0, NS - 1)
            out_proj(NC - 1, range(CH // P))

            def router(k):
                for b in range(B + 1):
                    if b < B:
                        transpose_pair(b, ("ln1_xn", "ln3_xn")[k], xn, f"f{k}_h2Tp", f"f{k}_h2T")
                    if b:
                        pe.wait_ge(s(f"f{k}_h2T"), b + CREDIT)
                        for t in (2 * b - 2, 2 * b - 1):
                            last = mm(pb[7][:, t * E:(t + 1) * E], h2T[:, t * P:(t + 1) * P], cent[:, k, :], start=True, stop=True)
                last.then_inc(s(f"f{k}_sc"), 1)
                pe.wait_ge(s(f"f{k}_oh"), 1)
                mm(pb[5][:, 0:NT * E], tri[:, :], ohb[:, :], start=True, stop=True).then_inc(s(f"f{k}_rank"), 1)
                mm(pb[6][:, 0:NT * E], ones_b[:, :], ohb[:, :], start=True, stop=True).then_inc(s(f"f{k}_rank"), 1)

            def experts(k):
                pe.wait_ge(s(f"f{k}_pos"), 1)

                def turn(i, m):
                    t = i * NB + m
                    pe.wait_ge(s(f"tile_in{m}"), i * 32 + (32 + 32 * k * (MT // NB)))
                    for q in range(2):
                        last = nc.tensor.transpose(pb[0][:, q * P:(q + 1) * P], xt[m][:, q * P:(q + 1) * P], ident[:, :])
                    last.then_inc(s(f"f{k}_xTp"), 1)

                def up(i, m):
                    t = i * NB + m
                    pe.wait_ge(s(f"f{k}_xtT"), t + 1)
                    for g in range(2):
                        pe.wait_ge(s(f"f{k}_h1"), t * FC + (2 * g - 2 + CREDIT))
                        for f in range(2):
                            last = mm(pb[1 + g][:, f * ET:(f + 1) * ET], blob[m][:, (2 * g + f) * P:(2 * g + f + 1) * P], xtT[m],
                                      start=True, stop=True)
                        last.then_inc(s(f"f{k}_hid"), 1)

                def down_(t, m):
                    pe.wait_ge(s(f"f{k}_h1"), t * FC + FC + CREDIT)
                    pe.wait_ge(s(f"f{k}_ytT"), t + CREDIT)
                    for f in range(FC):
                        last = mm(pb[3][:, 0:ET], blob[m][:, O_W2 + f * P:O_W2 + (f + 1) * P], h1[m][:, f, :],
                                  start=(f == 0), stop=(f == FC - 1))
                    last.then_inc(s(f"f{k}_yp"), 1)

                def back(t, m):
                    pe.wait_ge(s(f"f{k}_ytT"), t + 1 + CREDIT)
                    pe.wait_ge(s(f"f{k}_ys"), t + CREDIT)
                    for q in range(2):
                        last = nc.tensor.transpose(pb[4][:, q * P:(q + 1) * P], ytT[m][:, q * P:(q + 1) * P], ident[:, :])
                    last.then_inc(s(f"f{k}_yb"), 1)

                for m in range(NB):
                    if m:
                        pe.wait_ge(s(f"f{k}_xtT"), m)
                    turn(0, m)
                    if m >= 2:
                        down_(m - 2, m - 2)
                    if m >= 3:
                        back(m - 3, m - 3)
                    up(0, m)
                with pe.Fori(1, MT // NB) as i:
                    for m in range(NB):
                        pe.wait_ge(s(f"f{k}_xtT"), i * NB + m)
                        turn(i, m)
                        down_(i * NB + (m - 2), (m - 2) % NB)
                        back(i * NB + (m - 3), (m - 3) % NB)
                        up(i, m)
                down_(MT - 2, NB - 2)
                back(MT - 3, NB - 3)
                down_(MT - 1, NB - 1)
                back(MT - 2, NB - 2)
                back(MT - 1, NB - 1)

            router(0)
            mod_rows(1)
            pe.wait_ge(s("m1_cp"), B)
            experts(0)

            def qkv(c):
                for b in (2 * c, 2 * c + 1):
                    transpose_pair(b, "ln2_xn", xn, "ln2_xT", "ln2_hT", bank=6)
                pe.wait_ge(s("ln2_hT"), 2 * c + 2 + CREDIT)
                for qk in range(2):
                    if c:
                        pe.wait_ge(s("qf"), 2 * (c - 1) + qk + 1)
                    mm(pb[2 + qk][:, :], aw[:, qk, :], hT[:, 2 * c:2 * c + 2, :], start=True, stop=True).then_inc(s("qkp"), 1)
                if c >= 2:
                    pe.wait_ge(s("v"), c - 1)
                for t in range(CH // P):
                    last = mm(pb[4 + c % 2][:, t * P:(t + 1) * P],
                              hT[:, c * 2 + t // 2, (t % 2) * P:(t % 2 + 1) * P],
                              aw[:, 2, :], start=True, stop=True)
                last.then_inc(s("vp"), 1)

            def max_scores(b, m, h, first):
                if not (first and h < 2):
                    pe.wait_ge(s("mx"), b * H + (h - 1 + CREDIT))
                for q in range(2):
                    last = mm(pb[h % 2][:, q * L:(q + 1) * L], qA[m][0:KMAX, h, q * P:(q + 1) * P], kA[m][0:KMAX, h, :],
                              start=True, stop=True)
                last.then_inc(s("maxp"), 1)

            def max_T(b):
                pe.wait_ge(s("mneg"), b + 1)
                nc.tensor.transpose(pb[7][0:2 * H, 0:P], mneg, ident[:, :]).then_inc(s("mT"), 1)

            def exp_scores(b, m, h, first):
                if not (first and h < 2):
                    pe.wait_ge(s("pT"), b * H + (h - 1 + CREDIT))
                for k in range(2):
                    last = mm(pb[2 + h % 2][:, k * L:(k + 1) * L], kA[m][0:KEXP, h, k * P:(k + 1) * P], qA[m][0:KEXP, h, :],
                              start=True, stop=True)
                last.then_inc(s("sT"), 1)

            def values(b, m, h):
                g = h // (H // 2)
                pe.wait_ge(s("pT"), b * H + (h + 1 + CREDIT))
                if h % (H // 2) == 0:
                    pe.wait_ge(s("nrm"), b * 2 + (g - 1 + CREDIT))
                for k in range(2):
                    last = mm(pb[4 + g][:, 0:L], vz[m][:, 2 * k + g, h % HD, :], pexp[h % 4][:, k * L:(k + 1) * L],
                              start=(h % (H // 2) == 0 and k == 0), stop=(h % (H // 2) == H // 2 - 1 and k == 1))
                last.then_inc(s("pv"), 1)

            def out_proj(b):
                pe.wait_ge(s("nrm"), b * 2 + 2 + CREDIT)
                pe.wait_ge(s("x_b"), b + CREDIT)
                for q in range(2):
                    last = mm(pb[6][:, q * D:(q + 1) * D], oT[:, q * P:(q + 1) * P], aw[:, 3, :], start=True, stop=True)
                last.then_inc(s("aop"), 1)

            def attn(b, m, first, last_b, loads):
                pe.wait_ge(s("max_in"), b * 32 + 32)
                pe.wait_ge(s("vz"), b + 1 + CREDIT)
                for h in range(H):
                    exp_scores(b, m, h, first)
                    if h:
                        values(b, m, h - 1)
                    if h == 2 and not first:
                        out_proj(b - 1)
                    if not last_b:
                        if h == 3:
                            pe.wait_ge(s(f"qk_in{1 - m}"), loads * 64)
                        if 3 <= h < 11:
                            max_scores(b + 1, 1 - m, 2 * (h - 3), False)
                            max_scores(b + 1, 1 - m, 2 * (h - 3) + 1, False)
                        if h == 12:
                            max_T(b + 1)
                values(b, m, H - 1)

            for c in range(NC - 1):
                qkv(c)
            pe.wait_ge(s("rows_in"), 96)
            pe.wait_ge(s("qk_in0"), 64)
            for h in range(H):
                if h == 2:
                    qkv(NC - 1)
                max_scores(0, 0, h, True)
            max_T(0)
            pe.wait_ge(s("v"), NC)
            pe.wait_ge(s("qf"), 2 * NC)
            attn(0, 0, True, False, 1)
            with pe.Fori(0, (B - 2) // 2) as i:
                for m in (1, 0):
                    attn(i * 2 + (2 - m), m, False, False, i + 2)
            attn(B - 1, 1, False, True, 0)
            out_proj(B - 1)

            router(1)
            experts(1)


def _kernel_arrays(i):
    g = {k: np.asarray(v) for k, v in i.items()}
    c = np.ascontiguousarray
    halves = lambda w: c(w.reshape(2, P, -1).transpose(1, 0, 2))
    by_dim = lambda w: w.reshape((H, HD) + w.shape[1:]).swapaxes(0, 1).reshape(w.shape)
    f32 = np.float32
    pos = np.arange(L, dtype=f32)
    slopes = np.power(f32(2.0), np.linspace(-4.0, -0.3, H, dtype=f32)).astype(f32)
    bias = -(slopes[:, None] * pos[None, :])
    bf = mybir.dt.np(mybir.dt.bfloat16)
    rows, rest = [], bias
    for _ in range(3):
        part = rest.astype(bf)
        rows.append(part)
        rest = rest - part.astype(f32)

    def blob(w1, w2, b1, b2, gamma, beta):
        cols = [w1, w2.reshape(E, FC, P, D).transpose(0, 2, 1, 3).reshape(E, P, FC * D),
                b2[:, :, None], b1.reshape(E, FC, P).transpose(0, 2, 1),
                gamma[:, :, None], beta[:, :, None]]
        return c(np.concatenate(cols, axis=2))

    none = np.zeros((E, D), f32)
    return {
        "x": c(g["L0_attn_x"].reshape(T, D)),
        "cT": c(np.concatenate([g["L0_c"].T, g["L1_c"].T], axis=1)),
        "wmod": c(np.stack([g["L0_wmod"], g["L1_wmod"]], axis=1)),
        "in_w": c(g["L0_attn_in_proj_w"]),
        "conv_w": halves(g["L0_attn_conv_w"].reshape(DI, TAPS)),
        "conv_b": c(g["L0_attn_conv_b"].reshape(2, P).T),
        "A_log": c(halves(g["L0_attn_A_log"]).reshape(P, 2 * NS)),
        "xp_w": halves(g["L0_attn_x_proj_w"]),
        "dt_w": c(g["L0_attn_dt_proj_w"]),
        "dt_b": c(g["L0_attn_dt_proj_b"].reshape(2, P).T),
        "adj": halves(g["L0_attn_adj"]),
        "d_skip": c(g["L0_attn_D"].reshape(2, P).T),
        "out_w": halves(g["L0_attn_out_proj_w"]),
        "router_w": c(np.stack([g["L0_ffn_centroids"].T, g["L1_ffn_Wr"]], axis=1)),
        "br": c(np.broadcast_to(g["L1_ffn_br"], (P, E))),
        "attn_w": c(np.stack([by_dim(g["L1_attn_Wq"]).T, by_dim(g["L1_attn_Wk"]).T, g["L1_attn_Wv"].T, g["L1_attn_Wo"].T], axis=1)),
        "attn_b": c(np.stack([by_dim(g["L1_attn_bq"]), by_dim(g["L1_attn_bk"])], axis=1)),
        "attn_row": c(np.broadcast_to(np.stack([g["L1_attn_bv"], g["L1_attn_bo"]])[None], (P, 2, D))),
        "bias_rows": c(np.stack(rows)),
        "one_rows": np.ones((5, H, L), bf),
        "blob0": blob(g["L0_ffn_W1"].transpose(0, 2, 1), g["L0_ffn_W2"].transpose(0, 2, 1), g["L0_ffn_b1"], g["L0_ffn_b2"],
                      g["L0_ffn_gamma"], g["L0_ffn_beta"]),
        "blob1": blob(g["L1_ffn_W1"], g["L1_ffn_W2"], g["L1_ffn_b1"], g["L1_ffn_b2"], none, none),
    }


def kernel(**inputs):
    import concourse.bacc as _bacc
    from concourse.bass_utils import run_bass_kernel_spmd as _run

    nc = _bacc.Bacc("TRN2", target_bir_lowering=False, num_devices=1)
    arrays = _kernel_arrays(inputs)
    aps = {name: nc.dram_tensor(f"in_{name}", v.shape, mybir.dt.from_np(v.dtype), kind="ExternalInput").ap()
           for name, v in arrays.items()}
    out = nc.dram_tensor("out", (T, D), mybir.dt.float32, kind="ExternalOutput").ap()
    build(nc, aps, out)
    r = _run(nc, [{f"in_{name}": v for name, v in arrays.items()}], core_ids=[0])
    return r.results[0]["out"].reshape(B, L, D)
```
